# Optimizing a Trainium2 kernel written in Bass

```python
import numpy as np
import jax
import jax.numpy as jnp

def _softmax(x, axis=-1):
    return jax.nn.softmax(x, axis=axis)

def _gelu(x):
    return jax.nn.gelu(x, approximate=True)

def _silu(x):
    return jax.nn.silu(x)

def _sigmoid(x):
    return jax.nn.sigmoid(x)

def _layernorm(x, axis=-1, eps=1e-05):
    m = jnp.mean(x, axis=axis, keepdims=True)
    v = jnp.var(x, axis=axis, keepdims=True)
    return (x - m) / jnp.sqrt(v + eps)

def _scatter_add(tgt, idx, src, axis=0):
    return tgt.at[idx].add(src)

def _segment_sum(src, seg, n):
    return jax.ops.segment_sum(src, seg, n)
kernel_name = 'mk_sandwich_d1_jaxref_r8_494994'

def setup_inputs(seed: int=0):
    np.random.seed(seed)
    _w = jnp.asarray

    def _L0_attn_setup():
        import jax, jax.numpy as jnp
        import numpy as np
        B, S, D = (2, 256, 128)
        H, DH = (16, 64)
        DQL, DKVL = (64, 64)
        DR = 64
        TOPK = 64
        LN_EPS = 1e-05
        ROPE_BASE = 10000.0

        def _rope_tables(seq_len, dim):
            inv_freq = 1.0 / ROPE_BASE ** (np.arange(0, dim, 2, dtype=np.float32) / dim)
            t = np.arange(seq_len, dtype=np.float32)
            freqs = np.outer(t, inv_freq)
            cos = np.concatenate([np.cos(freqs), np.cos(freqs)], -1)[:, ::2]
            sin = np.concatenate([np.sin(freqs), np.sin(freqs)], -1)[:, ::2]
            return (jnp.asarray(cos), jnp.asarray(sin))

        def _apply_rope_subspace(x, d_rope):
            s = x.shape[-2]
            cos, sin = _rope_tables(s, d_rope)
            xr, xp = (x[..., :d_rope], x[..., d_rope:])
            e, o = (xr[..., 0::2], xr[..., 1::2])
            rot = jnp.stack([e * cos - o * sin, e * sin + o * cos], axis=-1).reshape(xr.shape)
            return jnp.concatenate([rot, xp], axis=-1)

        def _reference_tuple_inner(x, w_down_q, w_down_kv, w_up_q, w_up_k, w_up_v, w_out, ln_scale, ln_bias):
            b, s, d = x.shape
            residual = x
            mu = jnp.mean(x, axis=-1, keepdims=True)
            var = jnp.mean((x - mu) ** 2, axis=-1, keepdims=True)
            h = (x - mu) * jax.lax.rsqrt(var + LN_EPS) * ln_scale + ln_bias
            c_q = h @ w_down_q.T
            c_kv = h @ w_down_kv.T
            q = (c_q @ w_up_q.T).reshape(b, s, H, DH).transpose(0, 2, 1, 3)
            k = (c_kv @ w_up_k.T).reshape(b, s, H, DH).transpose(0, 2, 1, 3)
            v = (c_kv @ w_up_v.T).reshape(b, s, H, DH).transpose(0, 2, 1, 3)
            q = _apply_rope_subspace(q, DR)
            k = _apply_rope_subspace(k, DR)
            scale = 1.0 / np.sqrt(DH).astype(np.float32)
            scores = jnp.einsum('bhqd,bhkd->bhqk', q, k) * scale
            _, indices = jax.lax.top_k(scores, min(TOPK, s))
            attn = jax.nn.softmax(scores, axis=-1)
            out = jnp.einsum('bhqk,bhkd->bhqd', attn, v)
            out = out.transpose(0, 2, 1, 3).reshape(b, s, H * DH)
            out = out @ w_out.T + residual
            return (out, indices.astype(jnp.int64))
        key = jax.random.key(seed)
        ks = jax.random.split(key, 7)
        init = lambda k, shape: jax.random.normal(k, shape, jnp.float32) * 0.02
        return {'x': jax.random.normal(ks[0], (B, S, D), jnp.float32), 'w_down_q': init(ks[1], (DQL, D)), 'w_down_kv': init(ks[2], (DKVL, D)), 'w_up_q': init(ks[3], (H * DH, DQL)), 'w_up_k': init(ks[4], (H * DH, DKVL)), 'w_up_v': init(ks[5], (H * DH, DKVL)), 'w_out': init(ks[6], (D, H * DH)), 'ln_scale': jnp.ones((D,), jnp.float32), 'ln_bias': jnp.zeros((D,), jnp.float32)}
    _L0_attn_in = _L0_attn_setup()

    def _L0_ffn_setup():
        import jax, jax.numpy as jnp
        import numpy as np
        TOP_K = 2
        key = jax.random.key(seed)
        k1, k2, k3, k4, k5 = jax.random.split(key, 5)
        B, S, D, F, E = (2, 128, 128, 256, 8)
        return {'x': jax.random.normal(k1, (B, S, D), dtype=jnp.float32), 'router_kernel_DE': jax.random.normal(k2, (D, E), dtype=jnp.float32) * 0.02, 'kernel_gating_EDF': jax.random.normal(k3, (E, D, F), dtype=jnp.float32) * 0.02, 'kernel_up_EDF': jax.random.normal(k4, (E, D, F), dtype=jnp.float32) * 0.02, 'kernel_down_EFD': jax.random.normal(k5, (E, F, D), dtype=jnp.float32) * 0.02}
    _L0_ffn_in = _L0_ffn_setup()
    _d = {'L0_attn_x': _L0_attn_in['x'], 'L0_attn_w_down_q': _L0_attn_in['w_down_q'], 'L0_attn_w_down_kv': _L0_attn_in['w_down_kv'], 'L0_attn_w_up_q': _L0_attn_in['w_up_q'], 'L0_attn_w_up_k': _L0_attn_in['w_up_k'], 'L0_attn_w_up_v': _L0_attn_in['w_up_v'], 'L0_attn_w_out': _L0_attn_in['w_out'], 'L0_attn_ln_scale': _L0_attn_in['ln_scale'], 'L0_attn_ln_bias': _L0_attn_in['ln_bias'], 'L0_ffn_router_kernel_DE': _L0_ffn_in['router_kernel_DE'], 'L0_ffn_kernel_gating_EDF': _L0_ffn_in['kernel_gating_EDF'], 'L0_ffn_kernel_up_EDF': _L0_ffn_in['kernel_up_EDF'], 'L0_ffn_kernel_down_EFD': _L0_ffn_in['kernel_down_EFD']}
    _x0 = _d['L0_attn_x']
    _d['L0_attn_x'] = jax.random.normal(jax.random.fold_in(jax.random.key(seed), 1), (4, 1024, 128), dtype=_x0.dtype)
    del _x0
    return _d

def reference(L0_attn_x, L0_attn_w_down_q, L0_attn_w_down_kv, L0_attn_w_up_q, L0_attn_w_up_k, L0_attn_w_up_v, L0_attn_w_out, L0_attn_ln_scale, L0_attn_ln_bias, L0_ffn_router_kernel_DE, L0_ffn_kernel_gating_EDF, L0_ffn_kernel_up_EDF, L0_ffn_kernel_down_EFD):

    def _L0_attn_ref(x, w_down_q, w_down_kv, w_up_q, w_up_k, w_up_v, w_out, ln_scale, ln_bias):
        import jax, jax.numpy as jnp
        import numpy as np
        B, S, D = (2, 256, 128)
        H, DH = (16, 64)
        DQL, DKVL = (64, 64)
        DR = 64
        TOPK = 64
        LN_EPS = 1e-05
        ROPE_BASE = 10000.0

        def _rope_tables(seq_len, dim):
            inv_freq = 1.0 / ROPE_BASE ** (np.arange(0, dim, 2, dtype=np.float32) / dim)
            t = np.arange(seq_len, dtype=np.float32)
            freqs = np.outer(t, inv_freq)
            cos = np.concatenate([np.cos(freqs), np.cos(freqs)], -1)[:, ::2]
            sin = np.concatenate([np.sin(freqs), np.sin(freqs)], -1)[:, ::2]
            return (jnp.asarray(cos), jnp.asarray(sin))

        def _apply_rope_subspace(x, d_rope):
            s = x.shape[-2]
            cos, sin = _rope_tables(s, d_rope)
            xr, xp = (x[..., :d_rope], x[..., d_rope:])
            e, o = (xr[..., 0::2], xr[..., 1::2])
            rot = jnp.stack([e * cos - o * sin, e * sin + o * cos], axis=-1).reshape(xr.shape)
            return jnp.concatenate([rot, xp], axis=-1)

        def _reference_tuple_inner(x, w_down_q, w_down_kv, w_up_q, w_up_k, w_up_v, w_out, ln_scale, ln_bias):
            b, s, d = x.shape
            residual = x
            mu = jnp.mean(x, axis=-1, keepdims=True)
            var = jnp.mean((x - mu) ** 2, axis=-1, keepdims=True)
            h = (x - mu) * jax.lax.rsqrt(var + LN_EPS) * ln_scale + ln_bias
            c_q = h @ w_down_q.T
            c_kv = h @ w_down_kv.T
            q = (c_q @ w_up_q.T).reshape(b, s, H, DH).transpose(0, 2, 1, 3)
            k = (c_kv @ w_up_k.T).reshape(b, s, H, DH).transpose(0, 2, 1, 3)
            v = (c_kv @ w_up_v.T).reshape(b, s, H, DH).transpose(0, 2, 1, 3)
            q = _apply_rope_subspace(q, DR)
            k = _apply_rope_subspace(k, DR)
            scale = 1.0 / np.sqrt(DH).astype(np.float32)
            scores = jnp.einsum('bhqd,bhkd->bhqk', q, k) * scale
            _, indices = jax.lax.top_k(scores, min(TOPK, s))
            attn = jax.nn.softmax(scores, axis=-1)
            out = jnp.einsum('bhqk,bhkd->bhqd', attn, v)
            out = out.transpose(0, 2, 1, 3).reshape(b, s, H * DH)
            out = out @ w_out.T + residual
            return (out, indices.astype(jnp.int64))
        return _reference_tuple_inner(x, w_down_q, w_down_kv, w_up_q, w_up_k, w_up_v, w_out, ln_scale, ln_bias)[0]

    def _L0_ffn_ref(x, router_kernel_DE, kernel_gating_EDF, kernel_up_EDF, kernel_down_EFD):
        import jax, jax.numpy as jnp
        import numpy as np
        TOP_K = 2
        E = router_kernel_DE.shape[-1]
        x = x.astype(jnp.float32)
        logits_BSE = jnp.einsum('BSD,DE->BSE', x, router_kernel_DE)
        probs_BSE = jax.nn.softmax(logits_BSE.astype(jnp.float32), axis=-1)
        weights_BSK, indices_BSK = jax.lax.top_k(probs_BSE, TOP_K)
        norm_weights_BSK = jax.nn.softmax(weights_BSK, axis=-1)
        one_hot_BSKE = jax.nn.one_hot(indices_BSK, num_classes=E, dtype=x.dtype)
        full_weights_BSE = jnp.sum(one_hot_BSKE * norm_weights_BSK[..., None], axis=2)
        gating_BSEF = jnp.einsum('BSD,EDF->BSEF', x, kernel_gating_EDF)
        act_BSEF = jax.nn.silu(gating_BSEF)
        up_BSEF = jnp.einsum('BSD,EDF->BSEF', x, kernel_up_EDF)
        fuse_BSEF = act_BSEF * up_BSEF
        down_BSED = jnp.einsum('BSEF,EFD->BSED', fuse_BSEF, kernel_down_EFD)
        out_BSD = jnp.einsum('BSED,BSE->BSD', down_BSED, full_weights_BSE)
        return out_BSD.astype(jnp.float32)
    x = L0_attn_x
    x = x + _layernorm(_L0_attn_ref(_layernorm(x, axis=-1), L0_attn_w_down_q, L0_attn_w_down_kv, L0_attn_w_up_q, L0_attn_w_up_k, L0_attn_w_up_v, L0_attn_w_out, L0_attn_ln_scale, L0_attn_ln_bias), axis=-1)
    x = x + _layernorm(_L0_ffn_ref(_layernorm(x, axis=-1), L0_ffn_router_kernel_DE, L0_ffn_kernel_gating_EDF, L0_ffn_kernel_up_EDF, L0_ffn_kernel_down_EFD), axis=-1)
    return x

_drawn_inputs = setup_inputs


def setup_inputs(seed=0):
    import zlib

    import numpy as np

    out = dict(_drawn_inputs(seed))
    spreads = {'L0_attn_ln_scale': (1.0, 0.6), 'L0_attn_ln_bias': (0.0, 0.46)}
    factors = {'L0_attn_w_down_q': 8.0,
     'L0_attn_w_down_kv': 3.359,
     'L0_attn_w_up_q': 8.0,
     'L0_attn_w_up_k': 8.0,
     'L0_attn_w_up_v': 3.452,
     'L0_attn_w_out': 3.817}
    for name, (base, spread) in spreads.items():
        noise = np.random.default_rng([zlib.crc32(name.encode()), seed]).standard_normal(out[name].shape)
        drawn = base * np.exp(spread * noise) if base else spread * noise
        out[name] = jnp.asarray(drawn.astype(out[name].dtype))
    for name, factor in factors.items():
        out[name] = (out[name] * factor).astype(out[name].dtype)
    return out
```

```python
from contextlib import ExitStack

import numpy as np
import concourse.bass as bass
from concourse import mybir

F32 = mybir.dt.float32
F32R = mybir.dt.float32r
F16 = mybir.dt.float16
BF16 = mybir.dt.bfloat16
U32 = mybir.dt.uint32
ALU = mybir.AluOpType
ACT = mybir.ActivationFunctionType
AX = mybir.AxisListType.X

P = 128
B, S, D = 4, 1024, 128
H, DH = 16, 64
E, F = 8, 256
LN_EPS = 1e-5
ROPE_BASE = 10000.0
SCALE = 1.0 / 8.0

TILES = S // P
HALF = 512
CHUNKS = S // HALF
PAIRS = H // 2
STEPS = 16
FT = F // P
VW = 130
VLO = VW - DH
WBLOCKS = 6
AHEAD = 3
UNITS = CHUNKS * E
ROUTE = 15

FEED = ([("proj", a, c) for a in range(2) for c in range(CHUNKS)] + [("value", 0, 0)]
        + [("max", 0, t) for t in range(TILES)] + [("max", 1, 0), ("max", 1, 1), ("turn", 0, 0)]
        + [("max", 1, t) for t in range(2, TILES)] + [("turn", 1, 0)])
NFEED = len(FEED)
FEED_AT = {job: n for n, job in enumerate(FEED)}
ATTN, OUT = ("attn", 0, 0), ("out", 0, 0)
FEED_IN = {0: FEED[0:2], 1: FEED[2:4], 2: FEED[4:5], 7: FEED[5:7], 8: FEED[7:9], 9: FEED[9:11], 10: FEED[11:13],
           11: FEED[13:15], 12: FEED[15:18], 13: FEED[18:20], 14: FEED[20:22], 15: FEED[22:23]}
ATTN_STEP, OUT_STEP = 5, 15
POOL_STEPS = (6, 7, 8, 9, 10, 11, 12, 13)
DVE_STEPS = tuple(s for s in range(STEPS) if s not in POOL_STEPS)
LAG = 2


def jobs_in(step, feeds, finishes):
    jobs = list(FEED_IN.get(step, [])) if feeds else []
    if finishes and step == ATTN_STEP:
        jobs = jobs + [ATTN]
    if finishes and step == OUT_STEP:
        jobs = [OUT] + jobs
    return jobs


def low_parts_done(step):
    own = POOL_STEPS if step % STEPS in POOL_STEPS else DVE_STEPS
    return own is POOL_STEPS, len(own) * (step // STEPS) + own.index(step % STEPS) + 1


def program(nc, x, w_pairs, w_down, ln_scale, ln_bias, router, w_gate, w_up, w_dn,
            rope_cos, rope_sin, identity, expert_rows, expert_ids, out):
    with ExitStack() as ctx:
        def sb(name, shape, dt=F32, where=ctx):
            return where.enter_context(nc.sbuf_tensor(name, shape, dt))

        def sem(name):
            return ctx.enter_context(nc.semaphore(name))

        scores = ctx.enter_context(nc.psum_tensor("scores", [P, 2, 2, HALF], F32))
        aux = ctx.enter_context(nc.psum_tensor("aux", [P, 2 * HALF], F32))
        outacc = ctx.enter_context(nc.psum_tensor("outacc", [P, 2, HALF], F32))
        slot = [scores[:, i].rearrange("p a n -> p (a n)") for i in range(2)]
        gate_ps = [scores[:, i] for i in range(2)]
        wrow_ps = aux[:, 0:HALF]
        down_ps = aux[:, HALF:2 * HALF]

        ident = sb("ident", [P, P])
        eps = sb("eps", [P, 1])
        spare = sb("spare", [P, 1])
        x1_all = sb("x1_all", [P, B * TILES, D])
        stats = sb("stats", [P, TILES, 6])
        moments = sb("moments", [P, TILES, 2])
        sdev = sb("sdev", [P, TILES])
        rstd = sb("rstd", [P, TILES])
        n_sb = sb("n_sb", [P, TILES, D])
        res_sb = sb("res_sb", [P, TILES, D])

        with ExitStack() as phase:
            def sb1(name, shape, dt=F32):
                return sb(name, shape, dt, phase)

            cos_sb = sb1("cos_sb", [P, S])
            sin_sb = sb1("sin_sb", [P, S])
            scale_sb = sb1("scale_sb", [P, 1])
            bias_sb = sb1("bias_sb", [P, 1])
            wd_sb = sb1("wd_sb", [D, 4 * DH])
            x_sb = sb1("x_sb", [P, TILES, D])
            c_hi = [sb1(f"c_hi{i}", [P, S], F32R) for i in range(2)]
            c_lo = [sb1(f"c_lo{i}", [P, S], F32R) for i in range(2)]
            oacc = sb1("oacc", [D, S])
            w_raw = sb1("w_raw", [P, WBLOCKS, P])
            wsl = [sb1(f"wsl{i}", [P, WBLOCKS, P], F32R) for i in range(2)]
            wo_lo = [sb1(f"wo_lo{i}", [P, P], F32R) for i in range(2)]
            vsl = [sb1(f"vsl{i}", [P, TILES, 2, VW], F16) for i in range(2)]
            t_sin = [sb1(f"t_sin{i}", [P, HALF]) for i in range(2)]
            rot = [sb1(f"rot{i}", [P, S]) for i in range(2)]
            qk_hi = [sb1(f"qk_hi{i}", [P, S], F32R) for i in range(2)]
            q_both = [[sb1(f"q_both{i}{h}", [P, S], F32R) for h in range(2)] for i in range(2)]
            k_twice = [[sb1(f"k_twice{i}{h}", [P, S], F32R) for h in range(2)] for i in range(2)]
            q_max = [sb1(f"q_max{h}", [DH + 2, S], F32R) for h in range(2)]
            k_ones = [sb1(f"k_ones{h}", [DH + 2, S], F32R) for h in range(2)]
            row_max = [sb1(f"row_max{h}", [P, TILES]) for h in range(2)]
            max_parts = [sb1(f"max_parts{h}", [P, 2 * TILES], F32R) for h in range(2)]
            max_turned = [sb1(f"max_turned{h}", [2 * TILES, P], F32R) for h in range(2)]
            probs = [sb1(f"probs{i}", [P, 2, HALF]) for i in range(4)]
            probs_lo = [sb1(f"probs_lo{i}", [P, 2, HALF], F16) for i in range(2)]
            o_sb = [sb1(f"o_sb{i}", [P, 2, 2, VW]) for i in range(2)]
            o_sum = [sb1(f"o_sum{i}", [P, 4, DH]) for i in range(2)]
            o_rden = [sb1(f"o_rden{i}", [P, 4]) for i in range(2)]
            attn = sb1("attn", [P, TILES, P])
            aT_hi = sb1("aT_hi", [P, S], F32R)
            aT_lo = sb1("aT_lo", [P, S], F32R)
            hT = rot[0]

        router_sb = sb("router_sb", [D, E])
        ids_sb = sb("ids_sb", [P, TILES, E])
        rows_in = sb("rows_in", [E, E * P])
        rows_r = sb("rows_r", [E, E * P], F32R)
        stage = [sb(f"stage{i}", [P, E * F]) for i in range(3)]
        wg_hi = sb("wg_hi", [D, E * F], F32R)
        wg_lo = sb("wg_lo", [D, E * F], F32R)
        wu_hi = sb("wu_hi", [D, E * F], F32R)
        wu_lo = sb("wu_lo", [D, E * F], F32R)
        wn_hi = sb("wn_hi", [P, E * FT * D], F32R)
        wn_lo = sb("wn_lo", [P, E * FT * D], F32R)
        zT = sb("zT", [D, S])
        zT_hi = sb("zT_hi", [D, S], F32R)
        zT_lo = sb("zT_lo", [D, S], F32R)
        lg = sb("lg", [P, TILES, E])
        lmax = sb("lmax", [P, TILES])
        lexp = sb("lexp", [P, TILES, E])
        lsum = sb("lsum", [P, TILES])
        lrec = sb("lrec", [P, TILES])
        pr = sb("pr", [P, TILES, E])
        top = sb("top", [P, TILES, 8])
        top_at = sb("top_at", [P, TILES, 8], U32)
        top_f = sb("top_f", [P, TILES, 8])
        gap = sb("gap", [P, TILES])
        egap = sb("egap", [P, TILES])
        eden = sb("eden", [P, TILES])
        w_1 = sb("w_1", [P, TILES])
        w_2 = sb("w_2", [P, TILES])
        hot_1 = sb("hot_1", [P, TILES, E])
        hot_2 = sb("hot_2", [P, TILES, E])
        hot_w1 = sb("hot_w1", [P, TILES, E])
        hot_w2 = sb("hot_w2", [P, TILES, E])
        wfull = sb("wfull", [P, TILES, E])
        wT_hi = sb("wT_hi", [E, S], F32R)
        wT_lo = sb("wT_lo", [E, S], F32R)
        act_sb = [sb(f"act_sb{i}", [P, FT, HALF]) for i in range(2)]
        wrow_sb = [sb(f"wrow_sb{i}", [P, HALF]) for i in range(2)]
        actw_sb = [sb(f"actw_sb{i}", [P, FT, HALF]) for i in range(2)]
        fuse = [sb(f"fuse{i}", [P, FT, HALF]) for i in range(2)]
        f_hi = [sb(f"f_hi{i}", [P, FT, HALF], F32R) for i in range(3)]
        f_lo = [sb(f"f_lo{i}", [P, FT, HALF], F32R) for i in range(3)]
        dT = sb("dT", [D, HALF])

        consts_in, fills_done, x_in = sem("consts_in"), sem("fills_done"), sem("x_in")
        ln_stats, ln_moments, ln_sdev, ln_rstd, ln_done = (
            sem("ln_stats"), sem("ln_moments"), sem("ln_sdev"), sem("ln_rstd"), sem("ln_done"))
        n_turned, h_done = sem("n_turned"), sem("h_done")
        c_ready, c_hi_done, c_lo_done = sem("c_ready"), sem("c_hi_done"), sem("c_lo_done")
        raw_in, w_hi_done, w_done, v_hi_done = sem("raw_in"), sem("w_hi_done"), sem("w_done"), sem("v_hi_done")
        aux_ready, aux_taken = sem("aux_ready"), sem("aux_taken")
        out_ready, out_taken, aT_hi_done = sem("out_ready"), sem("out_taken"), sem("aT_hi_done")
        rope_sum, qk_hi_done, qk_lo_done = sem("rope_sum"), sem("qk_hi_done"), sem("qk_lo_done")
        max_in = [sem("max_in0"), sem("max_in1")]
        score_in = [sem("score_in0"), sem("score_in1")]
        max_hi, max_split = sem("max_hi"), sem("max_split")
        rows_put = [sem("rows_put0"), sem("rows_put1")]
        scores_ready, probs_done = sem("scores_ready"), sem("probs_done")
        lo_dve, lo_pool = sem("lo_dve"), sem("lo_pool")
        pv_done, o_copied, o_recip, o_added, o_done = (
            sem("pv_done"), sem("o_copied"), sem("o_recip"), sem("o_added"), sem("o_done"))
        o_turned, res_done, x1_done = sem("o_turned"), sem("res_done"), sem("x1_done")
        econsts_in, rows_done = sem("econsts_in"), sem("rows_done")
        stage_in = [sem(f"stage_in{i}") for i in range(3)]
        stage_hi, stage_lo = sem("stage_hi"), sem("stage_lo")
        z_turned, zT_done, z_lo_done = sem("z_turned"), sem("zT_done"), sem("z_lo_done")
        logits_ready, route_dve, route_act = sem("logits_ready"), sem("route_dve"), sem("route_act")
        w_turned, wT_hi_done, wT_lo_done = sem("w_turned"), sem("wT_hi_done"), sem("wT_lo_done")
        gate_ready, wrow_ready, up_ready, down_done = (
            sem("gate_ready"), sem("wrow_ready"), sem("up_ready"), sem("down_done"))
        act_done, wrow_done, actw_done = sem("act_done"), sem("wrow_done"), sem("actw_done")
        fuse_done, f_hi_done, f_lo_done = sem("fuse_done"), sem("f_hi_done"), sem("f_lo_done")
        dT_done, d_turned, d_taken, result_done, stored = (
            sem("dT_done"), sem("d_turned"), sem("d_taken"), sem("result_done"), sem("stored"))

        experts = [(w_gate, wg_hi, wg_lo), (w_up, wu_hi, wu_lo), (w_dn, wn_hi, wn_lo)]
        first_consts = ((ident, identity), (cos_sb, rope_cos), (sin_sb, rope_sin), (scale_sb, ln_scale),
                        (bias_sb, ln_bias), (wd_sb, w_down))
        expert_consts = ((router_sb, router), (ids_sb, expert_ids), (rows_in, expert_rows))
        NORMS = 3
        NORMS_2 = 2

        block = ctx.enter_context(nc.Block())

        def batch_of(t, b):
            return t[:, bass.ds(b * TILES, TILES), :]

        def in_dram(t, b):
            return t[bass.ds(b, 1)].rearrange("b (t p) d -> p (b t) d", p=P)

        @block.sync
        def _(sp):
            for dst, src in first_consts:
                sp.dma_start(dst[:], src).then_inc(consts_in, 16)
            sp.dma_start(x_sb[:], in_dram(x, 0)).then_inc(x_in, 16)

            def load_raw(pair):
                sp.dma_start(w_raw[:], w_pairs[bass.ds(pair, 1)].rearrange("a p c n -> p (a c) n")).then_inc(raw_in, 16)

            load_raw(0)
            for n in range(1, AHEAD):
                sp.wait_ge(w_done, n)
                load_raw(n)

            def put(dst, src, h, signal):
                sp.dma_start(dst.bitcast(F32), src[h * DH:(h + 1) * DH, :].bitcast(F32)).then_inc(signal, 16)

            def feed(n, par, pair_before):
                sp.wait_ge(qk_hi_done, 2 * n + 2)
                for h in range(2):
                    put(q_both[par][h][0:DH, :], qk_hi[0], h, max_in[h])
                    put(k_twice[par][h][0:DH, :], qk_hi[1], h, max_in[h])
                    put(k_twice[par][h][DH:P, :], qk_hi[1], h, max_in[h])
                    if h == 0:
                        sp.wait_ge(qk_lo_done, 2 * n + 1)
                    put(q_both[par][h][DH:P, :], rot[0], h, max_in[h])
                if pair_before is not None:
                    more_weights(n - 1, pair_before)
                sp.wait_ge(qk_lo_done, 2 * n + 2)
                for h in range(2):
                    if pair_before is not None:
                        sp.wait_ge(scores_ready, n * STEPS - (STEPS // 2) * (1 - h))
                    put(q_max[h][0:DH, :], qk_hi[0], h, score_in[h])
                    put(k_ones[h][0:DH, :], rot[1], h, score_in[h])
                    sp.wait_ge(aux_taken, n * NFEED + (FEED_AT[("turn", h, 0)] + 1))
                    for part in range(2):
                        sp.dma_start(q_max[h][DH + part:DH + part + 1, :].bitcast(F32),
                                     max_turned[h][part * TILES:(part + 1) * TILES, :].bitcast(F32)).then_inc(rows_put[h], 16)

            def more_weights(g, pair):
                sp.wait_ge(w_done, g + AHEAD)
                load_raw(pair + AHEAD)

            with sp.Fori(0, B) as b:
                n0 = b * PAIRS
                feed(n0, 0, None)
                feed(n0 + 1, 1, 0)
                with sp.Fori(0, PAIRS // 2 - 1) as i:
                    feed(n0 + i * 2 + 2, 0, i * 2 + 1)
                    feed(n0 + i * 2 + 3, 1, i * 2 + 2)
                more_weights(n0 + (PAIRS - 1), PAIRS - 1)
                sp.wait_ge(x1_done, b + 1)
                sp.dma_start(x_sb[:], in_dram(x, (b + 1) % B)).then_inc(x_in, 16)
            sp.wait_ge(x_in, 16 * (B + 1))
            sp.wait_ge(raw_in, 16 * (B * PAIRS + AHEAD))
            for dst, src in expert_consts:
                sp.dma_start(dst[:], src).then_inc(econsts_in, 16)
            for n, (src, _, _) in enumerate(experts):
                sp.dma_start(stage[n][:], src).then_inc(stage_in[n], 16)
            with sp.Fori(0, B) as b:
                sp.wait_ge(result_done, b + 1)
                sp.dma_start(in_dram(out, b), batch_of(x1_all, b)).then_inc(stored, 16)
            sp.wait_ge(stored, 16 * B)

        @block.tensor
        def _(pe):
            def free(n, m, before):
                if before in (ATTN, OUT):
                    pe.wait_ge(out_taken, 2 * m + (1 if before == ATTN else 2))
                elif before is not None:
                    pe.wait_ge(aux_taken, n * NFEED + (FEED_AT[before] + 1))

            def feed_job(n, par, which):
                kind, a, t = which
                if kind == "proj":
                    if which == FEED[0]:
                        pe.wait_ge(w_done, n + 1)
                    for swapped in range(2):
                        for c in (c_hi, c_lo):
                            mm = pe.matmul(aux[:, swapped * HALF:(swapped + 1) * HALF], wsl[par][:, 2 * a + swapped, :],
                                           c[a][:, t * HALF:(t + 1) * HALF], start=c is c_hi, stop=c is c_lo)
                elif kind == "value":
                    for t in range(TILES):
                        for c in (c_hi, c_lo):
                            mm = pe.matmul(aux[:, t * P:(t + 1) * P], c[1][:, t * P:(t + 1) * P], wsl[par][:, 4, :],
                                           start=c is c_hi, stop=c is c_lo)
                elif kind == "max":
                    if t == 0:
                        pe.wait_ge(max_in[a], 64 * n + 64)
                    for c in range(CHUNKS):
                        mm = pe.matmul(aux[:, c * HALF:(c + 1) * HALF], q_both[par][a][:, t * P:(t + 1) * P],
                                       k_twice[par][a][:, c * HALF:(c + 1) * HALF], start=True, stop=True)
                else:
                    pe.wait_ge(max_split, 2 * n + (a + 1))
                    mm = pe.transpose(aux[0:2 * TILES, 0:P], max_parts[a][:].bitcast(F32), ident[:])
                mm.then_inc(aux_ready, 1)

            def turn_attention(m):
                pe.wait_ge(o_done, m * 4 + 4)
                for t in range(TILES):
                    mm = pe.transpose(aux[:, t * P:(t + 1) * P], attn[:, t, :], ident[:])
                mm.then_inc(out_ready, 1)

            def project_out(m, par):
                pe.wait_ge(out_taken, 2 * m + 1)
                pe.wait_ge(w_done, m + 3)
                for c in range(CHUNKS):
                    terms = ((wsl[par][:, 5, :], aT_hi), (wo_lo[par][:], aT_hi), (wsl[par][:, 5, :], aT_lo))
                    for k, (w, a) in enumerate(terms):
                        mm = pe.matmul(aux[:, c * HALF:(c + 1) * HALF], w, a[:, c * HALF:(c + 1) * HALF],
                                       start=k == 0, stop=k == 2)
                mm.then_inc(out_ready, 1)

            def score(g, par, s, first):
                h, qh, kp = s // 8, s % 8 // 4, s % 4
                if s >= 2 or not first:
                    pe.wait_ge(probs_done, g * STEPS + (s - 1))
                if s % 8 == 0:
                    pe.wait_ge(score_in[h], 32 * g + 32)
                    pe.wait_ge(rows_put[h], 32 * g + 32)
                for i in range(2):
                    k0 = (2 * kp + i) * P
                    pe.matmul(scores[:, s % 2, i, :], k_twice[par][h][:, k0:k0 + P],
                              q_both[par][h][:, qh * HALF:(qh + 1) * HALF], start=True, stop=False)
                    mm = pe.matmul(scores[:, s % 2, i, :], k_ones[h][:, k0:k0 + P],
                                   q_max[h][:, qh * HALF:(qh + 1) * HALF], start=False, stop=True)
                mm.then_inc(scores_ready, 1)

            def values(g, par, s, first):
                t = s % STEPS
                h, kp = t // 8, t % 4
                pool, count = low_parts_done(s)
                if s == 0:
                    pe.wait_ge(aux_taken, g * NFEED + (FEED_AT[("value", 0, 0)] + 1))
                if kp == 0 and not (first and s == 0):
                    pe.wait_ge(o_copied, g * 4 + s // 4)
                pe.wait_ge(lo_pool if pool else lo_dve, g * 8 + count)
                for i in range(2):
                    high = probs[t % 4][:, i, :].bitcast(BF16).rearrange("p (n two) -> p n two", two=2)
                    v = vsl[par][:, 2 * kp + i, h, :]
                    for q in range(4):
                        acc = outacc[:, q // 2, q % 2 * VW:(q % 2 + 1) * VW]
                        opens = kp == 0 and i == 0 and q % 2 == 0
                        pe.matmul(acc, high[:, q * P:(q + 1) * P, 1], v, start=opens, stop=False, skip_group_check=True)
                        mm = pe.matmul(acc[:, 0:VLO], probs_lo[t % 2][:, i, q * P:(q + 1) * P], v[:, 0:VLO],
                                       start=False, stop=kp == 3 and i == 1, skip_group_check=True)
                mm.then_inc(pv_done, 1)

            def attend(g, par, feeds, finishes):
                before = FEED[-1]
                n = g
                for s in range(STEPS):
                    score(g, par, s, not finishes)
                    jobs = jobs_in(s, feeds, finishes)
                    for k, which in enumerate(jobs or [None]):
                        if which is not None:
                            free(n, g - 1, before)
                            if which == ATTN:
                                turn_attention(g - 1)
                            elif which == OUT:
                                project_out(g - 1, 1 - par)
                            else:
                                feed_job(g + 1, 1 - par, which)
                                n = g + 1
                            before = which
                        if k == 0 and (s >= LAG or finishes):
                            values(g, par if s >= LAG else 1 - par, s - LAG, not finishes)

            pe.wait_ge(consts_in, 16 * len(first_consts))
            pe.wait_ge(fills_done, 1)
            with pe.Fori(0, B) as b:
                n0 = b * PAIRS
                last = n0 + (PAIRS - 1)
                pe.wait_ge(ln_done, b * NORMS + 2)
                for t in range(TILES):
                    mm = pe.transpose(aux[:, t * P:(t + 1) * P], n_sb[:, t, :], ident[:])
                mm.then_inc(n_turned, 1)
                pe.wait_ge(h_done, b + 1)
                for i in range(2):
                    for c in range(CHUNKS):
                        mm = pe.matmul(scores[:, i, c, :], wd_sb[:, i * P:(i + 1) * P], hT[:, c * HALF:(c + 1) * HALF],
                                       start=True, stop=True)
                    mm.then_inc(c_ready, 1)
                pe.wait_ge(c_lo_done, 2 * b + 2)
                before = None
                for which in FEED:
                    free(n0, None, before)
                    feed_job(n0, 0, which)
                    before = which
                attend(n0, 0, True, False)
                with pe.Fori(0, PAIRS // 2 - 1) as i:
                    attend(n0 + i * 2 + 1, 1, True, True)
                    attend(n0 + i * 2 + 2, 0, True, True)
                attend(last, 1, False, True)
                for s in range(STEPS, STEPS + LAG):
                    values(last, 1, s - LAG, False)
                free(None, last - 1, OUT)
                turn_attention(last)
                project_out(last, 1)
                pe.wait_ge(out_taken, 2 * last + 2)
                for t in range(TILES):
                    mm = pe.transpose(slot[0][:, t * P:(t + 1) * P], oacc[:, t * P:(t + 1) * P], ident[:])
                mm.then_inc(o_turned, 1)

            pe.wait_ge(econsts_in, 16 * len(expert_consts))
            pe.wait_ge(rows_done, 1)
            with pe.Fori(0, B) as b:
                pe.wait_ge(ln_done, b * NORMS_2 + (B * NORMS + 1))
                for t in range(TILES):
                    mm = pe.transpose(aux[:, t * P:(t + 1) * P], n_sb[:, t, :], ident[:])
                mm.then_inc(z_turned, 1)
                pe.wait_ge(zT_done, b + 1)
                for t in range(TILES):
                    mm = pe.matmul(outacc[:, 0, t * E:(t + 1) * E], zT[:, t * P:(t + 1) * P], router_sb[:], start=True, stop=True)
                mm.then_inc(logits_ready, 1)
                pe.wait_ge(z_lo_done, b + 1)
                pe.wait_ge(stage_lo, len(experts))

                def hidden(dst, w_hi, w_lo, e, c):
                    for ft in range(FT):
                        f0 = e * F + ft * P
                        for k, (w, z) in enumerate(((w_hi, zT_hi), (w_lo, zT_hi), (w_hi, zT_lo))):
                            mm = pe.matmul(dst[:, ft, :], w[:, f0:f0 + P], z[:, c * HALF:(c + 1) * HALF],
                                           start=k == 0, stop=k == 2)
                    return mm

                def down(u):
                    c, e = u // E, u % E
                    if e == 0 and c:
                        pe.wait_ge(d_taken, CHUNKS * b + c)
                    pe.wait_ge(f_lo_done, UNITS * b + (u + 1))
                    for ft in range(FT):
                        w0 = (e * FT + ft) * D
                        for k, (w, f) in enumerate(((wn_hi, f_hi), (wn_lo, f_hi), (wn_hi, f_lo))):
                            mm = pe.matmul(down_ps, w[:, w0:w0 + D], f[u % 3][:, ft, :],
                                           start=e == 0 and ft == 0 and k == 0,
                                           stop=e == E - 1 and ft == FT - 1 and k == 2)
                    mm.then_inc(down_done, 1)
                    if e == E - 1:
                        pe.wait_ge(dT_done, CHUNKS * b + (c + 1))
                        for t in range(HALF // P):
                            mm = pe.transpose(down_ps[:, t * P:(t + 1) * P], dT[:, t * P:(t + 1) * P], ident[:])
                        mm.then_inc(d_turned, 1)

                for u in range(UNITS):
                    c, e = u // E, u % E
                    if u >= 2:
                        pe.wait_ge(act_done, UNITS * b + (u - 1))
                    hidden(gate_ps[u % 2], wg_hi, wg_lo, e, c).then_inc(gate_ready, 1)
                    if u == 0:
                        pe.wait_ge(route_dve, ROUTE * b + ROUTE)
                        for t in range(TILES):
                            mm = pe.transpose(outacc[0:E, t // 4, t % 4 * P:(t % 4 + 1) * P], wfull[:, t, :], ident[:])
                        mm.then_inc(w_turned, 1)
                        pe.wait_ge(wT_lo_done, b + 1)
                    else:
                        pe.wait_ge(wrow_done, UNITS * b + u)
                    for w in (wT_hi, wT_lo):
                        mm = pe.matmul(wrow_ps, rows_r[:, e * P:(e + 1) * P], w[:, c * HALF:(c + 1) * HALF],
                                       start=w is wT_hi, stop=w is wT_lo)
                    mm.then_inc(wrow_ready, 1)
                    if u:
                        pe.wait_ge(fuse_done, UNITS * b + u)
                    hidden(outacc, wu_hi, wu_lo, e, c).then_inc(up_ready, 1)
                    if u >= 2:
                        down(u - 2)
                down(UNITS - 2)
                down(UNITS - 1)

        @block.scalar
        def _(act):
            def split_weights(n, par):
                act.wait_ge(raw_in, 16 * n + 16)
                act.activation(wsl[par][:], w_raw[:], ACT.Copy).then_inc(w_hi_done, 1)

            def sdev_of(k):
                act.wait_ge(ln_moments, k)
                act.activation(sdev[:], moments[:, :, 1], ACT.Sqrt, bias=eps[:]).then_inc(ln_sdev, 1)

            def split_rotated(n, a, first):
                act.wait_ge(rope_sum, n * 4 + (2 * a + 2))
                if not first:
                    act.wait_ge(score_in[1], 32 * n)
                act.activation(qk_hi[a][:], rot[a][:], ACT.Copy).then_inc(qk_hi_done, 1)

            def split_values(n, par):
                act.wait_ge(aux_ready, n * NFEED + (FEED_AT[("value", 0, 0)] + 1))
                act.activation(vsl[par][:, :, :, 0:DH], aux[:].rearrange("p (t h d) -> p t h d", h=2, d=DH),
                               ACT.Copy).then_inc(v_hi_done, 1)

            def split_attention(m):
                act.wait_ge(out_ready, 2 * m + 1)
                act.activation(aT_hi[:], aux[:], ACT.Copy).then_inc(aT_hi_done, 1)

            def exponent(g, s):
                act.wait_ge(scores_ready, g * STEPS + (s + 1))
                act.activation(probs[s % 4][:].rearrange("p a n -> p (a n)"), slot[s % 2], ACT.Exp,
                               scale=SCALE).then_inc(probs_done, 1)

            def copy_out(g, s):
                act.wait_ge(pv_done, g * STEPS + (s + 1))
                act.activation(o_sb[s // 4 % 2][:].rearrange("p a q n -> p a (q n)"), outacc[:, :, 0:2 * VW],
                               ACT.Copy).then_inc(o_copied, 1)

            def normalise(g, s):
                half = s // 4
                act.wait_ge(o_added, g * 4 + (half + 1))
                act.wait_ge(o_recip, g * 4 + (half + 1))
                t = s % STEPS
                h, qh = t // 8, t % 8 // 4
                for q in range(4):
                    last = act.activation(attn[:, qh * 4 + q, h * DH:(h + 1) * DH], o_sum[half % 2][:, q, :], ACT.Copy,
                                          scale=o_rden[half % 2][:, q:q + 1])
                last.then_inc(o_done, 1)

            def lagged(g, s, finishes):
                if s % 4 == 2 and (s >= 6 or finishes):
                    copy_out(g, s - 3)
                if s % 4 == 1 and (s >= 9 or finishes):
                    normalise(g, s - 6)

            def attend(g, par, feeds, finishes):
                for s in range(STEPS):
                    lagged(g, s, finishes)
                    if finishes and s == ATTN_STEP + 1:
                        split_attention(g - 1)
                    exponent(g, s)
                    if feeds and s in (2, 3):
                        split_rotated(g + 1, s - 2, False)
                    if feeds and s == 3:
                        split_values(g + 1, 1 - par)
                    if s == 4:
                        split_weights(g + 2, par)

            act.wait_ge(fills_done, 1)
            split_weights(0, 0)
            split_weights(1, 1)
            act.wait_ge(consts_in, 16 * len(first_consts))
            with act.Fori(0, B) as b:
                n0 = b * PAIRS
                last = n0 + (PAIRS - 1)
                sdev_of(b * NORMS + 1)
                sdev_of(b * NORMS + 2)
                act.wait_ge(n_turned, b + 1)
                act.activation(hT[:], aux[:], ACT.Identity, scale=scale_sb[:], bias=bias_sb[:]).then_inc(h_done, 1)
                for i in range(2):
                    act.wait_ge(c_ready, 2 * b + (i + 1))
                    act.activation(c_hi[i][:], slot[i], ACT.Copy).then_inc(c_hi_done, 1)
                split_rotated(n0, 0, True)
                split_rotated(n0, 1, True)
                split_values(n0, 0)
                attend(n0, 0, True, False)
                with act.Fori(0, PAIRS // 2 - 1) as i:
                    attend(n0 + i * 2 + 1, 1, True, True)
                    attend(n0 + i * 2 + 2, 0, True, True)
                attend(last, 1, False, True)
                for s in range(STEPS, STEPS + 6):
                    lagged(last, s, True)
                split_attention(last)
                sdev_of(b * NORMS + 3)

            for n, (_, hi, _) in enumerate(experts):
                act.wait_ge(stage_in[n], 16)
                act.activation(hi[:], stage[n][:], ACT.Copy).then_inc(stage_hi, 1)
            with act.Fori(0, B) as b:
                sdev_of(b * NORMS_2 + (B * NORMS + 1))
                act.wait_ge(z_turned, b + 1)
                act.activation(zT[:], aux[:], ACT.Copy)
                act.activation(zT_hi[:], aux[:], ACT.Copy).then_inc(zT_done, 1)
                act.wait_ge(route_dve, ROUTE * b + 2)
                act.activation(lexp[:], lg[:], ACT.Exp).then_inc(route_act, 1)
                act.wait_ge(route_dve, ROUTE * b + 7)
                act.activation(egap[:], gap[:], ACT.Exp).then_inc(route_act, 1)

                def high(u):
                    act.wait_ge(fuse_done, UNITS * b + (u + 1))
                    if u >= 3:
                        act.wait_ge(down_done, UNITS * b + (u - 2))
                    act.activation(f_hi[u % 3][:], fuse[u % 2][:], ACT.Copy).then_inc(f_hi_done, 1)

                def turn_back(c):
                    act.wait_ge(down_done, UNITS * b + (c + 1) * E)
                    act.activation(dT[:], down_ps, ACT.Copy).then_inc(dT_done, 1)

                for u in range(UNITS):
                    act.wait_ge(gate_ready, UNITS * b + (u + 1))
                    if u >= 2:
                        act.wait_ge(actw_done, UNITS * b + (u - 1))
                    act.activation(act_sb[u % 2][:], gate_ps[u % 2], ACT.Silu).then_inc(act_done, 1)
                    if u == 0:
                        act.wait_ge(w_turned, b + 1)
                        act.activation(wT_hi[:], outacc[0:E].rearrange("p a n -> p (a n)"), ACT.Copy).then_inc(wT_hi_done, 1)
                    act.wait_ge(wrow_ready, UNITS * b + (u + 1))
                    act.activation(wrow_sb[u % 2][:], wrow_ps, ACT.Copy).then_inc(wrow_done, 1)
                    if u:
                        high(u - 1)
                    if u == E + 1:
                        turn_back(0)
                high(UNITS - 1)
                turn_back(1)
                sdev_of(b * NORMS_2 + (B * NORMS + 2))

        @block.vector
        def _(dve):
            def flat(t):
                return t[:].rearrange("p t d -> p (t d)")

            dve.memset(eps[:], LN_EPS)
            for h in range(2):
                dve.memset(k_ones[h][DH:DH + 2, :].bitcast(F32), 1.0)
                dve.memset(vsl[h][:, :, :, DH:DH + 1], 1.0)
                last = dve.memset(vsl[h][:, :, :, DH + 1:DH + 2], 0.0)
            last.then_inc(fills_done, 1)

            def split_weights(n, par):
                dve.wait_ge(w_hi_done, n + 1)
                dve.tensor_tensor(wsl[par][DH:P, 0:5, :], w_raw[DH:P, 0:5, :], wsl[par][DH:P, 0:5, :], ALU.subtract)
                dve.tensor_tensor(wo_lo[par][:], w_raw[:, 5, :], wsl[par][:, 5, :], ALU.subtract).then_inc(w_done, 1)

            def standing():
                dve.memset(spare[:], 0.0)

            def layer_norm(k, src, dst):
                standing()
                for t in range(TILES):
                    last = dve.bn_stats(stats[:, t, :], src[:, t, :])
                last.then_inc(ln_stats, 1)
                dve.wait_ge(ln_stats, k)
                standing()
                for t in range(TILES):
                    last = dve.bn_aggr(moments[:, t, :], stats[:, t, :])
                last.then_inc(ln_moments, 1)
                dve.wait_ge(ln_sdev, k)
                dve.reciprocal(rstd[:], sdev[:]).then_inc(ln_rstd, 1)
                dve.wait_ge(ln_rstd, k)
                for t in range(TILES):
                    last = dve.tensor_scalar(dst[:, t, :], src[:, t, :], moments[:, t, 0:1], rstd[:, t:t + 1],
                                             ALU.subtract, ALU.mult)
                last.then_inc(ln_done, 1)
                dve.wait_ge(ln_done, k)

            def feed_job(n, par, which, first):
                at = FEED_AT[which]
                kind, a, t = which
                if kind != "value":
                    dve.wait_ge(aux_ready, n * NFEED + (at + 1))
                if kind == "proj":
                    if at >= 2:
                        dve.wait_ge(rope_sum, n * 4 + (at - 1))
                        if not first:
                            dve.wait_ge(score_in[1], 32 * n)
                    cols = slice(t * HALF, (t + 1) * HALF)
                    dve.tensor_tensor(rot[a][:, cols], aux[:, 0:HALF], cos_sb[:, cols], ALU.mult)
                    dve.tensor_tensor(t_sin[at % 2][:], aux[:, HALF:2 * HALF], sin_sb[:, cols], ALU.mult).then_inc(aux_taken, 1)
                elif kind == "value":
                    dve.wait_ge(v_hi_done, n + 1)
                    dve.tensor_tensor(vsl[par][:, :, :, VLO:VW], aux[:].rearrange("p (t h d) -> p t h d", h=2, d=DH),
                                      vsl[par][:, :, :, 0:DH], ALU.subtract).then_inc(aux_taken, 1)
                elif kind == "max":
                    dve.tensor_reduce(row_max[a][:, t:t + 1], aux[:], AX, ALU.max).then_inc(aux_taken, 1)
                    if t == TILES - 1:
                        dve.wait_ge(aux_taken, n * NFEED + (at + 1))
                        dve.tensor_scalar(max_parts[a][:, 0:TILES], row_max[a][:], -1.0, None, ALU.mult).then_inc(max_hi, 1)
                        dve.wait_ge(max_hi, 2 * n + (a + 1))
                        dve.scalar_tensor_tensor(out=max_parts[a][:, TILES:2 * TILES], in0=row_max[a][:], scalar=-1.0,
                                                 in1=max_parts[a][:, 0:TILES], op0=ALU.mult,
                                                 op1=ALU.subtract).then_inc(max_split, 1)
                else:
                    dve.tensor_copy(max_turned[a][:], aux[0:2 * TILES, 0:P]).then_inc(aux_taken, 1)

            def split_attention(m):
                dve.wait_ge(aT_hi_done, m + 1)
                dve.tensor_tensor(aT_lo[:], aux[:], aT_hi[:], ALU.subtract).then_inc(out_taken, 1)

            def add_projected(m):
                dve.wait_ge(out_ready, 2 * m + 2)
                dve.tensor_tensor(oacc[:], aux[:], oacc[:], ALU.add).then_inc(out_taken, 1)

            def low(g, s):
                dve.wait_ge(probs_done, g * STEPS + (s + 1))
                p = probs[s % 4][:].rearrange("p a n -> p (a n)")
                dve.tensor_tensor(probs_lo[s % 2][:].rearrange("p a n -> p (a n)"), p,
                                  p.bitcast(BF16).rearrange("p (n two) -> p n two", two=2)[:, :, 1],
                                  ALU.subtract).then_inc(lo_dve, 1)

            def lagged(g, s, finishes):
                if (s >= 1 or finishes) and s <= STEPS and (s - 1) % STEPS in DVE_STEPS:
                    if s >= 3 or finishes:
                        dve.wait_ge(pv_done, g * STEPS + (s - 2))
                    low(g, s - 1)
                if s % 4 == 3 and (s >= 7 or finishes):
                    half = (s - 4) // 4
                    dve.wait_ge(o_copied, g * 4 + (half + 1))
                    sums = o_sb[half % 2][:].rearrange("p a q n -> p (a q) n")[:, :, DH]
                    dve.reciprocal(o_rden[half % 2][:], sums).then_inc(o_recip, 1)

            def attend(g, par, feeds, finishes):
                for s in range(STEPS):
                    jobs = [j for j in jobs_in(s, feeds, finishes) if j[0] != "value"]
                    if feeds and s == 3:
                        jobs = [("value", 0, 0)]
                    for k, which in enumerate(jobs or [None]):
                        if which == ATTN:
                            pass
                        elif which == OUT:
                            add_projected(g - 1)
                        elif which is not None:
                            feed_job(g + 1, 1 - par, which, False)
                        if k == 0:
                            lagged(g, s, finishes)
                    if s == 5:
                        split_weights(g + 2, par)
                    if finishes and s == ATTN_STEP + 1:
                        split_attention(g - 1)

            split_weights(0, 0)
            split_weights(1, 1)
            dve.wait_ge(consts_in, 16 * len(first_consts))
            with dve.Fori(0, B) as b:
                n0 = b * PAIRS
                last = n0 + (PAIRS - 1)
                dve.wait_ge(x_in, 16 * b + 16)
                dve.memset(oacc[:], 0.0)
                layer_norm(b * NORMS + 1, x_sb, batch_of(x1_all, b))
                layer_norm(b * NORMS + 2, batch_of(x1_all, b), n_sb)
                for i in range(2):
                    dve.wait_ge(c_hi_done, 2 * b + (i + 1))
                    dve.tensor_tensor(c_lo[i][:], slot[i], c_hi[i][:], ALU.subtract).then_inc(c_lo_done, 1)
                for which in FEED:
                    feed_job(n0, 0, which, True)
                attend(n0, 0, True, False)
                with dve.Fori(0, PAIRS // 2 - 1) as i:
                    attend(n0 + i * 2 + 1, 1, True, True)
                    attend(n0 + i * 2 + 2, 0, True, True)
                attend(last, 1, False, True)
                for s in (STEPS, STEPS + 3):
                    lagged(last, s, True)
                split_attention(last)
                add_projected(last)
                x1 = batch_of(x1_all, b)
                dve.wait_ge(o_turned, b + 1)
                dve.tensor_tensor(res_sb[:], slot[0].rearrange("p (t d) -> p t d", d=D), x1, ALU.add).then_inc(res_done, 1)
                dve.wait_ge(res_done, b + 1)
                layer_norm(b * NORMS + 3, res_sb, n_sb)
                dve.tensor_tensor(x1, x_sb[:], n_sb[:], ALU.add).then_inc(x1_done, 1)
                dve.wait_ge(x1_done, b + 1)

            dve.wait_ge(econsts_in, 16 * len(expert_consts))
            dve.tensor_copy(rows_r[:], rows_in[:]).then_inc(rows_done, 1)
            for n, (_, hi, lo) in enumerate(experts):
                dve.wait_ge(stage_hi, n + 1)
                dve.tensor_tensor(lo[:], stage[n][:], hi[:], ALU.subtract).then_inc(stage_lo, 1)
            with dve.Fori(0, B) as b:
                x1 = batch_of(x1_all, b)
                layer_norm(b * NORMS_2 + (B * NORMS + 1), x1, n_sb)
                dve.wait_ge(zT_done, b + 1)
                dve.tensor_tensor(zT_lo[:], aux[:], zT_hi[:], ALU.subtract).then_inc(z_lo_done, 1)

                def over(t):
                    return t.unsqueeze(2).to_broadcast([P, TILES, E])

                def step(ins, n):
                    ins.then_inc(route_dve, 1)
                    dve.wait_ge(route_dve, ROUTE * b + n)

                dve.wait_ge(logits_ready, b + 1)
                logits = outacc[:, 0, 0:TILES * E].rearrange("p (t e) -> p t e", e=E)
                step(dve.tensor_reduce(lmax[:], logits, AX, ALU.max), 1)
                step(dve.tensor_tensor(lg[:], logits, over(lmax[:]), ALU.subtract), 2)
                dve.wait_ge(route_act, 2 * b + 1)
                step(dve.tensor_reduce(lsum[:], lexp[:], AX, ALU.add), 3)
                step(dve.reciprocal(lrec[:], lsum[:]), 4)
                step(dve.tensor_tensor(pr[:], lexp[:], over(lrec[:]), ALU.mult), 5)
                standing()
                for t in range(TILES):
                    last = dve.max(top[:, t, :], pr[:, t, :])
                step(last, 6)
                step(dve.tensor_tensor(gap[:], top[:, :, 1], top[:, :, 0], ALU.subtract), 7)
                standing()
                for t in range(TILES):
                    last = dve.max_index(top_at[:, t, :], top[:, t, :], pr[:, t, :])
                step(last, 8)
                step(dve.tensor_copy(top_f[:], top_at[:]), 9)
                dve.wait_ge(route_act, 2 * b + 2)
                step(dve.tensor_scalar(eden[:], egap[:], 1.0, None, ALU.add), 10)
                step(dve.reciprocal(w_1[:], eden[:]), 11)
                step(dve.tensor_tensor(w_2[:], egap[:], w_1[:], ALU.mult), 12)
                dve.tensor_tensor(hot_1[:], ids_sb[:], over(top_f[:, :, 0]), ALU.is_equal)
                step(dve.tensor_tensor(hot_2[:], ids_sb[:], over(top_f[:, :, 1]), ALU.is_equal), 13)
                dve.tensor_tensor(hot_w1[:], hot_1[:], over(w_1[:]), ALU.mult)
                step(dve.tensor_tensor(hot_w2[:], hot_2[:], over(w_2[:]), ALU.mult), 14)
                step(dve.tensor_tensor(wfull[:], hot_w1[:], hot_w2[:], ALU.add), ROUTE)
                dve.wait_ge(wT_hi_done, b + 1)
                dve.tensor_tensor(wT_lo[:], outacc[0:E].rearrange("p a n -> p (a n)"), wT_hi[:], ALU.subtract).then_inc(wT_lo_done, 1)

                def low_hidden(u):
                    dve.wait_ge(f_hi_done, UNITS * b + (u + 1))
                    dve.tensor_tensor(flat(f_lo[u % 3]), flat(fuse[u % 2]), flat(f_hi[u % 3]), ALU.subtract).then_inc(f_lo_done, 1)

                def take_down(c):
                    dve.wait_ge(d_turned, CHUNKS * b + (c + 1))
                    tiles = TILES // CHUNKS
                    dve.tensor_copy(res_sb[:, c * tiles:(c + 1) * tiles, :].rearrange("p t d -> p (t d)"),
                                    down_ps).then_inc(d_taken, 1)

                for u in range(UNITS):
                    dve.wait_ge(up_ready, UNITS * b + (u + 1))
                    dve.wait_ge(actw_done, UNITS * b + (u + 1))
                    if u >= 2:
                        dve.wait_ge(f_lo_done, UNITS * b + (u - 1))
                    dve.tensor_tensor(flat(fuse[u % 2]), outacc[:].rearrange("p a n -> p (a n)"), flat(actw_sb[u % 2]),
                                      ALU.mult).then_inc(fuse_done, 1)
                    if u:
                        low_hidden(u - 1)
                    if u == E + 1:
                        take_down(0)
                low_hidden(UNITS - 1)
                take_down(1)
                dve.wait_ge(d_taken, CHUNKS * b + CHUNKS)
                layer_norm(b * NORMS_2 + (B * NORMS + 2), res_sb, n_sb)
                dve.tensor_tensor(x1, x1, n_sb[:], ALU.add).then_inc(result_done, 1)

        @block.gpsimd
        def _(pool):
            def rope_add(n, at):
                pool.wait_ge(aux_taken, n * NFEED + (at + 1))
                a, t = at // 2, at % 2
                part = rot[a][:, t * HALF:(t + 1) * HALF]
                pool.tensor_tensor(part, part, t_sin[at % 2][:], ALU.add).then_inc(rope_sum, 1)

            def low_rotated(n, a):
                pool.wait_ge(qk_hi_done, 2 * n + (a + 1))
                pool.tensor_tensor(rot[a][:], rot[a][:], qk_hi[a][:].bitcast(F32), ALU.subtract).then_inc(qk_lo_done, 1)

            def low(g, s):
                pool.wait_ge(probs_done, g * STEPS + (s + 1))
                pool.wait_ge(pv_done, g * STEPS + (s - 1))
                p = probs[s % 4][:].rearrange("p a n -> p (a n)")
                pool.tensor_tensor(probs_lo[s % 2][:].rearrange("p a n -> p (a n)"), p,
                                   p.bitcast(BF16).rearrange("p (n two) -> p n two", two=2)[:, :, 1],
                                   ALU.subtract).then_inc(lo_pool, 1)

            def add_parts(g, s):
                half = (s - 4) // 4
                pool.wait_ge(o_copied, g * 4 + (half + 1))
                sums = o_sb[half % 2][:].rearrange("p a q n -> p (a q) n")
                pool.tensor_tensor(o_sum[half % 2][:], sums[:, :, 0:DH], sums[:, :, VLO:VW], ALU.add).then_inc(o_added, 1)

            def attend(g, feeds, finishes):
                for s in range(STEPS):
                    if s % 4 == 3 and (s >= 7 or finishes):
                        add_parts(g, s)
                    if s - 1 in POOL_STEPS:
                        low(g, s - 1)
                    if feeds and s in (1, 2):
                        rope_add(g + 1, 2 * s - 2)
                        rope_add(g + 1, 2 * s - 1)
                    if feeds and s in (3, 4):
                        low_rotated(g + 1, s - 3)

            with pool.Fori(0, B) as b:
                n0 = b * PAIRS
                last = n0 + (PAIRS - 1)
                for at in range(4):
                    rope_add(n0, at)
                low_rotated(n0, 0)
                low_rotated(n0, 1)
                attend(n0, True, False)
                with pool.Fori(0, PAIRS // 2 - 1) as i:
                    attend(n0 + i * 2 + 1, True, True)
                    attend(n0 + i * 2 + 2, True, True)
                attend(last, False, True)
                add_parts(last, STEPS + 3)

            with pool.Fori(0, B) as b:
                for u in range(UNITS):
                    pool.wait_ge(act_done, UNITS * b + (u + 1))
                    pool.wait_ge(wrow_done, UNITS * b + (u + 1))
                    if u >= 2:
                        pool.wait_ge(fuse_done, UNITS * b + (u - 1))
                    pool.tensor_tensor(actw_sb[u % 2][:], act_sb[u % 2][:],
                                       wrow_sb[u % 2][:].unsqueeze(1).to_broadcast([P, FT, HALF]),
                                       ALU.mult).then_inc(actw_done, 1)


def rope_tables():
    inv_freq = 1.0 / ROPE_BASE ** (np.arange(0, DH, 2, dtype=np.float32) / DH)
    angles = np.outer(np.arange(S, dtype=np.float32), inv_freq)
    cos = np.concatenate([np.cos(angles), np.cos(angles)], -1)[:, ::2]
    sin = np.concatenate([np.sin(angles), np.sin(angles)], -1)[:, ::2]
    cos = np.repeat(cos, 2, axis=1)
    sin = np.stack([-sin, sin], axis=-1).reshape(S, DH)
    return (np.ascontiguousarray(np.tile(cos, (1, 2)).T.astype(np.float32)),
            np.ascontiguousarray(np.tile(sin, (1, 2)).T.astype(np.float32)))


def kernel(**inputs):
    import concourse.bacc as _bacc
    from concourse import mybir as _mybir
    from concourse.bass_utils import run_bass_kernel_spmd as _run

    a = {k: np.asarray(v) for k, v in inputs.items()}

    def rows_twice(w):
        return np.concatenate([w.T, w.T], axis=0)

    def swapped(w):
        return w.reshape(H * DH // 2, 2, DH)[:, ::-1].reshape(H * DH, DH)

    wq, wk, wv = a["L0_attn_w_up_q"], a["L0_attn_w_up_k"], a["L0_attn_w_up_v"]
    blocks = [rows_twice(w).reshape(P, PAIRS, P) for w in (wq, swapped(wq), wk, swapped(wk), wv)]
    w_out = a["L0_attn_w_out"].T.reshape(PAIRS, P, D)
    own = [np.stack([blk[:, n % PAIRS] for blk in blocks] + [w_out[(n - 2) % PAIRS]], axis=1)
           for n in range(PAIRS + AHEAD)]
    cos, sin = rope_tables()
    arrays = {
        "x": a["L0_attn_x"],
        "w_pairs": np.stack(own),
        "w_down": np.concatenate([a["L0_attn_w_down_q"].T] * 2 + [a["L0_attn_w_down_kv"].T] * 2, axis=1),
        "ln_scale": a["L0_attn_ln_scale"].reshape(D, 1),
        "ln_bias": a["L0_attn_ln_bias"].reshape(D, 1),
        "router": a["L0_ffn_router_kernel_DE"],
        "w_gate": a["L0_ffn_kernel_gating_EDF"].transpose(1, 0, 2).reshape(D, E * F),
        "w_up": a["L0_ffn_kernel_up_EDF"].transpose(1, 0, 2).reshape(D, E * F),
        "w_dn": a["L0_ffn_kernel_down_EFD"].reshape(E, FT, P, D).transpose(2, 0, 1, 3).reshape(P, E * FT * D),
        "rope_cos": cos,
        "rope_sin": sin,
        "identity": np.eye(P, dtype=np.float32),
        "expert_rows": np.repeat(np.eye(E, dtype=np.float32), P, axis=1),
        "expert_ids": np.broadcast_to(np.arange(E, dtype=np.float32), (P, TILES, E)),
    }
    nc = _bacc.Bacc("TRN2", target_bir_lowering=False, num_devices=1)
    fed, args = {}, {}
    for name, value in arrays.items():
        fed[f"{name}_dram"] = np.ascontiguousarray(value)
        args[name] = nc.dram_tensor(f"{name}_dram", value.shape, _mybir.dt.from_np(value.dtype), kind="ExternalInput").ap()
    out = nc.dram_tensor("out_dram", (B, S, D), _mybir.dt.float32, kind="ExternalOutput").ap()
    program(nc, out=out, **args)
    r = _run(nc, [fed], core_ids=[0])
    return r.results[0]["out_dram"]
```

```python
from contextlib import ExitStack

import numpy as np
import concourse.bass as bass
from concourse import mybir

F32 = mybir.dt.float32
F32R = mybir.dt.float32r
F16 = mybir.dt.float16
BF16 = mybir.dt.bfloat16
U32 = mybir.dt.uint32
ALU = mybir.AluOpType
ACT = mybir.ActivationFunctionType
AX = mybir.AxisListType.X

P = 128
B, S, D = 4, 1024, 128
H, DH = 16, 64
E, F = 8, 256
LN_EPS = 1e-5
ROPE_BASE = 10000.0
SCALE = 1.0 / 8.0

TILES = S // P
HALF = 512
CHUNKS = S // HALF
PAIRS = H // 2
STEPS = 16
FT = F // P
VW = 130
VLO = VW - DH
WBLOCKS = 5
LAST = PAIRS * B - 1
UNITS = CHUNKS * E
ROUTE = 15

FEED = ([("proj", a, c, swap) for a in range(2) for c in range(CHUNKS) for swap in range(2)]
        + [("value", 0, c, 0) for c in range(CHUNKS)]
        + [("max", 0, t, c) for t in range(TILES) for c in range(CHUNKS)]
        + [("max", 1, 0, c) for c in range(CHUNKS)] + [("turn", 0, 0, 0)]
        + [("max", 1, t, c) for t in range(1, TILES) for c in range(CHUNKS)] + [("turn", 1, 0, 0)])
NFEED = len(FEED)
FEED_AT = {job: n for n, job in enumerate(FEED)}
ATTN = [("attn", 0, c, 0) for c in range(CHUNKS)]
OUT = [("out", 0, c, 0) for c in range(CHUNKS)]
FEED_IN = {0: FEED[0:4], 1: FEED[4:8], 2: FEED[8:10], 5: FEED[10:12], 6: FEED[12:14], 7: FEED[14:18],
           8: FEED[18:20], 9: FEED[20:24], 10: FEED[24:28], 11: FEED[28:31], 12: FEED[31:34], 13: FEED[34:38],
           14: FEED[38:42], 15: FEED[42:44]}
FINISH_IN = {6: ATTN, 8: OUT}
WEIGHTS_STEP, WOUT_STEP = 4, 12
POOL_STEPS = (6, 7, 8, 9, 10, 11, 12, 13)
DVE_STEPS = tuple(s for s in range(STEPS) if s not in POOL_STEPS)
LAG = 2


def jobs_in(step, feeds, finishes):
    return (FINISH_IN.get(step, []) if finishes else []) + (FEED_IN.get(step, []) if feeds else [])


def low_parts_done(step):
    own = POOL_STEPS if step % STEPS in POOL_STEPS else DVE_STEPS
    return own is POOL_STEPS, len(own) * (step // STEPS) + own.index(step % STEPS) + 1


def program(nc, x, w_pairs, w_out, w_down, ln_scale, ln_bias, router, w_gate, w_up, w_dn,
            rope_cos, rope_sin, identity, expert_rows, expert_ids, out):
    with ExitStack() as ctx:
        def sb(name, shape, dt=F32, where=ctx):
            return where.enter_context(nc.sbuf_tensor(name, shape, dt))

        def sem(name):
            return ctx.enter_context(nc.semaphore(name))

        scores = ctx.enter_context(nc.psum_tensor("scores", [P, 2, 2, HALF], F32))
        aux = ctx.enter_context(nc.psum_tensor("aux", [P, 2 * HALF], F32))
        outacc = ctx.enter_context(nc.psum_tensor("outacc", [P, 2, HALF], F32))
        bank = [aux[:, i * HALF:(i + 1) * HALF] for i in range(2)]
        slot = [scores[:, i].rearrange("p a n -> p (a n)") for i in range(2)]
        gate_ps = [scores[:, i] for i in range(2)]
        wrow_ps = aux[:, 0:HALF]
        down_ps = aux[:, HALF:2 * HALF]

        ident = sb("ident", [P, P])
        eps = sb("eps", [P, 1])
        spare = sb("spare", [P, 1])
        x_all = sb("x_all", [P, B * TILES, D])
        oacc = sb("oacc", [D, B, S])
        moments_x = sb("moments_x", [P, B * TILES, 2])
        rstd_x = sb("rstd_x", [P, B * TILES])
        stats = sb("stats", [P, TILES, 6])
        moments = sb("moments", [P, TILES, 2])
        sdev = sb("sdev", [P, TILES])
        rstd = sb("rstd", [P, TILES])

        with ExitStack() as phase:
            def sb1(name, shape, dt=F32):
                return sb(name, shape, dt, phase)

            cos_sb = sb1("cos_sb", [P, S])
            sin_sb = sb1("sin_sb", [P, S])
            scale_sb = sb1("scale_sb", [P, 1])
            bias_sb = sb1("bias_sb", [P, 1])
            wd_sb = sb1("wd_sb", [D, 4 * DH])
            c_both = [[sb1(f"c_both{i}{b}", [P, S], F32R) for b in range(B)] for i in range(2)]
            w_raw = sb1("w_raw", [P, WBLOCKS, P])
            w_hi = sb1("w_hi", [P, WBLOCKS, P], F32R)
            w_lo = sb1("w_lo", [P, WBLOCKS, P], F32R)
            wo_raw = sb1("wo_raw", [P, D])
            wo_hi = sb1("wo_hi", [P, D], F32R)
            wo_lo = sb1("wo_lo", [P, D], F32R)
            vsl = [sb1(f"vsl{i}", [P, TILES, 2, VW], F16) for i in range(2)]
            t_sin = [sb1(f"t_sin{i}", [P, HALF]) for i in range(2)]
            rot = [sb1(f"rot{i}", [P, S]) for i in range(2)]
            qk_hi = [sb1(f"qk_hi{i}", [P, S], F32R) for i in range(2)]
            q_both = [[sb1(f"q_both{i}{h}", [P, S], F32R) for h in range(2)] for i in range(2)]
            k_twice = [[sb1(f"k_twice{i}{h}", [P, S], F32R) for h in range(2)] for i in range(2)]
            q_max = [sb1(f"q_max{h}", [DH + 2, S], F32R) for h in range(2)]
            k_ones = [sb1(f"k_ones{h}", [DH + 2, S], F32R) for h in range(2)]
            row_max = [sb1(f"row_max{h}", [P, CHUNKS, TILES]) for h in range(2)]
            max_all = [sb1(f"max_all{h}", [P, TILES]) for h in range(2)]
            max_parts = [sb1(f"max_parts{h}", [P, 2 * TILES], F32R) for h in range(2)]
            max_turned = [sb1(f"max_turned{h}", [2 * TILES, P], F32R) for h in range(2)]
            probs = [sb1(f"probs{i}", [P, 2, HALF]) for i in range(4)]
            probs_lo = [sb1(f"probs_lo{i}", [P, 2, HALF], F16) for i in range(2)]
            o_sb = [sb1(f"o_sb{i}", [P, 2, 2, VW]) for i in range(2)]
            o_sum = [sb1(f"o_sum{i}", [P, 4, DH]) for i in range(2)]
            o_rden = [sb1(f"o_rden{i}", [P, 4]) for i in range(2)]
            attn = sb1("attn", [P, TILES, P])
            aT_hi = sb1("aT_hi", [P, S], F32R)
            aT_lo = sb1("aT_lo", [P, S], F32R)
            n_front = probs[0][:].rearrange("p a (t d) -> p (a t) d", d=D)
            hT = rot[0]
            var_y = sb1("var_y", [P, TILES])
            rstd_y = sb1("rstd_y", [P, TILES])
            sdev_y = sb1("sdev_y", [P, TILES])

        router_sb = sb("router_sb", [D, E])
        ids_sb = sb("ids_sb", [P, TILES, E])
        rows_in = sb("rows_in", [E, E * P])
        rows_r = sb("rows_r", [E, E * P], F32R)
        stage = [sb(f"stage{i}", [P, E * F]) for i in range(3)]
        wg_hi = sb("wg_hi", [D, E * F], F32R)
        wg_lo = sb("wg_lo", [D, E * F], F32R)
        wu_hi = sb("wu_hi", [D, E * F], F32R)
        wu_lo = sb("wu_lo", [D, E * F], F32R)
        wn_hi = sb("wn_hi", [P, E * FT * D], F32R)
        wn_lo = sb("wn_lo", [P, E * FT * D], F32R)
        n_sb = sb("n_sb", [P, TILES, D])
        res_sb = sb("res_sb", [P, TILES, D])
        o_now = sb("o_now", [D, S])
        zT = sb("zT", [D, S])
        zT_hi = sb("zT_hi", [D, S], F32R)
        zT_lo = sb("zT_lo", [D, S], F32R)
        lg = sb("lg", [P, TILES, E])
        lmax = sb("lmax", [P, TILES])
        lexp = sb("lexp", [P, TILES, E])
        lsum = sb("lsum", [P, TILES])
        lrec = sb("lrec", [P, TILES])
        pr = sb("pr", [P, TILES, E])
        top = sb("top", [P, TILES, 8])
        top_at = sb("top_at", [P, TILES, 8], U32)
        top_f = sb("top_f", [P, TILES, 8])
        gap = sb("gap", [P, TILES])
        egap = sb("egap", [P, TILES])
        eden = sb("eden", [P, TILES])
        w_1 = sb("w_1", [P, TILES])
        w_2 = sb("w_2", [P, TILES])
        hot_1 = sb("hot_1", [P, TILES, E])
        hot_2 = sb("hot_2", [P, TILES, E])
        hot_w1 = sb("hot_w1", [P, TILES, E])
        hot_w2 = sb("hot_w2", [P, TILES, E])
        wfull = sb("wfull", [P, TILES, E])
        wT_hi = sb("wT_hi", [E, S], F32R)
        wT_lo = sb("wT_lo", [E, S], F32R)
        act_sb = [sb(f"act_sb{i}", [P, FT, HALF]) for i in range(2)]
        wrow_sb = [sb(f"wrow_sb{i}", [P, HALF]) for i in range(2)]
        actw_sb = [sb(f"actw_sb{i}", [P, FT, HALF]) for i in range(2)]
        fuse = [sb(f"fuse{i}", [P, FT, HALF]) for i in range(2)]
        f_hi = [sb(f"f_hi{i}", [P, FT, HALF], F32R) for i in range(3)]
        f_lo = [sb(f"f_lo{i}", [P, FT, HALF], F32R) for i in range(3)]
        dT = sb("dT", [D, HALF])

        consts_in, fills_done, x_in = sem("consts_in"), sem("fills_done"), sem("x_in")
        ln_stats, ln_moments, ln_sdev, ln_rstd, ln_done = (
            sem("ln_stats"), sem("ln_moments"), sem("ln_sdev"), sem("ln_rstd"), sem("ln_done"))
        ln_steps, y_sdev, ln_y_inverse, n_ready = sem("ln_steps"), sem("y_sdev"), sem("ln_y_inverse"), sem("n_ready")
        n_turned, h_done = sem("n_turned"), sem("h_done")
        c_ready, c_hi_done, c_lo_done = sem("c_ready"), sem("c_hi_done"), sem("c_lo_done")
        raw_in, w_hi_done, w_done, v_hi_done = sem("raw_in"), sem("w_hi_done"), sem("w_done"), sem("v_hi_done")
        wo_in, wo_hi_done, wo_done = sem("wo_in"), sem("wo_hi_done"), sem("wo_done")
        aux_ready, aux_taken = sem("aux_ready"), sem("aux_taken")
        out_ready, out_taken, aT_hi_done = sem("out_ready"), sem("out_taken"), sem("aT_hi_done")
        rope_sum, qk_hi_done, qk_lo_done = sem("rope_sum"), sem("qk_hi_done"), sem("qk_lo_done")
        max_in = [sem("max_in0"), sem("max_in1")]
        score_in = [sem("score_in0"), sem("score_in1")]
        max_whole = sem("max_whole")
        max_hi, max_split = sem("max_hi"), sem("max_split")
        rows_put = [sem("rows_put0"), sem("rows_put1")]
        scores_ready, probs_done = sem("scores_ready"), sem("probs_done")
        lo_dve, lo_pool = sem("lo_dve"), sem("lo_pool")
        pv_done, o_copied, o_recip, o_added, o_done = (
            sem("pv_done"), sem("o_copied"), sem("o_recip"), sem("o_added"), sem("o_done"))
        o_moved, o_turned, y_done, res_done, x1_done = (
            sem("o_moved"), sem("o_turned"), sem("y_done"), sem("res_done"), sem("x1_done"))
        econsts_in, rows_done = sem("econsts_in"), sem("rows_done")
        stage_in = [sem(f"stage_in{i}") for i in range(3)]
        stage_hi, stage_lo = sem("stage_hi"), sem("stage_lo")
        z_turned, zT_done, z_lo_done = sem("z_turned"), sem("zT_done"), sem("z_lo_done")
        logits_ready, route_dve, route_act = sem("logits_ready"), sem("route_dve"), sem("route_act")
        w_turned, wT_hi_done, wT_lo_done = sem("w_turned"), sem("wT_hi_done"), sem("wT_lo_done")
        gate_ready, wrow_ready, up_ready, down_done = (
            sem("gate_ready"), sem("wrow_ready"), sem("up_ready"), sem("down_done"))
        act_done, wrow_done, actw_done = sem("act_done"), sem("wrow_done"), sem("actw_done")
        fuse_done, f_hi_done, f_lo_done = sem("fuse_done"), sem("f_hi_done"), sem("f_lo_done")
        dT_done, d_turned, d_taken, result_done, stored = (
            sem("dT_done"), sem("d_turned"), sem("d_taken"), sem("result_done"), sem("stored"))

        experts = [(w_gate, wg_hi, wg_lo), (w_up, wu_hi, wu_lo), (w_dn, wn_hi, wn_lo)]
        first_consts = ((ident, identity), (cos_sb, rope_cos), (sin_sb, rope_sin), (scale_sb, ln_scale),
                        (bias_sb, ln_bias), (wd_sb, w_down))
        expert_consts = ((router_sb, router), (ids_sb, expert_ids), (rows_in, expert_rows))
        NORMS = 3

        block = ctx.enter_context(nc.Block())

        def batch_of(t, b):
            return t[:, bass.ds(b * TILES, TILES), :]

        def in_dram(t, b):
            return t[bass.ds(b, 1)].rearrange("b (t p) d -> p (b t) d", p=P)

        @block.sync
        def _(sp):
            for dst, src in first_consts:
                sp.dma_start(dst[:], src).then_inc(consts_in, 16)
            for b in range(B):
                sp.dma_start(batch_of(x_all, b), in_dram(x, b)).then_inc(x_in, 16)

            def load_weights(pair):
                sp.dma_start(w_raw[:], w_pairs[bass.ds(pair, 1)].rearrange("a p c n -> p (a c) n")).then_inc(raw_in, 16)
                sp.dma_start(wo_raw[:], w_out[bass.ds(pair, 1)].rearrange("a p n -> (a p) n")).then_inc(wo_in, 16)

            load_weights(0)

            def put(dst, src, h, signal):
                sp.dma_start(dst.bitcast(F32), src[h * DH:(h + 1) * DH, :].bitcast(F32)).then_inc(signal, 16)

            def feed(n, par, first):
                sp.wait_ge(qk_hi_done, 2 * n + 2)
                for h in range(2):
                    put(q_both[par][h][0:DH, :], qk_hi[0], h, max_in[h])
                    put(k_twice[par][h][0:DH, :], qk_hi[1], h, max_in[h])
                    put(k_twice[par][h][DH:P, :], qk_hi[1], h, max_in[h])
                    if h == 0:
                        sp.wait_ge(qk_lo_done, 2 * n + 1)
                    put(q_both[par][h][DH:P, :], rot[0], h, max_in[h])
                sp.wait_ge(qk_lo_done, 2 * n + 2)
                for h in range(2):
                    if not first:
                        sp.wait_ge(scores_ready, n * STEPS - (STEPS // 2) * (1 - h))
                    put(q_max[h][0:DH, :], qk_hi[0], h, score_in[h])
                    put(k_ones[h][0:DH, :], rot[1], h, score_in[h])
                    sp.wait_ge(aux_taken, n * NFEED + (FEED_AT[("turn", h, 0, 0)] + 1))
                    for part in range(2):
                        sp.dma_start(q_max[h][DH + part:DH + part + 1, :].bitcast(F32),
                                     max_turned[h][part * TILES:(part + 1) * TILES, :].bitcast(F32)).then_inc(rows_put[h], 16)

            feed(0, 0, True)
            feed(1, 1, False)
            with sp.Fori(0, PAIRS - 1) as pair:
                sp.wait_ge(w_done, pair + 1)
                sp.wait_ge(wo_done, pair + 1)
                load_weights(pair + 1)
                for k in range(2, B + 2):
                    feed(pair * B + k, k % 2, False)
            for n in range(PAIRS * B - B + 2, PAIRS * B):
                feed(n, n % 2, False)
            sp.wait_ge(x_in, 16 * B)
            sp.wait_ge(out_taken, 4 * PAIRS * B)
            for dst, src in expert_consts:
                sp.dma_start(dst[:], src).then_inc(econsts_in, 16)
            for n, (src, _, _) in enumerate(experts):
                sp.dma_start(stage[n][:], src).then_inc(stage_in[n], 16)
            with sp.Fori(0, B) as b:
                sp.wait_ge(result_done, b + 1)
                sp.dma_start(in_dram(out, b), batch_of(x_all, b)).then_inc(stored, 16)
            sp.wait_ge(stored, 16 * B)

        @block.tensor
        def _(pe):
            def free(n, m, before):
                if before in ATTN:
                    pe.wait_ge(out_taken, 4 * m + (ATTN.index(before) + 1))
                elif before in OUT:
                    pe.wait_ge(out_taken, 4 * m + (OUT.index(before) + 3))
                elif before is not None:
                    pe.wait_ge(aux_taken, n * NFEED + (FEED_AT[before] + 1))

            def feed_job(n, b, bank, which):
                kind, a, t, c = which
                if kind == "proj":
                    for w in (w_hi, w_lo):
                        mm = pe.matmul(bank, w[:, 2 * a + c, :], c_both[a][b][:, t * HALF:(t + 1) * HALF],
                                       start=w is w_hi, stop=w is w_lo)
                elif kind == "value":
                    for i in range(HALF // P):
                        for w in (w_hi, w_lo):
                            k0 = t * HALF + i * P
                            mm = pe.matmul(bank[:, i * P:(i + 1) * P], c_both[1][b][:, k0:k0 + P], w[:, 4, :],
                                           start=w is w_hi, stop=w is w_lo)
                elif kind == "max":
                    if t == 0 and c == 0:
                        pe.wait_ge(max_in[a], 64 * n + 64)
                    mm = pe.matmul(bank, q_both[b % 2][a][:, t * P:(t + 1) * P],
                                   k_twice[b % 2][a][:, c * HALF:(c + 1) * HALF], start=True, stop=True)
                else:
                    pe.wait_ge(max_split, 2 * n + (a + 1))
                    mm = pe.transpose(bank[0:2 * TILES, 0:P], max_parts[a][:].bitcast(F32), ident[:])
                mm.then_inc(aux_ready, 1)

            def turn_attention(m, bank, c):
                pe.wait_ge(o_done, m * 4 + (3 + c))
                for t in range(HALF // P):
                    mm = pe.transpose(bank[:, t * P:(t + 1) * P], attn[:, c * (HALF // P) + t, :], ident[:])
                mm.then_inc(out_ready, 1)

            def project_out(m, bank, c):
                pe.wait_ge(out_taken, 4 * m + (c + 1))
                for k, (w, a) in enumerate(((wo_hi, aT_hi), (wo_lo, aT_hi), (wo_hi, aT_lo))):
                    mm = pe.matmul(bank, w[:], a[:, c * HALF:(c + 1) * HALF], start=k == 0, stop=k == 2)
                mm.then_inc(out_ready, 1)

            def score(g, par, s, first):
                h, qh, kp = s // 8, s % 8 // 4, s % 4
                if s >= 2 or not first:
                    pe.wait_ge(probs_done, g * STEPS + (s - 1))
                if s % 8 == 0:
                    pe.wait_ge(score_in[h], 32 * g + 32)
                    pe.wait_ge(rows_put[h], 32 * g + 32)
                for i in range(2):
                    k0 = (2 * kp + i) * P
                    pe.matmul(scores[:, s % 2, i, :], k_twice[par][h][:, k0:k0 + P],
                              q_both[par][h][:, qh * HALF:(qh + 1) * HALF], start=True, stop=False)
                    mm = pe.matmul(scores[:, s % 2, i, :], k_ones[h][:, k0:k0 + P],
                                   q_max[h][:, qh * HALF:(qh + 1) * HALF], start=False, stop=True)
                mm.then_inc(scores_ready, 1)

            def values(g, par, s, i, first):
                t = s % STEPS
                h, kp = t // 8, t % 4
                pool, count = low_parts_done(s)
                if i == 0:
                    if s == 0:
                        pe.wait_ge(aux_taken, g * NFEED + (FEED_AT[("value", 0, 1, 0)] + 1))
                    if kp == 0 and not (first and s == 0):
                        pe.wait_ge(o_copied, g * 4 + s // 4)
                    pe.wait_ge(lo_pool if pool else lo_dve, g * 8 + count)
                high = probs[t % 4][:, i, :].bitcast(BF16).rearrange("p (n two) -> p n two", two=2)
                v = vsl[par][:, 2 * kp + i, h, :]
                for q in range(4):
                    acc = outacc[:, q // 2, q % 2 * VW:(q % 2 + 1) * VW]
                    opens = kp == 0 and i == 0 and q % 2 == 0
                    pe.matmul(acc, high[:, q * P:(q + 1) * P, 1], v, start=opens, stop=False, skip_group_check=True)
                    mm = pe.matmul(acc[:, 0:VLO], probs_lo[t % 2][:, i, q * P:(q + 1) * P], v[:, 0:VLO],
                                   start=False, stop=kp == 3 and i == 1, skip_group_check=True)
                if i == 1:
                    mm.then_inc(pv_done, 1)

            def attend(g, b, pair, feeds, finishes):
                par = b % 2
                in_bank = [(g, FEED[-2]), (g, FEED[-1])]
                count = 0
                for s in range(STEPS):
                    score(g, par, s, not finishes)
                    jobs = jobs_in(s, feeds, finishes)
                    for k in range(max(len(jobs), 2)):
                        if k < len(jobs):
                            which, at = jobs[k], count % 2
                            count += 1
                            free(in_bank[at][0], g - 1, in_bank[at][1])
                            if which in ATTN:
                                turn_attention(g - 1, bank[at], which[2])
                            elif which in OUT:
                                if which == OUT[0] and b == 1:
                                    pe.wait_ge(wo_done, pair + 1)
                                project_out(g - 1, bank[at], which[2])
                            else:
                                if which == FEED[0] and b == B - 1:
                                    pe.wait_ge(w_done, pair + 2)
                                feed_job(g + 1, (b + 1) % B, bank[at], which)
                            in_bank[at] = (g + 1, which)
                        if k < 2 and (s >= LAG or finishes):
                            values(g, par if s >= LAG else 1 - par, s - LAG, k, not finishes)

            pe.wait_ge(consts_in, 16 * len(first_consts))
            pe.wait_ge(fills_done, 1)
            for b in range(B):
                pe.wait_ge(n_ready, b + 1)
                if b:
                    pe.wait_ge(h_done, b)
                for t in range(TILES):
                    mm = pe.transpose(aux[:, t * P:(t + 1) * P], n_front[:, t, :], ident[:])
                mm.then_inc(n_turned, 1)
                pe.wait_ge(h_done, b + 1)
                if b:
                    pe.wait_ge(c_lo_done, 2 * b)
                for i in range(2):
                    for c in range(CHUNKS):
                        mm = pe.matmul(scores[:, i, c, :], wd_sb[:, i * P:(i + 1) * P], hT[:, c * HALF:(c + 1) * HALF],
                                       start=True, stop=True)
                    mm.then_inc(c_ready, 1)
            pe.wait_ge(c_lo_done, 2 * B)
            pe.wait_ge(w_done, 1)
            for k, which in enumerate(FEED):
                free(0, None, FEED[k - 2] if k >= 2 else None)
                feed_job(0, 0, bank[k % 2], which)
            attend(0, 0, 0, True, False)
            with pe.Fori(0, PAIRS - 1) as pair:
                for b in range(1, B):
                    attend(pair * B + b, b, pair, True, True)
                attend(pair * B + B, 0, pair + 1, True, True)
            for b in range(1, B):
                attend(LAST - (B - 1 - b), b, PAIRS - 1, b < B - 1, True)
            for s in range(STEPS, STEPS + LAG):
                for i in range(2):
                    values(LAST, (B - 1) % 2, s - LAG, i, False)
            for c in range(CHUNKS):
                free(None, LAST - 1, OUT[c])
                turn_attention(LAST, bank[c], c)
            for c in range(CHUNKS):
                project_out(LAST, bank[c], c)

            pe.wait_ge(econsts_in, 16 * len(expert_consts))
            pe.wait_ge(rows_done, 1)
            with pe.Fori(0, B) as b:
                pe.wait_ge(o_moved, b + 1)
                for t in range(TILES):
                    mm = pe.transpose(aux[:, t * P:(t + 1) * P], o_now[:, t * P:(t + 1) * P], ident[:])
                mm.then_inc(o_turned, 1)
                pe.wait_ge(ln_done, b * NORMS + 2)
                for t in range(TILES):
                    mm = pe.transpose(aux[:, t * P:(t + 1) * P], n_sb[:, t, :], ident[:])
                mm.then_inc(z_turned, 1)
                pe.wait_ge(zT_done, b + 1)
                for t in range(TILES):
                    mm = pe.matmul(outacc[:, 0, t * E:(t + 1) * E], zT[:, t * P:(t + 1) * P], router_sb[:], start=True, stop=True)
                mm.then_inc(logits_ready, 1)
                pe.wait_ge(z_lo_done, b + 1)
                pe.wait_ge(stage_lo, len(experts))

                def hidden(dst, w_hi, w_lo, e, c):
                    for ft in range(FT):
                        f0 = e * F + ft * P
                        for k, (w, z) in enumerate(((w_hi, zT_hi), (w_lo, zT_hi), (w_hi, zT_lo))):
                            mm = pe.matmul(dst[:, ft, :], w[:, f0:f0 + P], z[:, c * HALF:(c + 1) * HALF],
                                           start=k == 0, stop=k == 2)
                    return mm

                def down(u):
                    c, e = u // E, u % E
                    if e == 0 and c:
                        pe.wait_ge(d_taken, CHUNKS * b + c)
                    pe.wait_ge(f_lo_done, UNITS * b + (u + 1))
                    for ft in range(FT):
                        w0 = (e * FT + ft) * D
                        for k, (w, f) in enumerate(((wn_hi, f_hi), (wn_lo, f_hi), (wn_hi, f_lo))):
                            mm = pe.matmul(down_ps, w[:, w0:w0 + D], f[u % 3][:, ft, :],
                                           start=e == 0 and ft == 0 and k == 0,
                                           stop=e == E - 1 and ft == FT - 1 and k == 2)
                    mm.then_inc(down_done, 1)
                    if e == E - 1:
                        pe.wait_ge(dT_done, CHUNKS * b + (c + 1))
                        for t in range(HALF // P):
                            mm = pe.transpose(down_ps[:, t * P:(t + 1) * P], dT[:, t * P:(t + 1) * P], ident[:])
                        mm.then_inc(d_turned, 1)

                for u in range(UNITS):
                    c, e = u // E, u % E
                    if u >= 2:
                        pe.wait_ge(act_done, UNITS * b + (u - 1))
                    hidden(gate_ps[u % 2], wg_hi, wg_lo, e, c).then_inc(gate_ready, 1)
                    if u == 0:
                        pe.wait_ge(route_dve, ROUTE * b + ROUTE)
                        for t in range(TILES):
                            mm = pe.transpose(outacc[0:E, t // 4, t % 4 * P:(t % 4 + 1) * P], wfull[:, t, :], ident[:])
                        mm.then_inc(w_turned, 1)
                        pe.wait_ge(wT_lo_done, b + 1)
                    else:
                        pe.wait_ge(wrow_done, UNITS * b + u)
                    for w in (wT_hi, wT_lo):
                        mm = pe.matmul(wrow_ps, rows_r[:, e * P:(e + 1) * P], w[:, c * HALF:(c + 1) * HALF],
                                       start=w is wT_hi, stop=w is wT_lo)
                    mm.then_inc(wrow_ready, 1)
                    if u:
                        pe.wait_ge(fuse_done, UNITS * b + u)
                    hidden(outacc, wu_hi, wu_lo, e, c).then_inc(up_ready, 1)
                    if u >= 2:
                        down(u - 2)
                down(UNITS - 2)
                down(UNITS - 1)

        @block.scalar
        def _(act):
            def split_weights(pair):
                act.wait_ge(raw_in, 16 * pair + 16)
                act.activation(w_hi[:], w_raw[:], ACT.Copy).then_inc(w_hi_done, 1)

            def split_output(pair):
                act.wait_ge(wo_in, 16 * pair + 16)
                act.activation(wo_hi[:], wo_raw[:], ACT.Copy).then_inc(wo_hi_done, 1)

            def sdev_of(k, variances):
                act.wait_ge(ln_moments, k)
                act.activation(sdev[:], variances, ACT.Sqrt, bias=eps[:]).then_inc(ln_sdev, 1)

            def split_rotated(n, a, first):
                act.wait_ge(rope_sum, n * 4 + (2 * a + 2))
                if not first:
                    act.wait_ge(score_in[1], 32 * n)
                act.activation(qk_hi[a][:], rot[a][:], ACT.Copy).then_inc(qk_hi_done, 1)

            def split_values(n, par, c):
                at = FEED_AT[("value", 0, c, 0)]
                tiles = HALF // P
                act.wait_ge(aux_ready, n * NFEED + (at + 1))
                act.activation(vsl[par][:, c * tiles:(c + 1) * tiles, :, 0:DH],
                               bank[at % 2].rearrange("p (t h d) -> p t h d", h=2, d=DH),
                               ACT.Copy).then_inc(v_hi_done, 1)

            def split_attention(m, c):
                act.wait_ge(out_ready, 4 * m + (c + 1))
                act.activation(aT_hi[:, c * HALF:(c + 1) * HALF], bank[c], ACT.Copy).then_inc(aT_hi_done, 1)

            def exponent(g, s):
                act.wait_ge(scores_ready, g * STEPS + (s + 1))
                act.activation(probs[s % 4][:].rearrange("p a n -> p (a n)"), slot[s % 2], ACT.Exp,
                               scale=SCALE).then_inc(probs_done, 1)

            def copy_out(g, s):
                act.wait_ge(pv_done, g * STEPS + (s + 1))
                act.activation(o_sb[s // 4 % 2][:].rearrange("p a q n -> p a (q n)"), outacc[:, :, 0:2 * VW],
                               ACT.Copy).then_inc(o_copied, 1)

            def normalise(g, s):
                half = s // 4
                act.wait_ge(o_added, g * 4 + (half + 1))
                act.wait_ge(o_recip, g * 4 + (half + 1))
                t = s % STEPS
                h, qh = t // 8, t % 8 // 4
                for q in range(4):
                    last = act.activation(attn[:, qh * 4 + q, h * DH:(h + 1) * DH], o_sum[half % 2][:, q, :], ACT.Copy,
                                          scale=o_rden[half % 2][:, q:q + 1])
                last.then_inc(o_done, 1)

            def lagged(g, s, finishes):
                if s % 4 == 2 and (s >= 6 or finishes):
                    copy_out(g, s - 3)
                if s % 4 == 1 and (s >= 9 or finishes):
                    normalise(g, s - 6)

            def attend(g, b, pair, feeds, finishes, more=True):
                for s in range(STEPS):
                    lagged(g, s, finishes)
                    exponent(g, s)
                    if finishes and s == 6:
                        for c in range(CHUNKS):
                            split_attention(g - 1, c)
                    if feeds and s in (1, 2):
                        split_rotated(g + 1, s - 1, False)
                    if feeds and s == 2:
                        for c in range(CHUNKS):
                            split_values(g + 1, 1 - b % 2, c)
                    if b == B - 2 and s == WEIGHTS_STEP and more:
                        act.wait_ge(aux_ready, (g + 1) * NFEED + (FEED_AT[("value", 0, 1, 0)] + 1))
                        split_weights(pair + 1)
                    if b == 0 and s == WOUT_STEP:
                        if finishes:
                            act.wait_ge(out_ready, 4 * g)
                        split_output(pair)

            act.wait_ge(fills_done, 1)
            split_weights(0)
            act.wait_ge(consts_in, 16 * len(first_consts))
            for b in range(B):
                if b:
                    act.wait_ge(ln_rstd, b)
                sdev_of(b + 1, moments_x[:, b * TILES:(b + 1) * TILES, 1])
                act.wait_ge(ln_steps, 2 * b + 2)
                act.activation(sdev_y[:], var_y[:], ACT.Sqrt, bias=eps[:]).then_inc(y_sdev, 1)
                if b:
                    for i in range(2):
                        act.wait_ge(c_ready, 2 * (b - 1) + (i + 1))
                        act.activation(c_both[i][b - 1][:], slot[i], ACT.Copy).then_inc(c_hi_done, 1)
                act.wait_ge(n_turned, b + 1)
                act.activation(hT[:], aux[:], ACT.Identity, scale=scale_sb[:], bias=bias_sb[:]).then_inc(h_done, 1)
            for i in range(2):
                act.wait_ge(c_ready, 2 * (B - 1) + (i + 1))
                act.activation(c_both[i][B - 1][:], slot[i], ACT.Copy).then_inc(c_hi_done, 1)
            split_rotated(0, 0, True)
            split_rotated(0, 1, True)
            for c in range(CHUNKS):
                split_values(0, 0, c)
            attend(0, 0, 0, True, False)
            with act.Fori(0, PAIRS - 1) as pair:
                for b in range(1, B):
                    attend(pair * B + b, b, pair, True, True)
                attend(pair * B + B, 0, pair + 1, True, True)
            for b in range(1, B):
                attend(LAST - (B - 1 - b), b, PAIRS - 1, b < B - 1, True, False)
            for s in range(STEPS, STEPS + 6):
                lagged(LAST, s, True)
            for c in range(CHUNKS):
                split_attention(LAST, c)

            for n, (_, hi, _) in enumerate(experts):
                act.wait_ge(stage_in[n], 16)
                act.activation(hi[:], stage[n][:], ACT.Copy).then_inc(stage_hi, 1)
            with act.Fori(0, B) as b:
                sdev_of(b * NORMS + (B + 1), moments[:, :, 1])
                sdev_of(b * NORMS + (B + 2), moments[:, :, 1])
                act.wait_ge(z_turned, b + 1)
                act.activation(zT[:], aux[:], ACT.Copy)
                act.activation(zT_hi[:], aux[:], ACT.Copy).then_inc(zT_done, 1)
                act.wait_ge(route_dve, ROUTE * b + 2)
                act.activation(lexp[:], lg[:], ACT.Exp).then_inc(route_act, 1)
                act.wait_ge(route_dve, ROUTE * b + 7)
                act.activation(egap[:], gap[:], ACT.Exp).then_inc(route_act, 1)

                def high(u):
                    act.wait_ge(fuse_done, UNITS * b + (u + 1))
                    if u >= 3:
                        act.wait_ge(down_done, UNITS * b + (u - 2))
                    act.activation(f_hi[u % 3][:], fuse[u % 2][:], ACT.Copy).then_inc(f_hi_done, 1)

                def turn_back(c):
                    act.wait_ge(down_done, UNITS * b + (c + 1) * E)
                    act.activation(dT[:], down_ps, ACT.Copy).then_inc(dT_done, 1)

                for u in range(UNITS):
                    act.wait_ge(gate_ready, UNITS * b + (u + 1))
                    if u >= 2:
                        act.wait_ge(actw_done, UNITS * b + (u - 1))
                    act.activation(act_sb[u % 2][:], gate_ps[u % 2], ACT.Silu).then_inc(act_done, 1)
                    if u == 0:
                        act.wait_ge(w_turned, b + 1)
                        act.activation(wT_hi[:], outacc[0:E].rearrange("p a n -> p (a n)"), ACT.Copy).then_inc(wT_hi_done, 1)
                    act.wait_ge(wrow_ready, UNITS * b + (u + 1))
                    act.activation(wrow_sb[u % 2][:], wrow_ps, ACT.Copy).then_inc(wrow_done, 1)
                    if u:
                        high(u - 1)
                    if u == E + 1:
                        turn_back(0)
                high(UNITS - 1)
                turn_back(1)
                sdev_of(b * NORMS + (B + 3), moments[:, :, 1])

        @block.vector
        def _(dve):
            def flat(t):
                return t[:].rearrange("p t d -> p (t d)")

            dve.memset(eps[:], LN_EPS)
            for h in range(2):
                dve.memset(k_ones[h][DH:DH + 2, :].bitcast(F32), 1.0)
                dve.memset(vsl[h][:, :, :, DH:DH + 1], 1.0)
                last = dve.memset(vsl[h][:, :, :, DH + 1:DH + 2], 0.0)
            last.then_inc(fills_done, 1)

            for b in range(B):
                dve.memset(oacc[:, b, :], 0.0)

            def split_weights(pair):
                dve.wait_ge(w_hi_done, pair + 1)
                dve.tensor_tensor(w_lo[:], w_raw[:], w_hi[:], ALU.subtract).then_inc(w_done, 1)

            def split_output(pair):
                dve.wait_ge(wo_hi_done, pair + 1)
                dve.tensor_tensor(wo_lo[:], wo_raw[:], wo_hi[:], ALU.subtract).then_inc(wo_done, 1)

            def standing():
                dve.memset(spare[:], 0.0)

            def moments_of(k, src, into, inverse):
                standing()
                for t in range(TILES):
                    last = dve.bn_stats(stats[:, t, :], src[:, t, :])
                last.then_inc(ln_stats, 1)
                dve.wait_ge(ln_stats, k)
                standing()
                for t in range(TILES):
                    last = dve.bn_aggr(into[:, t, :], stats[:, t, :])
                last.then_inc(ln_moments, 1)
                dve.wait_ge(ln_sdev, k)
                dve.reciprocal(inverse, sdev[:]).then_inc(ln_rstd, 1)
                dve.wait_ge(ln_rstd, k)

            def normalise(src, dst, means, inverse):
                for t in range(TILES):
                    last = dve.tensor_scalar(dst[:, t, :], src[:, t, :], means[:, t, 0:1], inverse[:, t:t + 1],
                                             ALU.subtract, ALU.mult)
                return last

            def layer_norm(n, src, dst):
                moments_of(n + B, src, moments, rstd[:])
                normalise(src, dst, moments, rstd).then_inc(ln_done, 1)
                dve.wait_ge(ln_done, n)

            def norm_twice(b):
                tokens = batch_of(x_all, b)
                means = moments_x[:, b * TILES:(b + 1) * TILES, :]
                inverse = rstd_x[:, b * TILES:(b + 1) * TILES]
                dve.wait_ge(x_in, 16 * B)
                moments_of(b + 1, tokens, means, inverse)
                dve.tensor_tensor(var_y[:], means[:, :, 1], inverse, ALU.mult).then_inc(ln_steps, 1)
                dve.wait_ge(ln_steps, 2 * b + 1)
                dve.tensor_tensor(var_y[:], var_y[:], inverse, ALU.mult).then_inc(ln_steps, 1)
                dve.wait_ge(y_sdev, b + 1)
                dve.reciprocal(rstd_y[:], sdev_y[:]).then_inc(ln_y_inverse, 1)
                dve.wait_ge(ln_y_inverse, 2 * b + 1)
                dve.tensor_tensor(rstd_y[:], rstd_y[:], inverse, ALU.mult).then_inc(ln_y_inverse, 1)
                dve.wait_ge(ln_y_inverse, 2 * b + 2)
                if b:
                    dve.wait_ge(n_turned, b)
                normalise(tokens, n_front, means, rstd_y).then_inc(n_ready, 1)

            def feed_job(n, par, which, first):
                at = FEED_AT[which]
                kind, a, t, c = which
                src = bank[at % 2]
                if kind != "value":
                    dve.wait_ge(aux_ready, n * NFEED + (at + 1))
                if kind == "proj":
                    k = 2 * a + t
                    cols = slice(t * HALF, (t + 1) * HALF)
                    if c == 0:
                        if k == 2 and not first:
                            dve.wait_ge(score_in[1], 32 * n)
                        dve.tensor_tensor(rot[a][:, cols], src, cos_sb[:, cols], ALU.mult).then_inc(aux_taken, 1)
                    else:
                        if k >= 2:
                            dve.wait_ge(rope_sum, n * 4 + (k - 1))
                        dve.tensor_tensor(t_sin[k % 2][:], src, sin_sb[:, cols], ALU.mult).then_inc(aux_taken, 1)
                elif kind == "value":
                    tiles = slice(t * (HALF // P), (t + 1) * (HALF // P))
                    dve.wait_ge(v_hi_done, CHUNKS * n + (t + 1))
                    dve.tensor_tensor(vsl[par][:, tiles, :, VLO:VW], src.rearrange("p (t h d) -> p t h d", h=2, d=DH),
                                      vsl[par][:, tiles, :, 0:DH], ALU.subtract).then_inc(aux_taken, 1)
                elif kind == "max":
                    dve.tensor_reduce(row_max[a][:, c, t:t + 1], src, AX, ALU.max).then_inc(aux_taken, 1)
                    if t == TILES - 1 and c == CHUNKS - 1:
                        dve.wait_ge(aux_taken, n * NFEED + (at + 1))
                        dve.tensor_tensor(max_all[a][:], row_max[a][:, 0, :], row_max[a][:, 1, :],
                                          ALU.max).then_inc(max_whole, 1)
                        dve.wait_ge(max_whole, 2 * n + (a + 1))
                        dve.tensor_scalar(max_parts[a][:, 0:TILES], max_all[a][:], -1.0, None, ALU.mult).then_inc(max_hi, 1)
                        dve.wait_ge(max_hi, 2 * n + (a + 1))
                        dve.scalar_tensor_tensor(out=max_parts[a][:, TILES:2 * TILES], in0=max_all[a][:], scalar=-1.0,
                                                 in1=max_parts[a][:, 0:TILES], op0=ALU.mult,
                                                 op1=ALU.subtract).then_inc(max_split, 1)
                else:
                    dve.tensor_copy(max_turned[a][:], src[0:2 * TILES, 0:P]).then_inc(aux_taken, 1)

            def split_attention(m, c):
                cols = slice(c * HALF, (c + 1) * HALF)
                dve.wait_ge(aT_hi_done, CHUNKS * m + (c + 1))
                dve.tensor_tensor(aT_lo[:, cols], bank[c], aT_hi[:, cols], ALU.subtract).then_inc(out_taken, 1)

            def add_projected(m, b, c):
                total = oacc[:, b, c * HALF:(c + 1) * HALF]
                dve.wait_ge(out_ready, 4 * m + (c + 3))
                dve.tensor_tensor(total, bank[c], total, ALU.add).then_inc(out_taken, 1)

            def low(g, s):
                dve.wait_ge(probs_done, g * STEPS + (s + 1))
                p = probs[s % 4][:].rearrange("p a n -> p (a n)")
                dve.tensor_tensor(probs_lo[s % 2][:].rearrange("p a n -> p (a n)"), p,
                                  p.bitcast(BF16).rearrange("p (n two) -> p n two", two=2)[:, :, 1],
                                  ALU.subtract).then_inc(lo_dve, 1)

            def lagged(g, s, finishes):
                if (s >= 1 or finishes) and s <= STEPS and (s - 1) % STEPS in DVE_STEPS:
                    if s >= 3 or finishes:
                        dve.wait_ge(pv_done, g * STEPS + (s - 2))
                    low(g, s - 1)
                if s % 4 == 3 and (s >= 7 or finishes):
                    half = (s - 4) // 4
                    dve.wait_ge(o_copied, g * 4 + (half + 1))
                    sums = o_sb[half % 2][:].rearrange("p a q n -> p (a q) n")[:, :, DH]
                    dve.reciprocal(o_rden[half % 2][:], sums).then_inc(o_recip, 1)

            def attend(g, b, pair, feeds, finishes, more=True):
                for s in range(STEPS):
                    jobs = jobs_in(s, feeds, finishes)
                    for k in range(max(len(jobs), 1)):
                        if k < len(jobs):
                            which = jobs[k]
                            if which in ATTN:
                                split_attention(g - 1, which[2])
                            elif which in OUT:
                                add_projected(g - 1, (b - 1) % B, which[2])
                            else:
                                feed_job(g + 1, 1 - b % 2, which, False)
                        if k == 0:
                            lagged(g, s, finishes)
                    if b == B - 2 and s == WEIGHTS_STEP and more:
                        split_weights(pair + 1)
                    if b == 0 and s == WOUT_STEP:
                        split_output(pair)

            split_weights(0)
            dve.wait_ge(consts_in, 16 * len(first_consts))
            for b in range(B + 1):
                if b < B:
                    norm_twice(b)
                if b:
                    for i in range(2):
                        dve.wait_ge(c_hi_done, 2 * (b - 1) + (i + 1))
                        c = c_both[i][b - 1][DH:P, :]
                        dve.tensor_tensor(c, slot[i][DH:P, :], c, ALU.subtract).then_inc(c_lo_done, 1)
            for which in FEED:
                feed_job(0, 0, which, True)
            attend(0, 0, 0, True, False)
            with dve.Fori(0, PAIRS - 1) as pair:
                for b in range(1, B):
                    attend(pair * B + b, b, pair, True, True)
                attend(pair * B + B, 0, pair + 1, True, True)
            for b in range(1, B):
                attend(LAST - (B - 1 - b), b, PAIRS - 1, b < B - 1, True, False)
            for s in (STEPS, STEPS + 3):
                lagged(LAST, s, True)
            for c in range(CHUNKS):
                split_attention(LAST, c)
            for c in range(CHUNKS):
                add_projected(LAST, B - 1, c)

            dve.wait_ge(econsts_in, 16 * len(expert_consts))
            dve.tensor_copy(rows_r[:], rows_in[:]).then_inc(rows_done, 1)
            for n, (_, hi, lo) in enumerate(experts):
                dve.wait_ge(stage_hi, n + 1)
                dve.tensor_tensor(lo[:], stage[n][:], hi[:], ALU.subtract).then_inc(stage_lo, 1)
            with dve.Fori(0, B) as b:
                x1 = batch_of(x_all, b)
                dve.tensor_copy(o_now[:], oacc[:, bass.ds(b, 1), :].rearrange("p a n -> p (a n)")).then_inc(o_moved, 1)
                normalise(x1, n_sb, batch_of(moments_x, b), rstd_x[:, bass.ds(b * TILES, TILES)]).then_inc(y_done, 1)
                dve.wait_ge(y_done, b + 1)
                dve.wait_ge(o_turned, b + 1)
                dve.tensor_tensor(res_sb[:], aux[:].rearrange("p (t d) -> p t d", d=D), n_sb[:], ALU.add).then_inc(res_done, 1)
                dve.wait_ge(res_done, b + 1)
                layer_norm(b * NORMS + 1, res_sb, n_sb)
                dve.tensor_tensor(x1, x1, n_sb[:], ALU.add).then_inc(x1_done, 1)
                dve.wait_ge(x1_done, b + 1)
                layer_norm(b * NORMS + 2, x1, n_sb)
                dve.wait_ge(zT_done, b + 1)
                dve.tensor_tensor(zT_lo[:], aux[:], zT_hi[:], ALU.subtract).then_inc(z_lo_done, 1)

                def over(t):
                    return t.unsqueeze(2).to_broadcast([P, TILES, E])

                def step(ins, n):
                    ins.then_inc(route_dve, 1)
                    dve.wait_ge(route_dve, ROUTE * b + n)

                dve.wait_ge(logits_ready, b + 1)
                logits = outacc[:, 0, 0:TILES * E].rearrange("p (t e) -> p t e", e=E)
                step(dve.tensor_reduce(lmax[:], logits, AX, ALU.max), 1)
                step(dve.tensor_tensor(lg[:], logits, over(lmax[:]), ALU.subtract), 2)
                dve.wait_ge(route_act, 2 * b + 1)
                step(dve.tensor_reduce(lsum[:], lexp[:], AX, ALU.add), 3)
                step(dve.reciprocal(lrec[:], lsum[:]), 4)
                step(dve.tensor_tensor(pr[:], lexp[:], over(lrec[:]), ALU.mult), 5)
                standing()
                for t in range(TILES):
                    last = dve.max(top[:, t, :], pr[:, t, :])
                step(last, 6)
                step(dve.tensor_tensor(gap[:], top[:, :, 1], top[:, :, 0], ALU.subtract), 7)
                standing()
                for t in range(TILES):
                    last = dve.max_index(top_at[:, t, :], top[:, t, :], pr[:, t, :])
                step(last, 8)
                step(dve.tensor_copy(top_f[:], top_at[:]), 9)
                dve.wait_ge(route_act, 2 * b + 2)
                step(dve.tensor_scalar(eden[:], egap[:], 1.0, None, ALU.add), 10)
                step(dve.reciprocal(w_1[:], eden[:]), 11)
                step(dve.tensor_tensor(w_2[:], egap[:], w_1[:], ALU.mult), 12)
                dve.tensor_tensor(hot_1[:], ids_sb[:], over(top_f[:, :, 0]), ALU.is_equal)
                step(dve.tensor_tensor(hot_2[:], ids_sb[:], over(top_f[:, :, 1]), ALU.is_equal), 13)
                dve.tensor_tensor(hot_w1[:], hot_1[:], over(w_1[:]), ALU.mult)
                step(dve.tensor_tensor(hot_w2[:], hot_2[:], over(w_2[:]), ALU.mult), 14)
                step(dve.tensor_tensor(wfull[:], hot_w1[:], hot_w2[:], ALU.add), ROUTE)
                dve.wait_ge(wT_hi_done, b + 1)
                dve.tensor_tensor(wT_lo[:], outacc[0:E].rearrange("p a n -> p (a n)"), wT_hi[:], ALU.subtract).then_inc(wT_lo_done, 1)

                def low_hidden(u):
                    dve.wait_ge(f_hi_done, UNITS * b + (u + 1))
                    dve.tensor_tensor(flat(f_lo[u % 3]), flat(fuse[u % 2]), flat(f_hi[u % 3]), ALU.subtract).then_inc(f_lo_done, 1)

                def take_down(c):
                    dve.wait_ge(d_turned, CHUNKS * b + (c + 1))
                    tiles = TILES // CHUNKS
                    dve.tensor_copy(res_sb[:, c * tiles:(c + 1) * tiles, :].rearrange("p t d -> p (t d)"),
                                    down_ps).then_inc(d_taken, 1)

                for u in range(UNITS):
                    dve.wait_ge(up_ready, UNITS * b + (u + 1))
                    dve.wait_ge(actw_done, UNITS * b + (u + 1))
                    if u >= 2:
                        dve.wait_ge(f_lo_done, UNITS * b + (u - 1))
                    dve.tensor_tensor(flat(fuse[u % 2]), outacc[:].rearrange("p a n -> p (a n)"), flat(actw_sb[u % 2]),
                                      ALU.mult).then_inc(fuse_done, 1)
                    if u:
                        low_hidden(u - 1)
                    if u == E + 1:
                        take_down(0)
                low_hidden(UNITS - 1)
                take_down(1)
                dve.wait_ge(d_taken, CHUNKS * b + CHUNKS)
                layer_norm(b * NORMS + 3, res_sb, n_sb)
                dve.tensor_tensor(x1, x1, n_sb[:], ALU.add).then_inc(result_done, 1)
                dve.wait_ge(result_done, b + 1)

        @block.gpsimd
        def _(pool):
            def rope_add(n, at):
                a, t = at // 2, at % 2
                pool.wait_ge(aux_taken, n * NFEED + (FEED_AT[("proj", a, t, 1)] + 1))
                part = rot[a][:, t * HALF:(t + 1) * HALF]
                pool.tensor_tensor(part, part, t_sin[at % 2][:], ALU.add).then_inc(rope_sum, 1)

            def low_rotated(n, a):
                pool.wait_ge(qk_hi_done, 2 * n + (a + 1))
                pool.tensor_tensor(rot[a][:], rot[a][:], qk_hi[a][:].bitcast(F32), ALU.subtract).then_inc(qk_lo_done, 1)

            def low(g, s):
                pool.wait_ge(probs_done, g * STEPS + (s + 1))
                pool.wait_ge(pv_done, g * STEPS + (s - 1))
                p = probs[s % 4][:].rearrange("p a n -> p (a n)")
                pool.tensor_tensor(probs_lo[s % 2][:].rearrange("p a n -> p (a n)"), p,
                                   p.bitcast(BF16).rearrange("p (n two) -> p n two", two=2)[:, :, 1],
                                   ALU.subtract).then_inc(lo_pool, 1)

            def add_parts(g, s):
                half = (s - 4) // 4
                pool.wait_ge(o_copied, g * 4 + (half + 1))
                sums = o_sb[half % 2][:].rearrange("p a q n -> p (a q) n")
                pool.tensor_tensor(o_sum[half % 2][:], sums[:, :, 0:DH], sums[:, :, VLO:VW], ALU.add).then_inc(o_added, 1)

            def attend(g, feeds, finishes):
                for s in range(STEPS):
                    if s % 4 == 3 and (s >= 7 or finishes):
                        add_parts(g, s)
                    if s - 1 in POOL_STEPS:
                        low(g, s - 1)
                    if feeds and s in (0, 1):
                        rope_add(g + 1, 2 * s)
                        rope_add(g + 1, 2 * s + 1)
                    if feeds and s in (2, 3):
                        low_rotated(g + 1, s - 2)

            for at in range(4):
                rope_add(0, at)
            low_rotated(0, 0)
            low_rotated(0, 1)
            attend(0, True, False)
            with pool.Fori(0, PAIRS - 1) as pair:
                for b in range(1, B + 1):
                    attend(pair * B + b, True, True)
            for b in range(1, B):
                attend(LAST - (B - 1 - b), b < B - 1, True)
            add_parts(LAST, STEPS + 3)

            with pool.Fori(0, B) as b:
                for u in range(UNITS):
                    pool.wait_ge(act_done, UNITS * b + (u + 1))
                    pool.wait_ge(wrow_done, UNITS * b + (u + 1))
                    if u >= 2:
                        pool.wait_ge(fuse_done, UNITS * b + (u - 1))
                    pool.tensor_tensor(actw_sb[u % 2][:], act_sb[u % 2][:],
                                       wrow_sb[u % 2][:].unsqueeze(1).to_broadcast([P, FT, HALF]),
                                       ALU.mult).then_inc(actw_done, 1)


def rope_tables():
    inv_freq = 1.0 / ROPE_BASE ** (np.arange(0, DH, 2, dtype=np.float32) / DH)
    angles = np.outer(np.arange(S, dtype=np.float32), inv_freq)
    cos = np.concatenate([np.cos(angles), np.cos(angles)], -1)[:, ::2]
    sin = np.concatenate([np.sin(angles), np.sin(angles)], -1)[:, ::2]
    cos = np.repeat(cos, 2, axis=1)
    sin = np.stack([-sin, sin], axis=-1).reshape(S, DH)
    return (np.ascontiguousarray(np.tile(cos, (1, 2)).T.astype(np.float32)),
            np.ascontiguousarray(np.tile(sin, (1, 2)).T.astype(np.float32)))


def kernel(**inputs):
    import concourse.bacc as _bacc
    from concourse import mybir as _mybir
    from concourse.bass_utils import run_bass_kernel_spmd as _run

    a = {k: np.asarray(v) for k, v in inputs.items()}

    def rows_twice(w):
        return np.concatenate([w.T, w.T], axis=0)

    def swapped(w):
        return w.reshape(H * DH // 2, 2, DH)[:, ::-1].reshape(H * DH, DH)

    wq, wk, wv = a["L0_attn_w_up_q"], a["L0_attn_w_up_k"], a["L0_attn_w_up_v"]
    blocks = [rows_twice(w).reshape(P, PAIRS, P) for w in (wq, swapped(wq), wk, swapped(wk), wv)]
    cos, sin = rope_tables()
    arrays = {
        "x": a["L0_attn_x"],
        "w_pairs": np.stack([np.stack([blk[:, n] for blk in blocks], axis=1) for n in range(PAIRS)]),
        "w_out": a["L0_attn_w_out"].T.reshape(PAIRS, P, D),
        "w_down": np.concatenate([a["L0_attn_w_down_q"].T] * 2 + [a["L0_attn_w_down_kv"].T] * 2, axis=1),
        "ln_scale": a["L0_attn_ln_scale"].reshape(D, 1),
        "ln_bias": a["L0_attn_ln_bias"].reshape(D, 1),
        "router": a["L0_ffn_router_kernel_DE"],
        "w_gate": a["L0_ffn_kernel_gating_EDF"].transpose(1, 0, 2).reshape(D, E * F),
        "w_up": a["L0_ffn_kernel_up_EDF"].transpose(1, 0, 2).reshape(D, E * F),
        "w_dn": a["L0_ffn_kernel_down_EFD"].reshape(E, FT, P, D).transpose(2, 0, 1, 3).reshape(P, E * FT * D),
        "rope_cos": cos,
        "rope_sin": sin,
        "identity": np.eye(P, dtype=np.float32),
        "expert_rows": np.repeat(np.eye(E, dtype=np.float32), P, axis=1),
        "expert_ids": np.broadcast_to(np.arange(E, dtype=np.float32), (P, TILES, E)),
    }
    nc = _bacc.Bacc("TRN2", target_bir_lowering=False, num_devices=1)
    fed, args = {}, {}
    for name, value in arrays.items():
        fed[f"{name}_dram"] = np.ascontiguousarray(value)
        args[name] = nc.dram_tensor(f"{name}_dram", value.shape, _mybir.dt.from_np(value.dtype), kind="ExternalInput").ap()
    out = nc.dram_tensor("out_dram", (B, S, D), _mybir.dt.float32, kind="ExternalOutput").ap()
    program(nc, out=out, **args)
    r = _run(nc, [fed], core_ids=[0])
    return r.results[0]["out_dram"]
```

```python
from contextlib import ExitStack
from itertools import count

import numpy as np
import concourse.bass as bass
from concourse import mybir

F32 = mybir.dt.float32
F32R = mybir.dt.float32r
F16 = mybir.dt.float16
BF16 = mybir.dt.bfloat16
U32 = mybir.dt.uint32
ALU = mybir.AluOpType
ACT = mybir.ActivationFunctionType
AX = mybir.AxisListType.X

P = 128
B, S, D = 4, 1024, 128
H, DH = 16, 64
E, F = 8, 256
LN_EPS = 1e-5
ROPE_BASE = 10000.0
SCALE = 1.0 / 8.0

TILES = S // P
HALF = 512
CHUNKS = S // HALF
PAIRS = H // 2
STEPS = 16
FT = F // P
VW = 130
VLO = VW - DH
WBLOCKS = 5
LAST = PAIRS * B - 1
EXPERT_UNITS = CHUNKS * E
TURNS = EXPERT_UNITS * FT
ROUTE_TURNS = (22, 24, 25, 26, 27, 28, 29, 29)
SPLIT_LAG = 2
DOWN_LAG = 4
HALF_TILES = HALF // P
ROUTE = 17

FEED = ([("proj", a, c, swap) for a in range(2) for c in range(CHUNKS) for swap in range(2)]
        + [("value", 0, c, 0) for c in range(CHUNKS)]
        + [("max", 0, t, c) for t in range(TILES) for c in range(CHUNKS)]
        + [("max", 1, t, c) for t in range(2) for c in range(CHUNKS)] + [("turn", 0, 0, 0)]
        + [("max", 1, t, c) for t in range(2, TILES) for c in range(CHUNKS)] + [("turn", 1, 0, 0)])
NFEED = len(FEED)
OWN = FEED[-1:]
LAST_MAX = [("max", a, TILES - 1, CHUNKS - 1) for a in range(2)]
FEED_AT = {job: n for n, job in enumerate(FEED)}
ATTN = [("attn", 0, c, 0) for c in range(CHUNKS)]
OUT = [("out", 0, c, 0) for c in range(CHUNKS)]
FEED_IN = {0: FEED[0:3], 1: FEED[3:6], 2: FEED[6:8], 3: FEED[8:10], 4: FEED[10:11], 5: FEED[11:15], 6: FEED[15:16],
           7: FEED[16:20], 8: FEED[20:22], 9: FEED[22:26], 10: FEED[26:29], 11: FEED[29:31], 12: FEED[31:35],
           13: FEED[35:39], 14: FEED[39:43]}
JOB_PLACES = {0: (), 1: (3,), 2: (0, 1), 3: (0, 1, 3), 4: (0, 1, 2, 3)}
FINISH_IN = {6: ATTN, 8: OUT}
SCORE_BANKS, JOB_BANKS = 3, 3
KEY_TILES = 2 * STEPS
ROTATED_STEPS = (2, 3)
ROTATED_LOW_STEPS = (2, 6)
WEIGHTS_STEP, WOUT_STEP = 4, 12
POOL_STEPS = (4, 6, 7, 8, 9, 11, 12, 13, 14)
DVE_STEPS = tuple(s for s in range(STEPS) if s not in POOL_STEPS)
OUTPUT_NORM, INPUT_NORM, INPUT_TURN = 5, 9, 11
FILLS = 7
LAG = 2


def jobs_in(step, feeds, finishes):
    return ((OWN if step == 0 else []) + (FINISH_IN.get(step, []) if finishes else [])
            + (FEED_IN.get(step, []) if feeds else []))


IN_ORDER = [job for step in range(STEPS) for job in jobs_in(step, True, True)]
BANK_OF = {job: n % JOB_BANKS for n, job in enumerate(IN_ORDER)}


def low_parts_done(step):
    own = POOL_STEPS if step % STEPS in POOL_STEPS else DVE_STEPS
    return own is POOL_STEPS, len(own) * (step // STEPS) + own.index(step % STEPS) + 1


def program(nc, x, w_pairs, w_out, w_down, ln_scale, ln_bias, router, w_gate, w_up, w_dn,
            rope_cos, rope_sin, identity, expert_rows, expert_ids, out):
    with ExitStack() as ctx:
        def sb(name, shape, dt=F32, where=ctx):
            return where.enter_context(nc.sbuf_tensor(name, shape, dt))

        def sem(name):
            return ctx.enter_context(nc.semaphore(name))

        psum = ctx.enter_context(nc.psum_tensor("psum", [P, 8, HALF], F32))
        score_ps = [psum[:, i] for i in range(SCORE_BANKS)]
        bank = [psum[:, SCORE_BANKS + i] for i in range(JOB_BANKS)]
        outacc = psum[:, 6:8]
        latent_ps = psum[:, 0:2]
        turn_ps = psum[:, 6:8]
        gate_ps = [psum[:, i] for i in range(2)]
        up_ps = [psum[:, 2 + i] for i in range(2)]
        wrow_ps = psum[:, 4]
        down_ps = psum[:, 5]
        side_ps = [psum[:, 6 + i] for i in range(2)]
        first_ps = [b for k, b in enumerate(bank) if k != BANK_OF[OWN[0]]]
        last_ps = [score_ps[0], score_ps[1], outacc[:, 0], outacc[:, 1]]

        def flat(t):
            return t.rearrange("p a n -> p (a n)")

        ident = sb("ident", [P, P])
        eps = sb("eps", [P, 1])
        warm = sb("warm", [P, 1])
        spare = sb("spare", [P, 16])
        raw_two = sb("raw_two", [P, 2 * E * F])
        x_front = raw_two[:].rearrange("p (t d) -> p t d", d=D)
        oacc = sb("oacc", [D, B, S])
        moments_x = sb("moments_x", [P, B * TILES, 2])
        rstd_x = sb("rstd_x", [P, B * TILES])
        stats = sb("stats", [P, B * TILES, 6])
        sdev = sb("sdev", [P, B * TILES])

        with ExitStack() as phase:
            def sb1(name, shape, dt=F32):
                return sb(name, shape, dt, phase)

            cos_sb = sb1("cos_sb", [P, S])
            sin_sb = sb1("sin_sb", [P, S])
            c_both = [[sb1(f"c_both{i}{b}", [P, S], F32R) for b in range(B)] for i in range(2)]
            w_raw = sb1("w_raw", [P, WBLOCKS, P])
            w_hi = sb1("w_hi", [P, WBLOCKS, P], F32R)
            w_lo = sb1("w_lo", [P, WBLOCKS, P], F32R)
            t_sin = [sb1(f"t_sin{i}", [P, HALF]) for i in range(2)]
            rot = [sb1(f"rot{i}", [P, S]) for i in range(2)]
            qk_hi = [sb1(f"qk_hi{i}", [P, S], F32R) for i in range(2)]
            q_both, k_twice = [[], []], [[], []]
            for i in range(2):
                for h in range(2):
                    q_both[i].append(sb1(f"q_both{i}{h}", [P, S], F32R))
                    k_twice[i].append(sb1(f"k_twice{i}{h}", [P, S], F32R))
                if i == 0:
                    vsl = [sb1("vsl0", [P, TILES, 2, VW], F16)]
            scale_sb = sb1("scale_sb", [P, 1])
            bias_sb = sb1("bias_sb", [P, 1])
            wd_sb = sb1("wd_sb", [D, P])
            q_max = [sb1(f"q_max{h}", [DH + 2, S], F32R) for h in range(2)]
            k_ones = [sb1(f"k_ones{h}", [DH + 2, S], F32R) for h in range(2)]
            row_max = [sb1(f"row_max{h}", [P, CHUNKS, TILES]) for h in range(2)]
            max_all = [sb1(f"max_all{h}", [P, TILES]) for h in range(2)]
            max_parts = [sb1(f"max_parts{h}", [P, 2 * TILES], F32R) for h in range(2)]
            max_turned = [sb1(f"max_turned{h}", [2 * TILES, P], F32R) for h in range(2)]
            probs = [sb1(f"probs{i}", [P, 2, HALF]) for i in range(4)]
            probs_lo = [sb1(f"probs_lo{i}", [P, 2, HALF], F16) for i in range(4)]
            o_sb = [sb1(f"o_sb{i}", [P, 2, 2, VW]) for i in range(2)]
            o_sum = [sb1(f"o_sum{i}", [P, 4, DH]) for i in range(2)]
            o_rden = [sb1(f"o_rden{i}", [P, 4]) for i in range(2)]
            attn = sb1("attn", [P, TILES, P])
            o_part = [sb1(f"o_part{c}", [D, HALF]) for c in range(CHUNKS)]
            aT_hi = sb1("aT_hi", [P, S], F32R)
            aT_lo = sb1("aT_lo", [P, S], F32R)
            vsl.append(sb1("vsl1", [P, TILES, 2, VW], F16))
            wo_raw = sb1("wo_raw", [P, D])
            wo_hi = sb1("wo_hi", [P, D], F32R)
            wo_lo = sb1("wo_lo", [P, D], F32R)
            n_front = [probs[0][:].rearrange("p a (t d) -> p (a t) d", d=D), attn[:]]
            hT = probs[1][:].rearrange("p a n -> p (a n)")
            c_hi = probs[2][:].rearrange("p a n -> p (a n)").bitcast(F32R)
            c_lo = probs[3][:].rearrange("p a n -> p (a n)").bitcast(F32R)
            var_y = sb1("var_y", [P, B * TILES])
            rstd_y = sb1("rstd_y", [P, B * TILES])
            sdev_y = sb1("sdev_y", [P, B * TILES])
            shift_y = sb1("shift_y", [P, B * TILES])

        stage = [raw_two[:, k % 2 * E * F:(k % 2 + 1) * E * F] for k in range(3)]
        router_sb = sb("router_sb", [D, E])
        ids_sb = sb("ids_sb", [P, TILES, E])
        lg = sb("lg", [P, TILES, E])
        lmax = sb("lmax", [P, TILES])
        lexp = sb("lexp", [P, TILES, E])
        lsum = sb("lsum", [P, TILES])
        lrec = sb("lrec", [P, TILES])
        pr = sb("pr", [P, TILES, E])
        top = sb("top", [P, TILES, 8])
        top_at = sb("top_at", [P, TILES, 8], U32)
        top_f = sb("top_f", [P, TILES, 8])
        gap = sb("gap", [P, TILES])
        egap = sb("egap", [P, TILES])
        eden = sb("eden", [P, TILES])
        w_1 = sb("w_1", [P, TILES])
        w_2 = sb("w_2", [P, TILES])
        hot_1 = sb("hot_1", [P, TILES, E])
        hot_2 = sb("hot_2", [P, TILES, E])
        hot_w1 = sb("hot_w1", [P, TILES, E])
        hot_w2 = sb("hot_w2", [P, TILES, E])
        wfull = sb("wfull", [P, TILES, E])
        w_high = sb("w_high", [P, TILES, E], F32R)
        w_both = sb("w_both", [P, TILES, 2 * E])
        ln_st = [sb(f"ln_st{k}", [P, TILES, 6]) for k in range(3)]
        ln_mv = [sb(f"ln_mv{k}", [P, TILES, 2]) for k in range(3)]
        ln_dev = [sb(f"ln_dev{k}", [P, TILES]) for k in range(3)]
        ln_inv = [sb(f"ln_inv{k}", [P, TILES]) for k in range(3)]
        out_shift = sb("out_shift", [P, TILES])
        o_now = sb("o_now", [D, S])
        y_sb = sb("y_sb", [P, TILES, D])
        res_sb = sb("res_sb", [P, TILES, D])
        n1_sb = sb("n1_sb", [P, TILES, D])
        z_sb = sb("z_sb", [P, TILES, D])
        zT = sb("zT", [D, S])
        zT_hi = sb("zT_hi", [D, S], F32R)
        zT_lo = sb("zT_lo", [D, S], F32R)
        wg_hi = sb("wg_hi", [D, E * F], F32R)
        wg_lo = sb("wg_lo", [D, E * F], F32R)
        wu_hi = sb("wu_hi", [D, E * F], F32R)
        wu_lo = sb("wu_lo", [D, E * F], F32R)
        x_all = sb("x_all", [P, B * TILES, D])
        wn_hi = sb("wn_hi", [P, E * FT * D], F32R)
        wn_lo = sb("wn_lo", [P, E * FT * D], F32R)
        rows_in = sb("rows_in", [2 * E, E * P])
        rows_r = sb("rows_r", [2 * E, E * P], F32R)
        moe_sb = sb("moe_sb", [P, TILES, D])
        nf_sb = sb("nf_sb", [P, TILES, D])
        wT = sb("wT", [2 * E, S], F32R)
        act_sb = [sb(f"act_sb{i}", [P, HALF]) for i in range(2)]
        wrow_sb = [sb(f"wrow_sb{i}", [P, HALF]) for i in range(2)]
        actw_sb = [sb(f"actw_sb{i}", [P, HALF]) for i in range(2)]
        fuse = [sb(f"fuse{i}", [P, HALF]) for i in range(4)]
        f_hi = [sb(f"f_hi{i}", [P, HALF], F32R) for i in range(4)]
        f_lo = [sb(f"f_lo{i}", [P, HALF], F32R) for i in range(4)]
        dT = sb("dT", [D, HALF])

        consts_in, tables_in, eps_set, fills_done = sem("consts_in"), sem("tables_in"), sem("eps_set"), sem("fills_done")
        x_in = [sem(f"x_in{b}") for b in range(B)]
        x_first, x_rest = sem("x_first"), sem("x_rest")
        ln_stats, ln_moments, ln_sdev, ln_rstd = sem("ln_stats"), sem("ln_moments"), sem("ln_sdev"), sem("ln_rstd")
        ln_steps, y_sdev, ln_y_inverse = sem("ln_steps"), sem("y_sdev"), sem("ln_y_inverse")
        n_turned, h_done = sem("n_turned"), sem("h_done")
        c_ready, c_hi_done, c_lo_done, c_in = sem("c_ready"), sem("c_hi_done"), sem("c_lo_done"), sem("c_in")
        shift_done, n_ready = sem("shift_done"), [sem(f"n_ready{b}") for b in range(B)]
        raw_in, w_hi_done, w_done, v_hi_done = sem("raw_in"), sem("w_hi_done"), sem("w_done"), sem("v_hi_done")
        wo_in, wo_hi_done, wo_done = sem("wo_in"), sem("wo_hi_done"), sem("wo_done")
        aux_ready, aux_taken = sem("aux_ready"), sem("aux_taken")
        out_ready, attn_taken, aT_hi_done = sem("out_ready"), sem("attn_taken"), sem("aT_hi_done")
        out_copied, out_added = sem("out_copied"), sem("out_added")
        rope_sum, qk_hi_done, qk_lo_done = sem("rope_sum"), sem("qk_hi_done"), sem("qk_lo_done")
        both_in = [sem("both_in0"), sem("both_in1")]
        score_in = [sem("score_in0"), sem("score_in1")]
        max_whole = sem("max_whole")
        max_hi, max_split = sem("max_hi"), sem("max_split")
        rows_put = [sem("rows_put0"), sem("rows_put1")]
        scores_ready, probs_done = sem("scores_ready"), sem("probs_done")
        lo_dve, lo_pool = sem("lo_dve"), sem("lo_pool")
        pv_done, o_copied, o_recip, o_added, o_done = (
            sem("pv_done"), sem("o_copied"), sem("o_recip"), sem("o_added"), sem("o_done"))
        o_moved, o_turned, y_done, res_done, x1_done = (
            sem("o_moved"), sem("o_turned"), sem("y_done"), sem("res_done"), sem("x1_done"))
        econsts_in, rows_loaded, rows_done = sem("econsts_in"), sem("rows_loaded"), sem("rows_done")
        stage_in = [sem(f"stage_in{i}") for i in range(3)]
        stage_hi, stage_lo, down_lo = sem("stage_hi"), sem("stage_lo"), sem("down_lo")
        st_done, mv_done, dev_done, inv_done = (
            [sem(f"{name}{k}") for k in range(3)] for name in ("st_done", "mv_done", "dev_done", "inv_done"))
        n1_done, z_done, nf_done = sem("n1_done"), sem("z_done"), sem("nf_done")
        z_turned, z_copied, z_hi_done, z_lo_done = sem("z_turned"), sem("z_copied"), sem("z_hi_done"), sem("z_lo_done")
        logits_ready, route_dve, route_act = sem("logits_ready"), sem("route_dve"), sem("route_act")
        w_turned, wT_done = sem("w_turned"), sem("wT_done")
        gate_ready, wrow_ready, up_ready, down_done = (
            sem("gate_ready"), sem("wrow_ready"), sem("up_ready"), sem("down_done"))
        act_done, wrow_done, actw_done = sem("act_done"), sem("wrow_done"), sem("actw_done")
        fuse_done, f_hi_done, f_lo_done = sem("fuse_done"), sem("f_hi_done"), sem("f_lo_done")
        dT_done, d_turned, d_taken, result_done, stored = (
            sem("dT_done"), sem("d_turned"), sem("d_taken"), sem("result_done"), sem("stored"))

        experts = [(w_gate, wg_hi, wg_lo), (w_up, wu_hi, wu_lo), (w_dn, wn_hi, wn_lo)]
        first_consts = ((ident, identity), (scale_sb, ln_scale), (bias_sb, ln_bias), (wd_sb, w_down))
        tables = ((cos_sb, rope_cos), (sin_sb, rope_sin))
        FRONT_TILES = [slice(0, TILES), slice(TILES, B * TILES)]
        TURN_AFTER = {3: 1, 9: 2, 20: 3}
        LATENTS_AFTER = {7: 1, 12: 2, 24: 3}
        SPLIT_AFTER = {7: 1, 14: 2, 27: 3}
        expert_consts = ((router_sb, router), (ids_sb, expert_ids))

        block = ctx.enter_context(nc.Block())

        def sides(n):
            return first_ps if isinstance(n, int) and n == 0 else side_ps

        def batch_of(t, b):
            return t[:, bass.ds(b * TILES, TILES), :]

        def in_dram(t, b):
            return t[bass.ds(b, 1)].rearrange("b (t p) d -> p (b t) d", p=P)

        @block.sync
        def _(sp):
            sp.dma_start(batch_of(x_front, 0), in_dram(x, 0)).then_inc(x_in[0], 16)
            for dst, src in first_consts:
                sp.dma_start(dst[:], src).then_inc(consts_in, 16)

            def load_weights(pair):
                sp.dma_start(w_raw[:], w_pairs[bass.ds(pair, 1)].rearrange("a p c n -> p (a c) n")).then_inc(raw_in, 16)
                sp.dma_start(wo_raw[:], w_out[bass.ds(pair, 1)].rearrange("a p n -> (a p) n")).then_inc(wo_in, 16)

            load_weights(0)
            for dst, src in tables:
                sp.dma_start(dst[:], src).then_inc(tables_in, 16)
            for b in range(1, B):
                sp.dma_start(batch_of(x_front, b), in_dram(x, b)).then_inc(x_in[b], 16)
            for b in range(B):
                for part, (src, done) in enumerate(((c_hi, c_hi_done), (c_lo, c_lo_done))):
                    sp.wait_ge(done, b + 1)
                    for i in range(2):
                        sp.dma_start(c_both[i][b][part * DH:(part + 1) * DH, :].bitcast(F32),
                                     src[i * DH:(i + 1) * DH, :].bitcast(F32)).then_inc(c_in, 16)

            def put(dst, src, h, signal):
                sp.dma_start(dst.bitcast(F32), src[h * DH:(h + 1) * DH, :].bitcast(F32)).then_inc(signal, 16)

            def feed(n, par, first):
                sp.wait_ge(qk_hi_done, 2 * n + 2)
                for h in range(2):
                    put(q_both[par][h][0:DH, :], qk_hi[0], h, both_in[h])
                    put(k_twice[par][h][0:DH, :], qk_hi[1], h, both_in[h])
                    put(k_twice[par][h][DH:P, :], qk_hi[1], h, both_in[h])
                    if h == 0:
                        sp.wait_ge(qk_lo_done, 2 * n + 1)
                    put(q_both[par][h][DH:P, :], rot[0], h, both_in[h])
                sp.wait_ge(qk_lo_done, 2 * n + 2)
                for h in range(2):
                    if not first:
                        sp.wait_ge(scores_ready, n * KEY_TILES - (KEY_TILES // 2) * (1 - h))
                    put(q_max[h][0:DH, :], qk_hi[0], h, score_in[h])
                    put(k_ones[h][0:DH, :], rot[1], h, score_in[h])
                    sp.wait_ge(aux_taken, n * NFEED + (FEED_AT[("turn", h, 0, 0)] + 1))
                    for part in range(2):
                        sp.dma_start(q_max[h][DH + part:DH + part + 1, :].bitcast(F32),
                                     max_turned[h][part * TILES:(part + 1) * TILES, :].bitcast(F32)).then_inc(rows_put[h], 16)

            feed(0, 0, True)
            feed(1, 1, False)
            for b in range(B):
                sp.wait_ge(n_ready[b], 1)
            for n in range(2):
                sp.dma_start(stage[n], experts[n][0]).then_inc(stage_in[n], 16)
            with sp.Fori(0, PAIRS - 1) as pair:
                sp.wait_ge(w_done, pair + 1)
                sp.wait_ge(wo_done, pair + 1)
                load_weights(pair + 1)
                for k in range(2, B + 2):
                    feed(pair * B + k, k % 2, False)
            for n in range(PAIRS * B - B + 2, PAIRS * B):
                feed(n, n % 2, False)
            sp.wait_ge(pv_done, STEPS * LAST)
            sp.dma_start(batch_of(x_all, 0), in_dram(x, 0)).then_inc(x_first, 16)
            for dst, src in expert_consts:
                sp.dma_start(dst[:], src).then_inc(econsts_in, 16)
            sp.wait_ge(stage_lo, 1)
            sp.dma_start(stage[2], experts[2][0]).then_inc(stage_in[2], 16)
            sp.wait_ge(scores_ready, KEY_TILES * LAST + KEY_TILES // 2 + 1)
            for b in range(1, B):
                sp.dma_start(batch_of(x_all, b), in_dram(x, b)).then_inc(x_rest, 16)
            sp.wait_ge(scores_ready, KEY_TILES * PAIRS * B)
            sp.dma_start(rows_in[:], expert_rows).then_inc(rows_loaded, 16)
            with sp.Fori(0, B) as b:
                sp.wait_ge(result_done, b + 1)
                sp.dma_start(in_dram(out, b), batch_of(x_all, b)).then_inc(stored, 16)
            sp.wait_ge(stored, 16 * B)

        @block.tensor
        def _(pe):
            def free(n, m, before):
                if before in ATTN:
                    pe.wait_ge(attn_taken, 2 * m + (ATTN.index(before) + 1))
                elif before in OUT:
                    pe.wait_ge(out_copied, 2 * m + (OUT.index(before) + 1))
                elif before is not None:
                    pe.wait_ge(aux_taken, n * NFEED + (FEED_AT[before] + 1))

            def feed_job(n, b, bank, which):
                kind, a, t, c = which
                if kind == "proj":
                    for w in (w_hi, w_lo):
                        mm = pe.matmul(bank, w[:, 2 * a + c, :], c_both[a][b][:, t * HALF:(t + 1) * HALF],
                                       start=w is w_hi, stop=w is w_lo)
                elif kind == "value":
                    for i in range(HALF // P):
                        for w in (w_hi, w_lo):
                            k0 = t * HALF + i * P
                            mm = pe.matmul(bank[:, i * P:(i + 1) * P], c_both[1][b][:, k0:k0 + P], w[:, 4, :],
                                           start=w is w_hi, stop=w is w_lo)
                elif kind == "max":
                    if which == ("max", 0, 0, 0):
                        pe.wait_ge(qk_hi_done, 2 * n + 2)
                    rows = slice(a * DH, (a + 1) * DH)
                    mm = pe.matmul(bank, qk_hi[0][rows, t * P:(t + 1) * P], qk_hi[1][rows, c * HALF:(c + 1) * HALF],
                                   start=True, stop=True)
                else:
                    pe.wait_ge(max_split, 2 * n + (a + 1))
                    mm = pe.transpose(bank[0:2 * TILES, 0:P], max_parts[a][:].bitcast(F32), ident[:])
                mm.then_inc(aux_ready, 1)

            def turn_attention(m, bank, c):
                pe.wait_ge(o_done, m * 4 + (3 + c))
                for t in range(HALF // P):
                    mm = pe.transpose(bank[:, t * P:(t + 1) * P], attn[:, c * (HALF // P) + t, :], ident[:])
                mm.then_inc(out_ready, 1)

            def project_out(m, bank, c):
                pe.wait_ge(attn_taken, 2 * m + (c + 1))
                for k, (w, a) in enumerate(((wo_hi, aT_hi), (wo_lo, aT_hi), (wo_hi, aT_lo))):
                    mm = pe.matmul(bank, w[:], a[:, c * HALF:(c + 1) * HALF], start=k == 0, stop=k == 2)
                mm.then_inc(out_ready, 1)

            def score(g, par, s, i, first):
                h, qh, kp = s // 8, s % 8 // 4, s % 4
                tile = 2 * s + i
                at = tile % SCORE_BANKS
                if tile >= SCORE_BANKS:
                    pe.wait_ge(probs_done, g * KEY_TILES + (tile - SCORE_BANKS + 1))
                elif not first:
                    pe.wait_ge(probs_done, g * KEY_TILES - ((KEY_TILES - 1 - at) % SCORE_BANKS))
                if i == 0 and s % 8 == 0:
                    pe.wait_ge(both_in[h], 64 * g + 64)
                    pe.wait_ge(score_in[h], 32 * g + 32)
                    pe.wait_ge(rows_put[h], 32 * g + 32)
                k0 = (2 * kp + i) * P
                pe.matmul(score_ps[at], k_twice[par][h][:, k0:k0 + P],
                          q_both[par][h][:, qh * HALF:(qh + 1) * HALF], start=True, stop=False)
                mm = pe.matmul(score_ps[at], k_ones[h][:, k0:k0 + P],
                               q_max[h][:, qh * HALF:(qh + 1) * HALF], start=False, stop=True)
                mm.then_inc(scores_ready, 1)

            def values(g, par, s, i, first):
                t = s % STEPS
                h, kp = t // 8, t % 4
                pool, count = low_parts_done(s)
                if i == 0:
                    if s == 0:
                        pe.wait_ge(aux_taken, g * NFEED + (FEED_AT[("value", 0, 1, 0)] + 1))
                    if kp == 0 and not (first and s == 0):
                        pe.wait_ge(o_copied, g * 4 + s // 4)
                    pe.wait_ge(lo_pool if pool else lo_dve, g * len(POOL_STEPS if pool else DVE_STEPS) + count)
                high = probs[t % 4][:, i, :].bitcast(BF16).rearrange("p (n two) -> p n two", two=2)
                v = vsl[par][:, 2 * kp + i, h, :]
                for q in range(4):
                    acc = outacc[:, q // 2, q % 2 * VW:(q % 2 + 1) * VW]
                    opens = kp == 0 and i == 0 and q % 2 == 0
                    pe.matmul(acc, high[:, q * P:(q + 1) * P, 1], v, start=opens, stop=False, skip_group_check=True)
                    mm = pe.matmul(acc[:, 0:VLO], probs_lo[t % 4][:, i, q * P:(q + 1) * P], v[:, 0:VLO],
                                   start=False, stop=kp == 3 and i == 1, skip_group_check=True)
                if i == 1:
                    mm.then_inc(pv_done, 1)

            def attend(g, b, pair, feeds, finishes, beside=None):
                par = b % 2
                in_bank = {BANK_OF[job]: (g, job) for job in FEED[:-1]}
                for s in range(STEPS):
                    jobs = jobs_in(s, feeds, finishes)
                    places = JOB_PLACES[len(jobs)]
                    for k in range(4):
                        if k < 2:
                            score(g, par, s, k, not finishes)
                        elif s >= LAG or finishes:
                            values(g, par if s >= LAG else 1 - par, s - LAG, k - 2, not finishes)
                        if k in places:
                            which = jobs[places.index(k)]
                            at, n = BANK_OF[which], (g if which in OWN else g + 1)
                            free(in_bank[at][0], g - 1, in_bank[at][1])
                            if which in ATTN:
                                turn_attention(g - 1, bank[at], which[2])
                            elif which in OUT:
                                if which == OUT[0] and b == 1:
                                    pe.wait_ge(wo_done, pair + 1)
                                project_out(g - 1, bank[at], which[2])
                            else:
                                if which == FEED[0] and b == B - 1:
                                    pe.wait_ge(w_done, pair + 2)
                                feed_job(n, (b + 1) % B, bank[at], which)
                            in_bank[at] = (n, which)
                    if beside:
                        beside(s)

            def turn_tokens(side, src, at, signal, banks=side_ps):
                for t in range(HALF_TILES):
                    mm = pe.transpose(banks[side][:, t * P:(t + 1) * P], src(at * HALF_TILES + t), ident[:])
                mm.then_inc(signal, 1)

            def channels(t):
                return o_now[:, t * P:(t + 1) * P]

            def normed(t):
                return z_sb[:, t, :]

            def expert_sums(t):
                return dT[:, t % HALF_TILES * P:(t % HALF_TILES + 1) * P]

            def router_logits(n):
                pe.wait_ge(z_copied, CHUNKS * n + CHUNKS)
                for t in range(TILES):
                    mm = pe.matmul(sides(n)[0][:, t * E:(t + 1) * E], zT[:, t * P:(t + 1) * P], router_sb[:],
                                   start=True, stop=True)
                mm.then_inc(logits_ready, 1)

            def turn_routing(n):
                pe.wait_ge(route_dve, ROUTE * n + ROUTE)
                for c in range(CHUNKS):
                    for t in range(HALF_TILES):
                        mm = pe.transpose(sides(n)[1 - c][0:2 * E, t * P:(t + 1) * P],
                                          w_both[:, c * HALF_TILES + t, :], ident[:])
                    mm.then_inc(w_turned, 1)

            def hidden(dst, w_hi, w_lo, e, ft, c):
                f0 = e * F + ft * P
                for k, (w, z) in enumerate(((w_hi, zT_hi), (w_lo, zT_hi), (w_hi, zT_lo))):
                    mm = pe.matmul(dst, w[:, f0:f0 + P], z[:, c * HALF:(c + 1) * HALF], start=k == 0, stop=k == 2)
                return mm

            def down(b, v, first=False):
                c, e, ft = v % TURNS // (E * FT), v % (E * FT) // FT, v % FT
                if e == 0 and ft == 0 and not (first and c == 0):
                    pe.wait_ge(dT_done, CHUNKS * b + c)
                if first and v == 0:
                    pe.wait_ge(down_lo, 1)
                pe.wait_ge(f_lo_done, TURNS * b + (v + 1))
                w0 = (e * FT + ft) * D
                for k, (w, f) in enumerate(((wn_hi, f_hi), (wn_lo, f_hi), (wn_hi, f_lo))):
                    mm = pe.matmul(down_ps, w[:, w0:w0 + D], f[v % 4][:],
                                   start=e == 0 and ft == 0 and k == 0, stop=e == E - 1 and ft == FT - 1 and k == 2)
                mm.then_inc(down_done, 1)

            def spread_weights(b, u, first):
                c, e = u // E, u % E
                if e == 0:
                    pe.wait_ge(wT_done, CHUNKS if first and c == 0 else CHUNKS * b + (c + 1))
                if not first:
                    pe.wait_ge(wrow_done, EXPERT_UNITS * b + u)
                pe.matmul(wrow_ps, rows_r[:, e * P:(e + 1) * P], wT[:, c * HALF:(c + 1) * HALF],
                          start=True, stop=True).then_inc(wrow_ready, 1)

            def gate(b, v, first):
                c, e, ft = v // (E * FT), v % (E * FT) // FT, v % FT
                if v % (E * FT) == 0:
                    pe.wait_ge(z_lo_done, CHUNKS * b + (c + 1))
                if not first or v >= 2:
                    pe.wait_ge(act_done, TURNS * b + (v - 1))
                hidden(gate_ps[v % 2], wg_hi, wg_lo, e, ft, c).then_inc(gate_ready, 1)

            def expert_turns(b, first, front):
                n = b + 1
                for v in range(TURNS):
                    u, ft = v // FT, v % FT
                    c, e = v // (E * FT), v % (E * FT) // FT
                    if v == 0 and first:
                        gate(b, 0, first)
                    if v < TURNS - 1:
                        gate(b, v + 1, first)
                    elif front:
                        gate(n, 0, False)
                    if v == 0:
                        spread_weights(b, 0, first)
                    if ft == FT - 1 and v < TURNS - 1:
                        spread_weights(b, u + 1, False)
                    if not first or v >= 2:
                        pe.wait_ge(fuse_done, TURNS * b + (v - 1))
                    hidden(up_ps[v % 2], wu_hi, wu_lo, e, ft, c).then_inc(up_ready, 1)
                    if not first or v >= DOWN_LAG:
                        down(b, v - DOWN_LAG, first)
                    if v == 2 and front:
                        pe.wait_ge(o_moved, n + 1)
                        pe.wait_ge(wT_done, CHUNKS * b + 2)
                        turn_tokens(1, channels, 0, o_turned)
                        turn_tokens(0, channels, 1, o_turned)
                    if v == 6 and not first:
                        pe.wait_ge(res_done, CHUNKS * n + 2) if front else pe.wait_ge(wT_done, CHUNKS * b + 2)
                        pe.wait_ge(dT_done, CHUNKS * b)
                        turn_tokens(0, expert_sums, 1, d_turned)
                    if v == 19 and front:
                        if not first:
                            pe.wait_ge(d_taken, CHUNKS * b)
                        pe.wait_ge(z_done, CHUNKS * n + 1)
                        turn_tokens(0, normed, 0, z_turned)
                    if v == 20 and front:
                        pe.wait_ge(res_done, CHUNKS * n + 2)
                        pe.wait_ge(z_done, CHUNKS * n + 2)
                        turn_tokens(1, normed, 1, z_turned)
                    if v == 21 and front:
                        router_logits(n)
                    if v == 24:
                        pe.wait_ge(z_copied, CHUNKS * n + 2) if front else pe.wait_ge(wT_done, CHUNKS * b + 1)
                        pe.wait_ge(dT_done, CHUNKS * b + 1)
                        turn_tokens(1, expert_sums, 0, d_turned)
                    if v == 31 and front:
                        pe.wait_ge(d_taken, CHUNKS * b + 1)
                        turn_routing(n)

            def first_input(s):
                if s == 1:
                    pe.wait_ge(o_moved, 1)
                    turn_tokens(1, channels, 0, o_turned, first_ps)
                    turn_tokens(0, channels, 1, o_turned, first_ps)
                if s == 5:
                    pe.wait_ge(res_done, CHUNKS)
                if s == INPUT_TURN:
                    pe.wait_ge(out_copied, 2 * LAST)
                    pe.wait_ge(z_done, 1)
                    turn_tokens(0, normed, 0, z_turned, first_ps)
                    pe.wait_ge(z_done, 2)
                    turn_tokens(1, normed, 1, z_turned, first_ps)
                if s == INPUT_TURN + 2:
                    pe.wait_ge(econsts_in, 16 * len(expert_consts))
                    router_logits(0)

            def turn_batch(b):
                pe.wait_ge(n_ready[b], 1)
                if b:
                    pe.wait_ge(h_done, b)
                for t in range(TILES):
                    mm = pe.transpose(flat(turn_ps)[:, t * P:(t + 1) * P], n_front[1 - b % 2][:, t, :], ident[:])
                mm.then_inc(n_turned, 1)

            def latents(b):
                pe.wait_ge(h_done, b + 1)
                if b:
                    pe.wait_ge(c_lo_done, b)
                for c in range(CHUNKS):
                    mm = pe.matmul(latent_ps[:, c, :], wd_sb[:], hT[:, c * HALF:(c + 1) * HALF], start=True, stop=True)
                mm.then_inc(c_ready, 1)

            pe.wait_ge(consts_in, 16 * len(first_consts))
            turn_batch(0)
            latents(0)
            pe.wait_ge(w_done, 1)
            pe.wait_ge(c_in, 64)
            in_bank = {}
            for k, which in enumerate(FEED[:-1]):
                at = BANK_OF[which]
                free(0, None, in_bank.get(at))
                feed_job(0, 0, bank[at], which)
                in_bank[at] = which
                if k in TURN_AFTER:
                    turn_batch(TURN_AFTER[k])
                if k in LATENTS_AFTER:
                    latents(LATENTS_AFTER[k])
            pe.wait_ge(c_lo_done, B)
            pe.wait_ge(c_in, 64 * B)
            pe.wait_ge(fills_done, FILLS)
            attend(0, 0, 0, True, False)
            with pe.Fori(0, PAIRS - 1) as pair:
                for b in range(1, B):
                    attend(pair * B + b, b, pair, True, True)
                attend(pair * B + B, 0, pair + 1, True, True)
            for b in range(1, B - 1):
                attend(LAST - (B - 1 - b), b, PAIRS - 1, True, True)
            attend(LAST, B - 1, PAIRS - 1, False, True, first_input)
            for s in range(STEPS, STEPS + LAG):
                for i in range(2):
                    values(LAST, (B - 1) % 2, s - LAG, i, False)
            turn_routing(0)
            for c in range(CHUNKS):
                turn_attention(LAST, last_ps[c], c)
            for c in range(CHUNKS):
                project_out(LAST, last_ps[CHUNKS + c], c)

            pe.wait_ge(rows_done, 1)
            pe.wait_ge(stage_lo, 2)
            expert_turns(0, True, True)
            with pe.Fori(0, B - 2) as i:
                expert_turns(i + 1, False, True)
            expert_turns(B - 1, False, False)
            for v in range(DOWN_LAG):
                down(B, v - DOWN_LAG)
            pe.wait_ge(dT_done, CHUNKS * B)
            turn_tokens(0, expert_sums, 1, d_turned)

        @block.scalar
        def _(act):
            def split_weights(pair):
                act.wait_ge(raw_in, 16 * pair + 16)
                act.activation(w_hi[:], w_raw[:], ACT.Copy).then_inc(w_hi_done, 1)

            def split_output(pair):
                act.wait_ge(wo_in, 16 * pair + 16)
                act.activation(wo_hi[:], wo_raw[:], ACT.Copy).then_inc(wo_hi_done, 1)

            def front_deviations(k):
                tiles = FRONT_TILES[k]
                act.wait_ge(ln_moments, k + 1)
                act.activation(sdev[:, tiles], moments_x[:, tiles, 1], ACT.Sqrt, bias=eps[:]).then_inc(ln_sdev, 1)
                act.wait_ge(ln_steps, 2 * k + 2)
                act.activation(sdev_y[:, tiles], var_y[:, tiles], ACT.Sqrt, bias=eps[:]).then_inc(y_sdev, 1)

            def normalise_batch(b):
                act.wait_ge(shift_done, 1)
                act.wait_ge(n_turned, b - 1)
                for t in range(TILES):
                    at = b * TILES + t
                    last = act.activation(n_front[1 - b % 2][:, t, :], x_front[:, at, :], ACT.Identity, scale=rstd_y[:, at:at + 1],
                                          bias=shift_y[:, at:at + 1])
                last.then_inc(n_ready[b], 1)

            def scale_batch(b):
                act.wait_ge(n_turned, b + 1)
                if b:
                    act.wait_ge(c_ready, b)
                act.activation(hT, flat(turn_ps), ACT.Identity, scale=scale_sb[:], bias=bias_sb[:]).then_inc(h_done, 1)

            def split_latents(b):
                act.wait_ge(c_ready, b + 1)
                if b:
                    act.wait_ge(c_in, 64 * b)
                act.activation(c_hi, flat(latent_ps), ACT.Copy).then_inc(c_hi_done, 1)

            def split_rotated(n, a, first):
                act.wait_ge(rope_sum, n * 4 + (2 * a + 2))
                if not first:
                    act.wait_ge(score_in[1], 32 * n)
                act.activation(qk_hi[a][:], rot[a][:], ACT.Copy).then_inc(qk_hi_done, 1)

            def split_values(n, par, c):
                which = ("value", 0, c, 0)
                tiles = HALF // P
                act.wait_ge(aux_ready, n * NFEED + (FEED_AT[which] + 1))
                act.activation(vsl[par][:, c * tiles:(c + 1) * tiles, :, 0:DH],
                               bank[BANK_OF[which]].rearrange("p (t h d) -> p t h d", h=2, d=DH),
                               ACT.Copy).then_inc(v_hi_done, 1)

            def split_attention(m, c, src=None):
                act.wait_ge(out_ready, 4 * m + (c + 1))
                act.activation(aT_hi[:, c * HALF:(c + 1) * HALF], bank[BANK_OF[ATTN[c]]] if src is None else src, ACT.Copy).then_inc(aT_hi_done, 1)

            def copy_projected(m, c, src=None):
                act.wait_ge(out_ready, 4 * m + (c + 3))
                act.activation(o_part[c][:], bank[BANK_OF[OUT[c]]] if src is None else src, ACT.Copy).then_inc(out_copied, 1)

            def exponent(g, s, i):
                tile = 2 * s + i
                act.wait_ge(scores_ready, g * KEY_TILES + (tile + 1))
                act.activation(probs[s % 4][:, i, :], score_ps[tile % SCORE_BANKS], ACT.Exp,
                               scale=SCALE).then_inc(probs_done, 1)

            def copy_out(g, s):
                act.wait_ge(pv_done, g * STEPS + (s + 1))
                act.activation(o_sb[s // 4 % 2][:].rearrange("p a q n -> p a (q n)"), outacc[:, :, 0:2 * VW],
                               ACT.Copy).then_inc(o_copied, 1)

            def normalise(g, s):
                half = s // 4
                act.wait_ge(o_added, g * 4 + (half + 1))
                act.wait_ge(o_recip, g * 4 + (half + 1))
                t = s % STEPS
                h, qh = t // 8, t % 8 // 4
                for q in range(4):
                    last = act.activation(attn[:, qh * 4 + q, h * DH:(h + 1) * DH], o_sum[half % 2][:, q, :], ACT.Copy,
                                          scale=o_rden[half % 2][:, q:q + 1])
                last.then_inc(o_done, 1)

            def lagged(g, s, finishes):
                if s % 4 == 2 and (s >= 6 or finishes):
                    copy_out(g, s - 3)
                if s % 4 == 1 and (s >= 9 or finishes):
                    normalise(g, s - 6)

            def deviations(k, n):
                act.wait_ge(mv_done[k], n + 1)
                act.activation(ln_dev[k][:], ln_mv[k][:, :, 1], ACT.Sqrt, bias=eps[:]).then_inc(dev_done[k], 1)

            def copy_input(n, c):
                act.wait_ge(z_turned, CHUNKS * n + (c + 1))
                act.activation(zT[:, c * HALF:(c + 1) * HALF], sides(n)[c], ACT.Copy).then_inc(z_copied, 1)

            def split_input(n, c):
                cols = slice(c * HALF, (c + 1) * HALF)
                act.wait_ge(z_copied, CHUNKS * n + 2)
                act.activation(zT_hi[:, cols], zT[:, cols], ACT.Copy).then_inc(z_hi_done, 1)

            def router_exp(n):
                act.wait_ge(route_dve, ROUTE * n + 2)
                act.activation(lexp[:], lg[:], ACT.Exp).then_inc(route_act, 1)

            def chosen_exp(n):
                act.wait_ge(route_dve, ROUTE * n + 7)
                act.activation(egap[:], gap[:], ACT.Exp).then_inc(route_act, 1)

            def copy_routing(n, c):
                act.wait_ge(w_turned, CHUNKS * n + (c + 1))
                act.activation(wT[:, c * HALF:(c + 1) * HALF], sides(n)[1 - c][0:2 * E, :], ACT.Copy).then_inc(wT_done, 1)

            def copy_sums(count, chunks, alone=False):
                act.wait_ge(down_done, count)
                if not alone:
                    act.wait_ge(d_turned, chunks - 1)
                act.activation(dT[:], down_ps, ACT.Copy).then_inc(dT_done, 1)

            def normalise_output(n, quarter):
                if not quarter:
                    act.wait_ge(inv_done[2], 2 * n + 2)
                for k in range(TILES // 4):
                    t = quarter * (TILES // 4) + k
                    last = act.activation(nf_sb[:, t, :], moe_sb[:, t, :], ACT.Identity, scale=ln_inv[2][:, t:t + 1],
                                          bias=out_shift[:, t:t + 1])
                if quarter == 3:
                    last.then_inc(nf_done, 1)

            def high(b, v, first=False):
                act.wait_ge(fuse_done, TURNS * b + (v + 1))
                if not (first and v < 4):
                    act.wait_ge(down_done, TURNS * b + (v - 3))
                act.activation(f_hi[v % 4][:], fuse[v % 4][:], ACT.Copy).then_inc(f_hi_done, 1)

            def copy_weights(b, u):
                act.wait_ge(wrow_ready, EXPERT_UNITS * b + (u + 1))
                act.activation(wrow_sb[u % 2][:], wrow_ps, ACT.Copy).then_inc(wrow_done, 1)

            def expert_turns(b, first, front):
                n = b + 1
                for v in range(TURNS):
                    u = v // FT
                    if v == DOWN_LAG and not first:
                        copy_sums(TURNS * b, CHUNKS * b)
                    if v == TURNS // 2 + DOWN_LAG:
                        copy_sums(TURNS * b + TURNS // 2, CHUNKS * b + 1, first)
                    act.wait_ge(gate_ready, TURNS * b + (v + 1))
                    if not first or v >= 2:
                        act.wait_ge(actw_done, TURNS * b + (v - 1))
                    act.activation(act_sb[v % 2][:], gate_ps[v % 2], ACT.Silu).then_inc(act_done, 1)
                    if v == 0:
                        if not first:
                            copy_routing(b, 0)
                        copy_weights(b, 0)
                    if not first or v >= SPLIT_LAG:
                        high(b, v - SPLIT_LAG, first)
                    if v % FT == FT - 1 and v < TURNS - 1:
                        copy_weights(b, u + 1)
                    if v == 1 and not first:
                        act.wait_ge(wrow_ready, EXPERT_UNITS * b)
                        copy_routing(b, 1)
                    if v == 2:
                        if not first:
                            act.wait_ge(up_ready, TURNS * b)
                        split_input(b, 1)
                    if v == 8 and front:
                        deviations(0, n)
                    if v == 16 and not first:
                        deviations(2, b - 1)
                    if v == 16 and front:
                        deviations(1, n)
                    if v in (20, 21) and front:
                        copy_input(n, v - 20)
                    if v in (18, 19, 20, 21) and not first:
                        normalise_output(b - 1, v - 18)
                    if v == 22 and front:
                        act.wait_ge(up_ready, TURNS * b + TURNS // 2)
                        split_input(n, 0)
                    if v == 24 and front:
                        router_exp(n)
                    if v == 28 and front:
                        chosen_exp(n)

            def split_expert_weights(k):
                act.wait_ge(stage_in[k], 16)
                act.activation(experts[k][1][:], stage[k], ACT.Copy).then_inc(stage_hi, 1)

            def first_input(s):
                if s in (2, 6):
                    split_expert_weights(s // 6)
                if s == OUTPUT_NORM:
                    deviations(0, 0)
                if s == INPUT_NORM:
                    deviations(1, 0)
                if s == INPUT_TURN + 1:
                    for c in range(CHUNKS):
                        copy_input(0, c)
                    split_input(0, 0)
                if s == INPUT_TURN + 3:
                    router_exp(0)
                if s == INPUT_TURN + 4:
                    chosen_exp(0)

            def attend(g, b, pair, feeds, finishes, more=True, beside=None):
                for s in range(STEPS):
                    lagged(g, s, finishes)
                    exponent(g, s, 0)
                    if finishes and s == 6:
                        split_attention(g - 1, 0)
                    taken = [job for job in FEED_IN.get(s, []) if job[0] == "value"] if feeds else []
                    if len(taken) == 2:
                        split_values(g + 1, 1 - b % 2, 0)
                    exponent(g, s, 1)
                    if finishes and s == 6:
                        split_attention(g - 1, 1)
                    for c in range(CHUNKS):
                        if finishes and OUT[c] in FINISH_IN.get(s, ()):
                            copy_projected(g - 1, c)
                    if taken:
                        split_values(g + 1, 1 - b % 2, taken[-1][2])
                    for a in range(2):
                        if feeds and s == ROTATED_STEPS[a]:
                            split_rotated(g + 1, a, False)
                    if b == B - 2 and s == WEIGHTS_STEP and more:
                        act.wait_ge(aux_ready, (g + 1) * NFEED + (FEED_AT[("value", 0, 1, 0)] + 1))
                        split_weights(pair + 1)
                    if b == 0 and s == WOUT_STEP:
                        if finishes:
                            act.wait_ge(out_ready, 4 * g)
                        split_output(pair)
                    if beside:
                        beside(s)

            act.wait_ge(eps_set, 1)
            act.activation(warm[:], eps[:], ACT.Sqrt)
            front_deviations(0)
            split_weights(0)
            act.wait_ge(consts_in, 16 * len(first_consts))
            scale_batch(0)
            split_latents(0)
            front_deviations(1)
            normalise_batch(2)
            scale_batch(1)
            split_rotated(0, 0, True)
            split_latents(1)
            split_rotated(0, 1, True)
            for c in range(CHUNKS):
                split_values(0, 0, c)
            scale_batch(2)
            normalise_batch(3)
            split_latents(2)
            scale_batch(3)
            split_latents(3)
            act.wait_ge(c_in, 64 * B)
            attend(0, 0, 0, True, False)
            with act.Fori(0, PAIRS - 1) as pair:
                for b in range(1, B):
                    attend(pair * B + b, b, pair, True, True)
                attend(pair * B + B, 0, pair + 1, True, True)
            for b in range(1, B - 1):
                attend(LAST - (B - 1 - b), b, PAIRS - 1, True, True, False)
            attend(LAST, B - 1, PAIRS - 1, False, True, False, first_input)
            split_expert_weights(2)
            for s in range(STEPS, STEPS + 6):
                lagged(LAST, s, True)
            for c in range(CHUNKS):
                copy_routing(0, c)
            for c in range(CHUNKS):
                split_attention(LAST, c, last_ps[c])
            for c in range(CHUNKS):
                copy_projected(LAST, c, last_ps[CHUNKS + c])

            expert_turns(0, True, True)
            with act.Fori(0, B - 2) as i:
                expert_turns(i + 1, False, True)
            expert_turns(B - 1, False, False)
            for v in range(SPLIT_LAG):
                high(B, v - SPLIT_LAG)
            copy_sums(TURNS * B, CHUNKS * B)
            deviations(2, B - 1)
            for quarter in range(4):
                normalise_output(B - 1, quarter)

        @block.vector
        def _(dve):
            dve.memset(eps[:], LN_EPS).then_inc(eps_set, 1)

            def split_weights(pair):
                dve.wait_ge(w_hi_done, pair + 1)
                dve.tensor_tensor(w_lo[:], w_raw[:], w_hi[:], ALU.subtract).then_inc(w_done, 1)

            def split_output(pair):
                dve.wait_ge(wo_hi_done, pair + 1)
                dve.tensor_tensor(wo_lo[:], wo_raw[:], wo_hi[:], ALU.subtract).then_inc(wo_done, 1)

            spares = count()

            def standing():
                at = next(spares) % 16
                dve.memset(spare[:, at:at + 1], 0.0)

            def normalise(src, dst, means, inverse, tiles=range(TILES)):
                for t in tiles:
                    last = dve.tensor_scalar(dst[:, t, :], src[:, t, :], means[:, t, 0:1], inverse[:, t:t + 1],
                                             ALU.subtract, ALU.mult)
                return last

            def front_moments(k):
                tiles = range(B * TILES)[FRONT_TILES[k]]
                for t in tiles:
                    if t % TILES == 0:
                        dve.wait_ge(x_in[t // TILES], 16)
                    last = dve.bn_stats(stats[:, t, :], x_front[:, t, :])
                last.then_inc(ln_stats, 1)
                dve.wait_ge(ln_stats, k + 1)
                for t in tiles:
                    last = dve.bn_aggr(moments_x[:, t, :], stats[:, t, :])
                last.then_inc(ln_moments, 1)

            def front_inverses(k):
                tiles = FRONT_TILES[k]
                dve.wait_ge(ln_sdev, k + 1)
                dve.reciprocal(rstd_x[:, tiles], sdev[:, tiles]).then_inc(ln_rstd, 1)
                dve.wait_ge(ln_rstd, k + 1)
                dve.tensor_tensor(var_y[:, tiles], moments_x[:, tiles, 1], rstd_x[:, tiles], ALU.mult).then_inc(ln_steps, 1)
                dve.wait_ge(ln_steps, 2 * k + 1)
                dve.tensor_tensor(var_y[:, tiles], var_y[:, tiles], rstd_x[:, tiles], ALU.mult).then_inc(ln_steps, 1)
                dve.wait_ge(y_sdev, k + 1)
                dve.reciprocal(rstd_y[:, tiles], sdev_y[:, tiles]).then_inc(ln_y_inverse, 1)
                dve.wait_ge(ln_y_inverse, 2 * k + 1)
                dve.tensor_tensor(rstd_y[:, tiles], rstd_y[:, tiles], rstd_x[:, tiles], ALU.mult).then_inc(ln_y_inverse, 1)

            def split_latents(b):
                dve.wait_ge(c_hi_done, b + 1)
                dve.tensor_tensor(c_lo, flat(latent_ps), c_hi, ALU.subtract).then_inc(c_lo_done, 1)

            def feed_job(n, par, which, first):
                at = FEED_AT[which]
                kind, a, t, c = which
                src = bank[BANK_OF[which]]
                if kind != "value":
                    dve.wait_ge(aux_ready, n * NFEED + (at + 1))
                if kind == "proj":
                    k = 2 * a + t
                    cols = slice(t * HALF, (t + 1) * HALF)
                    if c == 0:
                        if k == 2 and not first:
                            dve.wait_ge(score_in[1], 32 * n)
                        dve.tensor_tensor(rot[a][:, cols], src, cos_sb[:, cols], ALU.mult).then_inc(aux_taken, 1)
                    else:
                        if k >= 2:
                            dve.wait_ge(rope_sum, n * 4 + (k - 1))
                        dve.tensor_tensor(t_sin[k % 2][:], src, sin_sb[:, cols], ALU.mult).then_inc(aux_taken, 1)
                elif kind == "value":
                    tiles = slice(t * (HALF // P), (t + 1) * (HALF // P))
                    dve.wait_ge(v_hi_done, CHUNKS * n + (t + 1))
                    dve.tensor_tensor(vsl[par][:, tiles, :, VLO:VW], src.rearrange("p (t h d) -> p t h d", h=2, d=DH),
                                      vsl[par][:, tiles, :, 0:DH], ALU.subtract).then_inc(aux_taken, 1)
                elif kind == "max":
                    dve.tensor_reduce(row_max[a][:, c, t:t + 1], src, AX, ALU.max).then_inc(aux_taken, 1)
                else:
                    dve.tensor_copy(max_turned[a][:], src[0:2 * TILES, 0:P]).then_inc(aux_taken, 1)

            def negate_maxima(n, a, step):
                if step == 0:
                    dve.wait_ge(aux_taken, n * NFEED + (FEED_AT[LAST_MAX[a]] + 1))
                    dve.tensor_tensor(max_all[a][:], row_max[a][:, 0, :], row_max[a][:, 1, :], ALU.max).then_inc(max_whole, 1)
                elif step == 1:
                    dve.wait_ge(max_whole, 2 * n + (a + 1))
                    dve.tensor_scalar(max_parts[a][:, 0:TILES], max_all[a][:], -1.0, None, ALU.mult).then_inc(max_hi, 1)
                else:
                    dve.wait_ge(max_hi, 2 * n + (a + 1))
                    dve.scalar_tensor_tensor(out=max_parts[a][:, TILES:2 * TILES], in0=max_all[a][:], scalar=-1.0,
                                             in1=max_parts[a][:, 0:TILES], op0=ALU.mult, op1=ALU.subtract).then_inc(max_split, 1)

            def split_attention(m, c, src=None):
                cols = slice(c * HALF, (c + 1) * HALF)
                dve.wait_ge(aT_hi_done, CHUNKS * m + (c + 1))
                dve.tensor_tensor(aT_lo[:, cols], bank[BANK_OF[ATTN[c]]] if src is None else src, aT_hi[:, cols], ALU.subtract).then_inc(attn_taken, 1)

            def low(g, s):
                dve.wait_ge(probs_done, g * KEY_TILES + (2 * s + 2))
                p = probs[s % 4][:].rearrange("p a n -> p (a n)")
                dve.tensor_tensor(probs_lo[s % 4][:].rearrange("p a n -> p (a n)"), p,
                                  p.bitcast(BF16).rearrange("p (n two) -> p n two", two=2)[:, :, 1],
                                  ALU.subtract).then_inc(lo_dve, 1)

            def lagged(g, s, finishes):
                if (s >= 1 or finishes) and s <= STEPS and (s - 1) % STEPS in DVE_STEPS:
                    low(g, s - 1)
                if s % 4 == 3 and (s >= 7 or finishes):
                    half = (s - 4) // 4
                    dve.wait_ge(o_copied, g * 4 + (half + 1))
                    sums = o_sb[half % 2][:].rearrange("p a q n -> p (a q) n")[:, :, DH]
                    dve.reciprocal(o_rden[half % 2][:], sums).then_inc(o_recip, 1)

            def move_projected(n):
                dve.tensor_copy(o_now[:], oacc[:, bass.ds(n, 1), :].rearrange("p a n -> p (a n)")).then_inc(o_moved, 1)

            def attention_residual(n, half):
                normalise(batch_of(x_all, n), y_sb, batch_of(moments_x, n), rstd_x[:, bass.ds(n * TILES, TILES)],
                          half_of(half)).then_inc(y_done, 1)

            def add_residual(n, c):
                tiles = slice(c * HALF_TILES, (c + 1) * HALF_TILES)
                dve.wait_ge(y_done, CHUNKS * n + (c + 1))
                dve.wait_ge(o_turned, CHUNKS * n + (c + 1))
                dve.tensor_tensor(res_sb[:, tiles, :], sides(n)[1 - c].rearrange("p (t d) -> p t d", d=D), y_sb[:, tiles, :],
                                  ALU.add).then_inc(res_done, 1)

            def statistics(k, n, src, half):
                if k == 2 or k == 0 and not half:
                    standing()
                for t in range(half * HALF_TILES, (half + 1) * HALF_TILES):
                    last = dve.bn_stats(ln_st[k][:, t, :], src[:, t, :])
                if half:
                    last.then_inc(st_done[k], 1)

            def means_of(k, n):
                dve.wait_ge(st_done[k], n + 1)
                standing()
                for t in range(TILES):
                    last = dve.bn_aggr(ln_mv[k][:, t, :], ln_st[k][:, t, :])
                last.then_inc(mv_done[k], 1)

            def inverses(k, n):
                dve.wait_ge(dev_done[k], n + 1)
                dve.reciprocal(ln_inv[k][:], ln_dev[k][:]).then_inc(inv_done[k], 1)

            def output_shift(n):
                dve.wait_ge(inv_done[2], 2 * n + 1)
                dve.scalar_tensor_tensor(out=out_shift[:], in0=ln_mv[2][:, :, 0], scalar=-1.0, in1=ln_inv[2][:],
                                         op0=ALU.mult, op1=ALU.mult).then_inc(inv_done[2], 1)

            def half_of(half):
                return range(half * HALF_TILES, (half + 1) * HALF_TILES)

            def normalise_attention(n, half):
                if not half:
                    dve.wait_ge(inv_done[0], n + 1)
                normalise(res_sb, n1_sb, ln_mv[0], ln_inv[0], half_of(half)).then_inc(n1_done, 1)

            def add_tokens(n):
                x1 = batch_of(x_all, n)
                dve.wait_ge(n1_done, 2 * n + 2)
                dve.tensor_tensor(x1, x1, n1_sb[:], ALU.add).then_inc(x1_done, 1)
                dve.wait_ge(x1_done, n + 1)

            def normalise_input(n, half):
                if not half:
                    dve.wait_ge(inv_done[1], n + 1)
                normalise(batch_of(x_all, n), z_sb, ln_mv[1], ln_inv[1], half_of(half)).then_inc(z_done, 1)

            def low_input(n, c):
                cols = slice(c * HALF, (c + 1) * HALF)
                dve.wait_ge(z_hi_done, CHUNKS * n + (c + 1))
                dve.tensor_tensor(zT_lo[:, cols], zT[:, cols], zT_hi[:, cols], ALU.subtract).then_inc(z_lo_done, 1)

            def over(t):
                return t.unsqueeze(2).to_broadcast([P, TILES, E])

            def route(n, part):
                def step(ins, k):
                    ins.then_inc(route_dve, 1)
                    dve.wait_ge(route_dve, ROUTE * n + k)

                if part == 0:
                    dve.wait_ge(logits_ready, n + 1)
                    logits = sides(n)[0][:, 0:TILES * E].rearrange("p (t e) -> p t e", e=E)
                    step(dve.tensor_reduce(lmax[:], logits, AX, ALU.max), 1)
                    step(dve.tensor_tensor(lg[:], logits, over(lmax[:]), ALU.subtract), 2)
                elif part == 1:
                    dve.wait_ge(route_act, 2 * n + 1)
                    step(dve.tensor_reduce(lsum[:], lexp[:], AX, ALU.add), 3)
                    step(dve.reciprocal(lrec[:], lsum[:]), 4)
                elif part == 2:
                    step(dve.tensor_tensor(pr[:], lexp[:], over(lrec[:]), ALU.mult), 5)
                    standing()
                    for t in range(TILES):
                        last = dve.max(top[:, t, :], pr[:, t, :])
                    step(last, 6)
                elif part == 3:
                    step(dve.tensor_tensor(gap[:], top[:, :, 1], top[:, :, 0], ALU.subtract), 7)
                    standing()
                    for t in range(TILES):
                        last = dve.max_index(top_at[:, t, :], top[:, t, :], pr[:, t, :])
                    step(last, 8)
                elif part == 4:
                    step(dve.tensor_copy(top_f[:], top_at[:]), 9)
                    dve.tensor_tensor(hot_1[:], ids_sb[:], over(top_f[:, :, 0]), ALU.is_equal)
                    step(dve.tensor_tensor(hot_2[:], ids_sb[:], over(top_f[:, :, 1]), ALU.is_equal), 10)
                elif part == 5:
                    dve.wait_ge(route_act, 2 * n + 2)
                    step(dve.tensor_scalar(eden[:], egap[:], 1.0, None, ALU.add), 11)
                    step(dve.reciprocal(w_1[:], eden[:]), 12)
                elif part == 6:
                    step(dve.tensor_tensor(w_2[:], egap[:], w_1[:], ALU.mult), 13)
                    dve.tensor_tensor(hot_w1[:], hot_1[:], over(w_1[:]), ALU.mult)
                    step(dve.tensor_tensor(hot_w2[:], hot_2[:], over(w_2[:]), ALU.mult), 14)
                else:
                    step(dve.tensor_tensor(wfull[:], hot_w1[:], hot_w2[:], ALU.add), 15)
                    step(dve.tensor_copy(w_high[:], wfull[:]), 16)
                    dve.tensor_copy(w_both[:, :, 0:E], w_high[:].bitcast(F32))
                    step(dve.tensor_tensor(w_both[:, :, E:2 * E], wfull[:], w_high[:].bitcast(F32), ALU.subtract), ROUTE)

            def low_hidden(b, v):
                dve.wait_ge(f_hi_done, TURNS * b + (v + 1))
                dve.tensor_tensor(f_lo[v % 4][:], fuse[v % 4][:], f_hi[v % 4][:], ALU.subtract).then_inc(f_lo_done, 1)

            def take_sums(c, side, chunks):
                dve.wait_ge(d_turned, chunks)
                dve.tensor_copy(moe_sb[:, c * HALF_TILES:(c + 1) * HALF_TILES, :].rearrange("p t d -> p (t d)"),
                                side_ps[side]).then_inc(d_taken, 1)

            def expert_turns(b, first, front):
                n = b + 1
                for v in range(TURNS):
                    dve.wait_ge(up_ready, TURNS * b + (v + 1))
                    dve.wait_ge(actw_done, TURNS * b + (v + 1))
                    if not first or v >= 4:
                        dve.wait_ge(f_lo_done, TURNS * b + (v - 3))
                    dve.tensor_tensor(fuse[v % 4][:], up_ps[v % 2], actw_sb[v % 2][:], ALU.mult).then_inc(fuse_done, 1)
                    if not first or v >= SPLIT_LAG:
                        low_hidden(b, v - SPLIT_LAG)
                    if front:
                        if v == 0:
                            move_projected(n)
                        if v in (0, 1):
                            attention_residual(n, v)
                        if v == 3:
                            add_residual(n, 0)
                            add_residual(n, 1)
                        if v in (4, 5):
                            if v == 4:
                                dve.wait_ge(res_done, CHUNKS * n + CHUNKS)
                            statistics(0, n, res_sb, v - 4)
                        if v == 6:
                            means_of(0, n)
                        if v == 8:
                            inverses(0, n)
                        if v in (9, 10):
                            normalise_attention(n, v - 9)
                        if v == 11:
                            add_tokens(n)
                        if v in (12, 13):
                            statistics(1, n, batch_of(x_all, n), v - 12)
                        if v == 14:
                            means_of(1, n)
                        if v == 16:
                            inverses(1, n)
                        if v in (17, 18):
                            normalise_input(n, v - 17)
                        if v == 23:
                            low_input(n, 0)
                        for part in range(len(ROUTE_TURNS)):
                            if v == ROUTE_TURNS[part]:
                                route(n, part)
                    if v == 2:
                        low_input(b, 1)
                    if not first:
                        if v == 7:
                            take_sums(1, 0, CHUNKS * b)
                        if v == 8:
                            dve.wait_ge(d_taken, CHUNKS * b)
                            statistics(2, b - 1, moe_sb, 1)
                        if v == 11:
                            means_of(2, b - 1)
                        if v == 16:
                            inverses(2, b - 1)
                            output_shift(b - 1)
                    if v == 25:
                        if not first:
                            dve.wait_ge(nf_done, b)
                        take_sums(0, 1, CHUNKS * b + 1)
                    if v == 26:
                        dve.wait_ge(d_taken, CHUNKS * b + 1)
                        statistics(2, b, moe_sb, 0)

            def low_weights(k):
                hi, lo = experts[k][1:]
                dve.wait_ge(stage_hi, k + 1)
                dve.tensor_tensor(lo[:], stage[k], hi[:], ALU.subtract).then_inc(stage_lo, 1)

            def first_input(s):
                if s == 0:
                    dve.wait_ge(out_added, 2 * (LAST - 2))
                    move_projected(0)
                if s == 2:
                    dve.wait_ge(x_first, 16)
                    for half in range(CHUNKS):
                        attention_residual(0, half)
                if s == 3:
                    for c in range(CHUNKS):
                        add_residual(0, c)
                    dve.wait_ge(res_done, CHUNKS)
                    for half in range(CHUNKS):
                        statistics(0, 0, res_sb, half)
                    means_of(0, 0)
                if s == OUTPUT_NORM:
                    low_weights(0)
                if s == OUTPUT_NORM + 1:
                    inverses(0, 0)
                    for half in range(CHUNKS):
                        normalise_attention(0, half)
                    add_tokens(0)
                if s == OUTPUT_NORM + 2:
                    for half in range(CHUNKS):
                        statistics(1, 0, batch_of(x_all, 0), half)
                    means_of(1, 0)
                if s == INPUT_NORM:
                    low_weights(1)
                if s == INPUT_NORM + 1:
                    inverses(1, 0)
                    for half in range(CHUNKS):
                        normalise_input(0, half)
                if s == INPUT_TURN + 2:
                    low_input(0, 0)
                if s == INPUT_TURN + 3:
                    route(0, 0)
                if s == INPUT_TURN + 4:
                    for part in range(1, 4):
                        route(0, part)

            def attend(g, b, pair, feeds, finishes, more=True, beside=None):
                for s in range(STEPS):
                    if s == 0 and finishes:
                        for step in (1, 2):
                            negate_maxima(g, 1, step)
                    lagged(g, s, finishes)
                    for which in jobs_in(s, feeds, finishes):
                        if which in ATTN:
                            split_attention(g - 1, which[2])
                        elif which not in OUT:
                            feed_job(g if which in OWN else g + 1, 1 - b % 2, which, False)
                            after = FEED_AT[which] - FEED_AT[LAST_MAX[0]]
                            if 1 <= after <= 3:
                                negate_maxima(g + 1, 0, after - 1)
                    if feeds and s == STEPS - 1:
                        negate_maxima(g + 1, 1, 0)
                    if b == B - 2 and s == WEIGHTS_STEP and more:
                        split_weights(pair + 1)
                    if b == 0 and s == WOUT_STEP:
                        split_output(pair)
                    if beside:
                        beside(s)

            front_moments(0)
            front_inverses(0)
            dve.wait_ge(ln_y_inverse, 2)
            normalise(x_front, n_front[1], moments_x, rstd_y, range(TILES)).then_inc(n_ready[0], 1)
            split_weights(0)
            front_moments(1)
            split_latents(0)
            front_inverses(1)
            dve.wait_ge(ln_y_inverse, 4)
            others = FRONT_TILES[1]
            dve.scalar_tensor_tensor(out=shift_y[:, others], in0=moments_x[:, others, 0], scalar=-1.0,
                                     in1=rstd_y[:, others], op0=ALU.mult, op1=ALU.mult).then_inc(shift_done, 1)
            normalise(batch_of(x_front, 1), n_front[0], batch_of(moments_x, 1), rstd_y[:, TILES:2 * TILES],
                      range(TILES)).then_inc(n_ready[1], 1)
            dve.wait_ge(tables_in, 16 * len(tables))
            for k, which in enumerate(FEED[:-1]):
                feed_job(0, 0, which, True)
                if which in LAST_MAX:
                    for step in range(3):
                        negate_maxima(0, LAST_MAX.index(which), step)
                if k in SPLIT_AFTER:
                    split_latents(SPLIT_AFTER[k])
            attend(0, 0, 0, True, False)
            with dve.Fori(0, PAIRS - 1) as pair:
                for b in range(1, B):
                    attend(pair * B + b, b, pair, True, True)
                attend(pair * B + B, 0, pair + 1, True, True)
            for b in range(1, B - 1):
                attend(LAST - (B - 1 - b), b, PAIRS - 1, True, True, False)
            attend(LAST, B - 1, PAIRS - 1, False, True, False, first_input)
            for s in (STEPS, STEPS + 3):
                if s > STEPS:
                    for part in range(4, len(ROUTE_TURNS)):
                        route(0, part)
                    dve.wait_ge(rows_loaded, 16)
                    dve.tensor_copy(rows_r[:], rows_in[:]).then_inc(rows_done, 1)
                lagged(LAST, s, True)
            for c in range(CHUNKS):
                split_attention(LAST, c, last_ps[c])

            dve.wait_ge(x_rest, 16 * (B - 1))
            dve.wait_ge(out_added, 2 * PAIRS * B)
            expert_turns(0, True, True)
            with dve.Fori(0, B - 2) as i:
                expert_turns(i + 1, False, True)
            expert_turns(B - 1, False, False)
            for v in range(SPLIT_LAG):
                low_hidden(B, v - SPLIT_LAG)
            take_sums(1, 0, CHUNKS * B)
            dve.wait_ge(d_taken, CHUNKS * B)
            statistics(2, B - 1, moe_sb, 1)
            means_of(2, B - 1)
            inverses(2, B - 1)
            output_shift(B - 1)

        @block.gpsimd
        def _(pool):
            def rope_add(n, at):
                a, t = at // 2, at % 2
                pool.wait_ge(aux_taken, n * NFEED + (FEED_AT[("proj", a, t, 1)] + 1))
                part = rot[a][:, t * HALF:(t + 1) * HALF]
                pool.tensor_tensor(part, part, t_sin[at % 2][:], ALU.add).then_inc(rope_sum, 1)

            def low_rotated(n, a):
                pool.wait_ge(qk_hi_done, 2 * n + (a + 1))
                pool.tensor_tensor(rot[a][:], rot[a][:], qk_hi[a][:].bitcast(F32), ALU.subtract).then_inc(qk_lo_done, 1)

            def low(g, s):
                pool.wait_ge(probs_done, g * KEY_TILES + (2 * s + 2))
                p = probs[s % 4][:].rearrange("p a n -> p (a n)")
                pool.tensor_tensor(probs_lo[s % 4][:].rearrange("p a n -> p (a n)"), p,
                                   p.bitcast(BF16).rearrange("p (n two) -> p n two", two=2)[:, :, 1],
                                   ALU.subtract).then_inc(lo_pool, 1)

            def add_parts(g, s):
                half = (s - 4) // 4
                pool.wait_ge(o_copied, g * 4 + (half + 1))
                sums = o_sb[half % 2][:].rearrange("p a q n -> p (a q) n")
                pool.tensor_tensor(o_sum[half % 2][:], sums[:, :, 0:DH], sums[:, :, VLO:VW], ALU.add).then_inc(o_added, 1)

            def add_projected(m, b, c):
                total = oacc[:, b, c * HALF:(c + 1) * HALF]
                pool.wait_ge(out_copied, 2 * m + (c + 1))
                pool.tensor_tensor(total, total, o_part[c][:], ALU.add).then_inc(out_added, 1)

            def attend(g, b, feeds, finishes):
                for s in range(STEPS):
                    if s % 4 == 3 and (s >= 7 or finishes):
                        add_parts(g, s)
                    if s - 1 in POOL_STEPS:
                        low(g, s - 1)
                    for c in range(CHUNKS):
                        if finishes and OUT[c] in FINISH_IN.get(s - 2, ()):
                            add_projected(g - 1, (b - 1) % B, c)
                    for at in range(4):
                        if feeds and FEED[2 * at + 1] in FEED_IN.get(s, ()):
                            rope_add(g + 1, at)
                    for a in range(2):
                        if feeds and s == ROTATED_LOW_STEPS[a]:
                            low_rotated(g + 1, a)

            fills = [(k_ones[h][DH:DH + 2, :].bitcast(F32), 1.0) for h in range(2)]
            fills += [(vsl[h][:, :, :, DH + k:DH + k + 1], 1.0 - k) for h in range(2) for k in range(2)]
            fills += [(oacc[:].rearrange("p b n -> p (b n)"), 0.0)]
            assert len(fills) == FILLS
            for k, (where, value) in enumerate(fills):
                if k:
                    pool.wait_ge(fills_done, k)
                pool.memset(where, value).then_inc(fills_done, 1)

            for at in range(4):
                rope_add(0, at)
            low_rotated(0, 0)
            low_rotated(0, 1)
            attend(0, 0, True, False)
            with pool.Fori(0, PAIRS - 1) as pair:
                for b in range(1, B + 1):
                    attend(pair * B + b, b % B, True, True)
            for b in range(1, B):
                attend(LAST - (B - 1 - b), b, b < B - 1, True)
            add_parts(LAST, STEPS + 3)
            _, down_high, down_low = experts[2]
            pool.wait_ge(stage_hi, len(experts))
            pool.tensor_tensor(down_low[:], stage[2], down_high[:].bitcast(F32), ALU.subtract).then_inc(down_lo, 1)
            for c in range(CHUNKS):
                add_projected(LAST, B - 1, c)

            def add_output(n):
                x1 = batch_of(x_all, n)
                pool.tensor_tensor(x1, x1, nf_sb[:], ALU.add).then_inc(result_done, 1)

            def expert_turns(b, first):
                for v in range(TURNS):
                    if v == 22 and not first:
                        pool.wait_ge(nf_done, b)
                    pool.wait_ge(act_done, TURNS * b + (v + 1))
                    pool.wait_ge(wrow_done, EXPERT_UNITS * b + (v // FT + 1))
                    if not first or v >= 2:
                        pool.wait_ge(fuse_done, TURNS * b + (v - 1))
                    pool.tensor_tensor(actw_sb[v % 2][:], act_sb[v % 2][:], wrow_sb[v // FT % 2][:],
                                       ALU.mult).then_inc(actw_done, 1)
                    if v == 22 and not first:
                        add_output(b - 1)

            expert_turns(0, True)
            with pool.Fori(0, B - 2) as i:
                expert_turns(i + 1, False)
            expert_turns(B - 1, False)
            pool.wait_ge(nf_done, B)
            add_output(B - 1)


def rope_tables():
    inv_freq = 1.0 / ROPE_BASE ** (np.arange(0, DH, 2, dtype=np.float32) / DH)
    angles = np.outer(np.arange(S, dtype=np.float32), inv_freq)
    cos = np.concatenate([np.cos(angles), np.cos(angles)], -1)[:, ::2]
    sin = np.concatenate([np.sin(angles), np.sin(angles)], -1)[:, ::2]
    cos = np.repeat(cos, 2, axis=1)
    sin = np.stack([-sin, sin], axis=-1).reshape(S, DH)
    return (np.ascontiguousarray(np.tile(cos, (1, 2)).T.astype(np.float32)),
            np.ascontiguousarray(np.tile(sin, (1, 2)).T.astype(np.float32)))


def kernel(**inputs):
    import concourse.bacc as _bacc
    from concourse import mybir as _mybir
    from concourse.bass_utils import run_bass_kernel_spmd as _run

    a = {k: np.asarray(v) for k, v in inputs.items()}

    def rows_twice(w):
        return np.concatenate([w.T, w.T], axis=0)

    def swapped(w):
        return w.reshape(H * DH // 2, 2, DH)[:, ::-1].reshape(H * DH, DH)

    wq, wk, wv = a["L0_attn_w_up_q"], a["L0_attn_w_up_k"], a["L0_attn_w_up_v"]
    blocks = [rows_twice(w).reshape(P, PAIRS, P) for w in (wq, swapped(wq), wk, swapped(wk), wv)]
    cos, sin = rope_tables()
    arrays = {
        "x": a["L0_attn_x"],
        "w_pairs": np.stack([np.stack([blk[:, n] for blk in blocks], axis=1) for n in range(PAIRS)]),
        "w_out": a["L0_attn_w_out"].T.reshape(PAIRS, P, D),
        "w_down": np.concatenate([a["L0_attn_w_down_q"].T, a["L0_attn_w_down_kv"].T], axis=1),
        "ln_scale": a["L0_attn_ln_scale"].reshape(D, 1),
        "ln_bias": a["L0_attn_ln_bias"].reshape(D, 1),
        "router": a["L0_ffn_router_kernel_DE"],
        "w_gate": a["L0_ffn_kernel_gating_EDF"].transpose(1, 0, 2).reshape(D, E * F),
        "w_up": a["L0_ffn_kernel_up_EDF"].transpose(1, 0, 2).reshape(D, E * F),
        "w_dn": a["L0_ffn_kernel_down_EFD"].reshape(E, FT, P, D).transpose(2, 0, 1, 3).reshape(P, E * FT * D),
        "rope_cos": cos,
        "rope_sin": sin,
        "identity": np.eye(P, dtype=np.float32),
        "expert_rows": np.repeat(np.concatenate([np.eye(E, dtype=np.float32)] * 2), P, axis=1),
        "expert_ids": np.broadcast_to(np.arange(E, dtype=np.float32), (P, TILES, E)),
    }
    nc = _bacc.Bacc("TRN2", target_bir_lowering=False, num_devices=1)
    fed, args = {}, {}
    for name, value in arrays.items():
        fed[f"{name}_dram"] = np.ascontiguousarray(value)
        args[name] = nc.dram_tensor(f"{name}_dram", value.shape, _mybir.dt.from_np(value.dtype), kind="ExternalInput").ap()
    out = nc.dram_tensor("out_dram", (B, S, D), _mybir.dt.float32, kind="ExternalOutput").ap()
    program(nc, out=out, **args)
    r = _run(nc, [fed], core_ids=[0])
    return r.results[0]["out_dram"]
```
